# Optimizing a Trainium2 kernel written in Bass

```python
import numpy as np
import jax
import jax.numpy as jnp

def _softmax(x, axis=-1):
    return jax.nn.softmax(x, axis=axis)

def _gelu(x):
    return jax.nn.gelu(x, approximate=True)

def _silu(x):
    return jax.nn.silu(x)

def _sigmoid(x):
    return jax.nn.sigmoid(x)

def _layernorm(x, axis=-1, eps=1e-05):
    m = jnp.mean(x, axis=axis, keepdims=True)
    v = jnp.var(x, axis=axis, keepdims=True)
    return (x - m) / jnp.sqrt(v + eps)

def _scatter_add(tgt, idx, src, axis=0):
    return tgt.at[idx].add(src)

def _segment_sum(src, seg, n):
    return jax.ops.segment_sum(src, seg, n)
kernel_name = 'mk_decoder_postln_d1_seqx_r8_0eec67'

def setup_inputs(seed: int=0):
    np.random.seed(seed)
    _w = jnp.asarray

    def _rec_inputs():
        import jax
        import jax.numpy as jnp
        _rk = jax.random.key(seed)
        x = -0.0002928 + 1 * jax.random.normal(jax.random.fold_in(_rk, 1), (1, 1024, 128), jnp.float32)
        _lenS = 1024 - jax.random.randint(jax.random.fold_in(_rk, 7), (1,), 0, max(1, 1024 // 4) + 1, jnp.int32)
        _lenS2 = 6404 - jax.random.randint(jax.random.fold_in(_rk, 8), (1,), 0, max(1, 6404 // 4) + 1, jnp.int32)
        _ctx_1024P = jax.random.normal(jax.random.fold_in(_rk, 11), (1, 16, 128), jnp.float32)
        _ctx_1024c = jax.random.dirichlet(jax.random.fold_in(_rk, 511), 0.3 * jnp.ones((16,), jnp.float32), (1, 6404))
        _ctx_1024t = jnp.einsum('bsk,bkd->bsd', _ctx_1024c, _ctx_1024P)
        _ctx_1024t = _ctx_1024t * jax.lax.rsqrt(jnp.mean(jnp.square(_ctx_1024t)) + 1e-12) * 0.953939
        ctx_1024 = -1.39393e-06 + 0.999914 * (_ctx_1024t + 0.3 * jax.random.normal(jax.random.fold_in(_rk, 611), (1, 6404, 128), jnp.float32))
        _validS = jnp.arange(1024)[None, :] < _lenS[:, None]
        _validS2 = jnp.arange(6404)[None, :] < _lenS2[:, None]
        _causal = jnp.tril(jnp.ones((1024, 1024), dtype=bool))
        mask_Bx1xSxS2_fk0 = jnp.where(jnp.broadcast_to(_validS2[:, None, None, :], (1, 1, 1024, 6404)), 0.0, 1.0).astype(jnp.float32)
        return (x, ctx_1024, mask_Bx1xSxS2_fk0)
    x, ctx_1024, mask_Bx1xSxS2_fk0 = _rec_inputs()

    def _L0_attn_setup():
        import jax, jax.numpy as jnp
        import numpy as np
        B, T, D, H = (4, 256, 128, 16)
        HD = D // H
        NEG = -np.finfo(np.float32).max
        key = jax.random.key(seed)
        ks = jax.random.split(key, 9)
        s = 1.0 / np.sqrt(D)
        return {'x': jax.random.normal(ks[0], (B, T, D), jnp.float32), 'wq': jax.random.normal(ks[1], (D, D), jnp.float32) * s, 'bq': jax.random.normal(ks[2], (D,), jnp.float32) * 0.02, 'wk': jax.random.normal(ks[3], (D, D), jnp.float32) * s, 'bk': jax.random.normal(ks[4], (D,), jnp.float32) * 0.02, 'wv': jax.random.normal(ks[5], (D, D), jnp.float32) * s, 'bv': jax.random.normal(ks[6], (D,), jnp.float32) * 0.02, 'wo': jax.random.normal(ks[7], (D, D), jnp.float32) * s, 'bo': jax.random.normal(ks[8], (D,), jnp.float32) * 0.02}
    _L0_attn_all = _L0_attn_setup()
    _L0_attn_in = {k: v for k, v in _L0_attn_all.items() if k in ('wq', 'bq', 'wk', 'bk', 'wv', 'bv', 'wo', 'bo')}
    del _L0_attn_all

    def _L0_xattn_setup():
        import jax, jax.numpy as jnp
        import numpy as np
        D_MODEL = 128
        N_HEADS = 16
        DEPTH = D_MODEL // N_HEADS
        B, S = (2, 256)

        def _split_heads(x):
            b, s, _ = x.shape
            return x.reshape(b, s, N_HEADS, DEPTH).transpose(0, 2, 1, 3)
        key = jax.random.key(seed)
        ks = jax.random.split(key, 13)
        scale = 1.0 / np.sqrt(D_MODEL)
        inp = {'query': jax.random.normal(ks[0], (B, S, D_MODEL), jnp.float32), 'key': jax.random.normal(ks[1], (B, S, D_MODEL), jnp.float32), 'value': jax.random.normal(ks[2], (B, S, D_MODEL), jnp.float32), 'mask': (jax.random.uniform(ks[3], (B, 1, S, S)) < 0.1).astype(jnp.float32), 'Wq': jax.random.normal(ks[4], (D_MODEL, D_MODEL), jnp.float32) * scale, 'bq': jnp.zeros((D_MODEL,), jnp.float32), 'Wk': jax.random.normal(ks[5], (D_MODEL, D_MODEL), jnp.float32) * scale, 'bk': jnp.zeros((D_MODEL,), jnp.float32), 'Wv': jax.random.normal(ks[6], (D_MODEL, D_MODEL), jnp.float32) * scale, 'bv': jnp.zeros((D_MODEL,), jnp.float32), 'Wo': jax.random.normal(ks[7], (D_MODEL, D_MODEL), jnp.float32) * scale, 'bo': jnp.zeros((D_MODEL,), jnp.float32)}
        return inp
    _L0_xattn_all = _L0_xattn_setup()
    _L0_xattn_in = {k: v for k, v in _L0_xattn_all.items() if k in ('Wq', 'bq', 'Wk', 'bk', 'Wv', 'bv', 'Wo', 'bo')}
    del _L0_xattn_all

    def _L0_ffn_setup():
        import jax, jax.numpy as jnp
        import numpy as np
        B, T, C = (4, 256, 128)
        E = 8
        K = 2
        H = 176
        HS = 176 * 2
        key = jax.random.key(seed)
        k = jax.random.split(key, 8)
        s = 0.02
        return {'x': jax.random.normal(k[0], (B, T, C), jnp.float32), 'Wg': jax.random.normal(k[1], (C, E), jnp.float32) * s, 'W1': jax.random.normal(k[2], (E, C, H), jnp.float32) * s, 'W2': jax.random.normal(k[3], (E, C, H), jnp.float32) * s, 'W3': jax.random.normal(k[4], (E, H, C), jnp.float32) * s, 'Ws1': jax.random.normal(k[5], (C, HS), jnp.float32) * s, 'Ws2': jax.random.normal(k[6], (C, HS), jnp.float32) * s, 'Ws3': jax.random.normal(k[7], (HS, C), jnp.float32) * s}
    _L0_ffn_all = _L0_ffn_setup()
    _L0_ffn_in = {k: v for k, v in _L0_ffn_all.items() if k in ('Wg', 'W1', 'W2', 'W3', 'Ws1', 'Ws2', 'Ws3')}
    del _L0_ffn_all
    return {'x': x, 'ctx_1024': ctx_1024, 'mask_Bx1xSxS2_fk0': mask_Bx1xSxS2_fk0, 'L0_attn_wq': _L0_attn_in['wq'], 'L0_attn_bq': _L0_attn_in['bq'], 'L0_attn_wk': _L0_attn_in['wk'], 'L0_attn_bk': _L0_attn_in['bk'], 'L0_attn_wv': _L0_attn_in['wv'], 'L0_attn_bv': _L0_attn_in['bv'], 'L0_attn_wo': _L0_attn_in['wo'], 'L0_attn_bo': _L0_attn_in['bo'], 'L0_xattn_Wq': _L0_xattn_in['Wq'], 'L0_xattn_bq': _L0_xattn_in['bq'], 'L0_xattn_Wk': _L0_xattn_in['Wk'], 'L0_xattn_bk': _L0_xattn_in['bk'], 'L0_xattn_Wv': _L0_xattn_in['Wv'], 'L0_xattn_bv': _L0_xattn_in['bv'], 'L0_xattn_Wo': _L0_xattn_in['Wo'], 'L0_xattn_bo': _L0_xattn_in['bo'], 'L0_ffn_Wg': _L0_ffn_in['Wg'], 'L0_ffn_W1': _L0_ffn_in['W1'], 'L0_ffn_W2': _L0_ffn_in['W2'], 'L0_ffn_W3': _L0_ffn_in['W3'], 'L0_ffn_Ws1': _L0_ffn_in['Ws1'], 'L0_ffn_Ws2': _L0_ffn_in['Ws2'], 'L0_ffn_Ws3': _L0_ffn_in['Ws3']}

def reference(x, ctx_1024, mask_Bx1xSxS2_fk0, L0_attn_wq, L0_attn_bq, L0_attn_wk, L0_attn_bk, L0_attn_wv, L0_attn_bv, L0_attn_wo, L0_attn_bo, L0_xattn_Wq, L0_xattn_bq, L0_xattn_Wk, L0_xattn_bk, L0_xattn_Wv, L0_xattn_bv, L0_xattn_Wo, L0_xattn_bo, L0_ffn_Wg, L0_ffn_W1, L0_ffn_W2, L0_ffn_W3, L0_ffn_Ws1, L0_ffn_Ws2, L0_ffn_Ws3):
    import jax
    import jax.numpy as jnp

    def _L0_attn_ref(x, wq, bq, wk, bk, wv, bv, wo, bo):
        import jax, jax.numpy as jnp
        import numpy as np
        B, T, D, H = (4, 256, 128, 16)
        HD = D // H
        NEG = -np.finfo(np.float32).max
        b, t, d = x.shape

        def proj(w, bias):
            y = x @ w + bias
            return y.reshape(b, t, H, HD).transpose(0, 2, 1, 3)
        q = proj(wq, bq)
        k = proj(wk, bk)
        v = proj(wv, bv)
        scale = 1.0 / np.sqrt(HD).astype(np.float32)
        scores = jnp.einsum('bhqd,bhkd->bhqk', q, k) * scale
        mask = jnp.triu(jnp.full((t, t), NEG, jnp.float32), k=1)
        attn = jax.nn.softmax(scores + mask, axis=-1)
        out = jnp.einsum('bhqk,bhkd->bhqd', attn, v)
        out = out.transpose(0, 2, 1, 3).reshape(b, t, d)
        return out @ wo + bo

    def _L0_xattn_ref(query, key, value, mask, Wq, bq, Wk, bk, Wv, bv, Wo, bo):
        import jax, jax.numpy as jnp
        import numpy as np
        D_MODEL = 128
        N_HEADS = 16
        DEPTH = D_MODEL // N_HEADS
        B, S = (2, 256)

        def _split_heads(x):
            b, s, _ = x.shape
            return x.reshape(b, s, N_HEADS, DEPTH).transpose(0, 2, 1, 3)
        q = _split_heads(query @ Wq.T + bq)
        k = _split_heads(key @ Wk.T + bk)
        v = _split_heads(value @ Wv.T + bv)
        scores = jnp.einsum('bhqd,bhkd->bhqk', q, k) / jnp.sqrt(jnp.float32(DEPTH))
        scores = scores + mask * jnp.float32(-1000000000.0)
        weights = jax.nn.softmax(scores, axis=-1)
        ctx = jnp.einsum('bhqk,bhkd->bhqd', weights, v)
        ctx = ctx.transpose(0, 2, 1, 3).reshape(query.shape[0], -1, D_MODEL)
        return ctx @ Wo.T + bo

    def _L0_ffn_ref(x, Wg, W1, W2, W3, Ws1, Ws2, Ws3):
        import jax, jax.numpy as jnp
        import numpy as np
        B, T, C = (4, 256, 128)
        E = 8
        K = 2
        H = 176
        HS = 176 * 2
        b, t, c = x.shape
        xf = x.reshape(-1, c)
        n = xf.shape[0]
        router = xf @ Wg
        top_logits, idx = jax.lax.top_k(router, K)
        probs = jax.nn.softmax(top_logits.astype(jnp.float32), axis=-1).astype(x.dtype)
        w = jnp.zeros((n, E), x.dtype).at[jnp.arange(n)[:, None], idx].add(probs)
        h = jax.nn.silu(jnp.einsum('tc,ech->eth', xf, W1)) * jnp.einsum('tc,ech->eth', xf, W2)
        y = jnp.einsum('eth,ehc,te->tc', h, W3, w)
        y = y.reshape(b, t, c)
        hs = jax.nn.silu(xf @ Ws1) * (xf @ Ws2)
        y = y + (hs @ Ws3).reshape(b, t, c)
        return y
    x = _layernorm(x + _L0_attn_ref(x, L0_attn_wq, L0_attn_bq, L0_attn_wk, L0_attn_bk, L0_attn_wv, L0_attn_bv, L0_attn_wo, L0_attn_bo), axis=-1)
    x = _layernorm(x + _L0_xattn_ref(x, ctx_1024, ctx_1024, mask_Bx1xSxS2_fk0, L0_xattn_Wq, L0_xattn_bq, L0_xattn_Wk, L0_xattn_bk, L0_xattn_Wv, L0_xattn_bv, L0_xattn_Wo, L0_xattn_bo), axis=-1)
    x = _layernorm(x + _L0_ffn_ref(x, L0_ffn_Wg, L0_ffn_W1, L0_ffn_W2, L0_ffn_W3, L0_ffn_Ws1, L0_ffn_Ws2, L0_ffn_Ws3), axis=-1)
    return x

_drawn_inputs = setup_inputs


def setup_inputs(seed=0):
    import zlib

    import numpy as np

    out = dict(_drawn_inputs(seed))
    spreads = {'L0_xattn_bq': (0.0, 0.333),
     'L0_xattn_bk': (0.0, 0.8),
     'L0_xattn_bv': (0.0, 0.1),
     'L0_xattn_bo': (0.0, 0.1)}
    factors = {'L0_attn_bq': 8.0,
     'L0_attn_bk': 8.0,
     'L0_attn_bo': 2.963,
     'L0_ffn_Wg': 8.0,
     'L0_ffn_W1': 8.0,
     'L0_ffn_W2': 8.0,
     'L0_ffn_W3': 8.0,
     'L0_ffn_Ws1': 5.876,
     'L0_ffn_Ws2': 5.818,
     'L0_ffn_Ws3': 5.852}
    for name, (base, spread) in spreads.items():
        noise = np.random.default_rng([zlib.crc32(name.encode()), seed]).standard_normal(out[name].shape)
        drawn = base * np.exp(spread * noise) if base else spread * noise
        out[name] = jnp.asarray(drawn.astype(out[name].dtype))
    for name, factor in factors.items():
        out[name] = (out[name] * factor).astype(out[name].dtype)
    return out
```

```python
from contextlib import ExitStack

import numpy as np

import concourse.bass as bass
from concourse import mybir

F32 = mybir.dt.float32
BF16 = mybir.dt.bfloat16
I32 = mybir.dt.int32
ALU = mybir.AluOpType
ACT = mybir.ActivationFunctionType
AX = mybir.AxisListType

P = 128
BANK = 512
T = 1024
D = 128
H = 16
HD = D // H
PAIRS = H // 2
QT = T // P
HALVES = T // BANK
LC = 6404
NC_ = -(-LC // P)
LP = NC_ * P
CH = [(c, min(BANK, LP - c)) for c in range(0, LP, BANK)]
E, HE, HS = 8, 176, 352
HID = E * HE + HS
FCH = [(c, min(P, HID - c)) for c in range(0, HID, P)]
FORDER = [j for j, (c, _) in enumerate(FCH) if c >= E * HE] + [j for j, (c, _) in enumerate(FCH) if c < E * HE]
NEXP = sum(c < E * HE for c, _ in FCH)
SCALE = float(1.0 / np.sqrt(np.float32(HD)))
MASKED = -1.0e9
EPS = 1e-5
SPREAD = 60.0
LARGEST = 1024.0
VW = HD + 1

QPART = (0, 1, 2, 0, 1, 0)
KPART = (0, 0, 0, 1, 1, 2)
NTERM = len(QPART)
STACK = 64
SHIFT_ROW = NTERM * HD
MASK_ROW = SHIFT_ROW + 1
RING = 6


class Plan:

    def __init__(self, name, tiles, slots, causal):
        self.name, self.tiles, self.slots, self.causal = name, tiles, slots, causal
        self.width = tiles * P
        self.lag = slots - 1
        self.steps = [(a, kt) for a in range(2) for kt in range(tiles)]
        self.n = len(self.steps)
        self.ring = RING if self.n % RING == 0 else 4
        assert self.n % slots == 0 and self.n % self.ring == 0
        self.groups = [(a, list(range(k, min(k + 2, tiles)))) for a in range(2) for k in range(0, tiles, 2)]
        self.per_head = len(self.groups) // 2

    def group_of(self, s):
        a, kt = self.steps[s]
        return a * self.per_head + kt // 2

    def last_step(self, g):
        a, kts = self.groups[g]
        return a * self.tiles + kts[-1]

    def first_query(self, kt, half):
        return max(half * BANK, kt * P if self.causal else 0)

    def halves(self, kt):
        return [x for x in range(HALVES) if self.first_query(kt, x) < (x + 1) * BANK]


SELF = Plan("self", T // P, 2, True)
CROSS = Plan("cross", NC_, 3, False)


def build(nc, A, out):
    ctx = ExitStack()
    with ctx:
        def sb(name, shape, dt=F32):
            return ctx.enter_context(nc.sbuf_tensor(name, shape, dt))

        def dram(name, shape, dt):
            return nc.dram_tensor(name, shape, dt)

        sems = {}

        def sem(name):
            if name not in sems:
                sems[name] = ctx.enter_context(nc.semaphore(name))
            return sems[name]

        class Chain:

            def __init__(self, eng, name):
                self.eng, self.sem, self.n = eng, sem(name), 0

            def link(self, ins):
                self.n += 1
                ins.then_inc(self.sem, 1)
                self.eng.wait_ge(self.sem, self.n)

        ps = ctx.enter_context(nc.psum_tensor("ps", [P, 8, BANK], F32))
        flat = ps[:, :, :].rearrange("p b n -> p (b n)")
        region_k = sb("region_k", [P, LP])
        region_m = sb("region_m", [P, LP])
        ctxT = region_k
        kT_cross = region_m
        kst = {"cross": region_k[:, :].bitcast(BF16), "self": sb("kst_self", [P, 2 * T], BF16)[:, :]}
        qs = sb("qs", [P, H, T], BF16)
        ring = sb("ring", [P, RING, T])
        vx = {"self": sb("vx_self", [P, H, SELF.tiles, VW]), "cross": sb("vx_cross", [P, H, CROSS.tiles, VW])}
        vh = [sb(f"vh{a}", [P, NC_, VW]) for a in range(2)]
        oev = [sb(f"oev{a}", [P, HALVES, BANK]) for a in range(2)]
        PIECE = LP // PAIRS
        spare = ring[:, 4:6, :].rearrange("p s n -> p (s n)")
        kp_tmp = spare[:, 0:PIECE]
        kp = spare[:, PIECE:PIECE + 3 * PIECE // 2].bitcast(BF16).rearrange("p (i n) -> p i n", i=3)
        qp = sb("qp", [P, 3, T], BF16)
        kp_self = spare[:, 0:3 * T // 2].bitcast(BF16).rearrange("p (i n) -> p i n", i=3)
        qT = {"self": sb("qT_self", [P, T]), "cross": sb("qT_cross", [P, T])}
        kT_self = sb("kT_self", [P, T])
        xT = sb("xT", [P, T])
        xn = sb("xn", [P, QT, D])
        yn = sb("yn", [P, QT, D])
        w = {n: sb("w_" + n, [P, D]) for n in ("q1", "k1", "v1", "o1", "q2", "k2", "v2", "o2")}
        bcol = {n: sb("b_" + n, [P, 1]) for n in ("q1", "k1", "q2", "k2")}
        brow = {n: sb("b_" + n, [P, D]) for n in ("v1", "o1", "v2", "o2")}
        ident = sb("ident", [P, P])
        identb = sb("identb", [P, P], BF16)
        trib = sb("trib", [P, P], BF16)
        hblk = sb("hblk", [P, H])
        ext = {n: sb("ext_" + n, [P, 2]) for n in ("self", "cross")}
        extc = sb("extc", [P, 2, 8])
        shift = sb("shift", [H, T], BF16)
        inr = sb("inr", [H, T])
        good = sb("good", [P, 72])
        mk = sb("mk", [P, NC_])
        mku = sb("mku", [P, NC_])
        mkp = sb("mkp", [P, 3, NC_], BF16)
        st = sb("st", [P, QT, 6])
        mv = sb("mv", [P, QT, 2])
        rstd = sb("rstd", [P, QT])
        wg = sb("wg", [P, E])
        tri8 = sb("tri8", [P, E, E])
        lg = sb("lg", [P, QT, E])
        mx8 = sb("mx8", [P, QT])
        rk = [spare[:, i * QT * E * E:(i + 1) * QT * E * E].rearrange("p (t e j) -> p t e j", e=E, j=E) for i in range(2)]
        sel = sb("sel", [P, QT, E])
        wT = sb("wT", [E, T])
        ones = sb("ones", [P, 1])
        goods = sb("goods", [P, 2])
        held = sb("held", [1, 4])
        flag = sb("flag", [1, 1], I32)
        stat = sb("stat", [P, 4])
        MW = -(-LC // 8)
        MPIECES = [(c, min(MW, LC - c)) for c in range(0, LC, MW)]
        MCOLS = len(MPIECES)
        mchk = [kst["self"].bitcast(F32), yn[:, :, :].rearrange("p t c -> p (t c)")]
        row0 = region_m[:, 0:LC]

        qscr = {n: dram("qscr_" + n, [H, 3, HD, T], BF16) for n in ("self", "cross")}
        kscr = {"self": dram("kscr_self", [H, 3, HD, T], BF16), "cross": dram("kscr_cross", [H, 3, HD, LP], BF16)}
        sscr = {n: dram("sscr_" + n, [H, T], BF16) for n in ("self", "cross")}
        mscr = dram("mscr", [3, LP], BF16)
        oscr = {n: dram("oscr_" + n, [2, H, VW, T], F32) for n in ("self", "cross")}
        wscr = dram("wscr", [E, T], F32)
        kTscr = dram("kTscr", [P, LP], F32)

        block = ctx.enter_context(nc.Block())
        g = lambda pair, per, off: pair * per + off

        def scores_and_values(pe, pl):
            n = pl.name
            scored, exped, valued = sem(n + "_scored"), sem(n + "_exped"), sem(n + "_valued")
            evicted, vh_ready, k_loaded = sem(n + "_evicted"), sem(n + "_vh_ready"), sem(n + "_k_loaded")

            def scores(p, first, s):
                a, kt = pl.steps[s]
                slot = s % pl.slots
                if not (first and s < pl.slots):
                    pe.wait_ge(exped, g(p, pl.n, s - pl.slots + 1))
                if s == 0:
                    pe.wait_ge(k_loaded, g(p, 16 * NTERM, 16 * NTERM))
                keys = kst[n][:, bass.ds((p % 2) * pl.width + kt * P, P)]
                for x in pl.halves(kt):
                    q0 = pl.first_query(kt, x)
                    queries = lambda lo, hi: qs[:, bass.ds(2 * p + a, 1), lo:hi].rearrange("p h n -> p (h n)")
                    at = 2 * slot * BANK
                    if pl.causal and q0 == kt * P:
                        pe.matmul(flat[:, at + q0:at + q0 + P], identb[:, :], trib[:, :], start=True, stop=False)
                        last = pe.matmul(flat[:, at + q0:at + q0 + P], keys, queries(q0, q0 + P), start=False, stop=True)
                        q0 += P
                    if q0 < (x + 1) * BANK:
                        last = pe.matmul(flat[:, at + q0:at + (x + 1) * BANK], keys, queries(q0, (x + 1) * BANK),
                                         start=True, stop=True)
                last.then_inc(scored, 1)

            def values(p, first, gi):
                a, kts = pl.groups[gi]
                pe.wait_ge(exped, g(p, pl.n, pl.last_step(gi) + 1))
                if gi % pl.per_head == 0:
                    pe.wait_ge(vh_ready, g(p, 2, a + 1))
                    if not (first and a == 0):
                        pe.wait_ge(evicted, g(p, 4, 2 * a))
                for kt in kts:
                    for x in pl.halves(kt):
                        q0 = pl.first_query(kt, x)
                        row = 32 * (2 * (kt % 2) + x)
                        last = pe.matmul(ps[row:row + VW, 6 + x, q0 - x * BANK:BANK], vh[a][:, kt, :],
                                         ring[:, (a * pl.tiles + kt) % pl.ring, q0:(x + 1) * BANK],
                                         start=kt < 2, stop=pl.causal or kt + 2 >= pl.tiles, skip_group_check=True)
                last.then_inc(valued, 1)

            def pair(p, first):
                for s in range(pl.n):
                    scores(p, first, s)
                    for gi in range(len(pl.groups)):
                        at = pl.last_step(gi) + pl.lag
                        if at == s:
                            values(p, first, gi)
                        elif at == s + pl.n and not first:
                            values(p - 1, False, gi)

            pair(0, True)
            with pe.Fori(1, PAIRS) as p:
                pair(p, False)
            for gi in range(len(pl.groups)):
                if pl.last_step(gi) + pl.lag >= pl.n:
                    values(PAIRS - 1, False, gi)

        def exponentials(act, pl):
            n = pl.name
            scored, exped, valued = sem(n + "_scored"), sem(n + "_exped"), sem(n + "_valued")

            def pair(p, first):
                for s in range(pl.n):
                    a, kt = pl.steps[s]
                    slot, q0 = s % pl.slots, pl.first_query(kt, pl.halves(kt)[0])
                    before = s - pl.ring
                    if before >= 0:
                        act.wait_ge(valued, g(p, len(pl.groups), pl.group_of(before) + 1))
                    elif not first:
                        act.wait_ge(valued, g(p - 1, len(pl.groups), pl.group_of(before + pl.n) + 1))
                    act.wait_ge(scored, g(p, pl.n, s + 1))
                    act.activation(ring[:, s % pl.ring, q0:], flat[:, 2 * slot * BANK + q0:2 * (slot + 1) * BANK],
                                   ACT.Exp).then_inc(exped, 1)

            pair(0, True)
            with act.Fori(1, PAIRS) as p:
                pair(p, False)

        def evict(dve, pl, p, first, a):
            n = pl.name
            dve.wait_ge(sem(n + "_valued"), g(p, len(pl.groups), (a + 1) * pl.per_head))
            if not first:
                dve.wait_ge(sem(f"{n}_stored{a}"), g(p, 64, 0))
            for x in range(HALVES):
                dve.tensor_copy(oev[a][:, x, :], ps[:, 6 + x, :]).then_inc(sem(n + "_evicted"), 1)

        def head_values(pool, pl, then):
            n = pl.name

            def pair(p, first):
                for a in range(2):
                    if not first:
                        pool.wait_ge(sem(n + "_valued"), g(p - 1, len(pl.groups), (a + 1) * pl.per_head))
                    pool.tensor_copy(vh[a][:, 0:pl.tiles, :],
                                     vx[n][:, bass.ds(2 * p + a, 1), :, :].rearrange("p h t c -> p (h t) c"))\
                        .then_inc(sem(n + "_vh_ready"), 1)
                then(p, first)

            pair(0, True)
            with pool.Fori(1, PAIRS) as p:
                pair(p, False)

        def load_keys(sp, pl, p):
            n = pl.name
            for a in range(2):
                row = STACK * a
                for part in range(3):
                    terms = [i for i in range(NTERM) if KPART[i] == part]
                    src = kscr[n][bass.ds(2 * p + a, 1), part]
                    src = bass.AP(src.tensor, src.offset, [[0, len(terms)], [pl.width, HD], [1, pl.width]])
                    sp.dma_start(kst[n][row:row + HD * len(terms), bass.ds((p % 2) * pl.width, pl.width)], src)\
                        .then_inc(sem(n + "_k_loaded"), 16)
                    row += HD * len(terms)

        def store_heads(sp, pl):
            n = pl.name

            def pair(p, first, last):
                if not last:
                    if not first:
                        sp.wait_ge(sem(n + "_scored"), g(p, pl.n, 0))
                    sp.wait_ge(sem(n + "_k_loaded"), g(p, 16 * NTERM, 16 * NTERM))
                    load_keys(sp, pl, p + 1)
                for a in range(2):
                    sp.wait_ge(sem(n + "_evicted"), g(p, 4, 2 * a + 2))
                    for part in range(2):
                        for x in range(HALVES):
                            row = 32 * (2 * part + x)
                            sp.dma_start(oscr[n][part, bass.ds(2 * p + a, 1), :, x * BANK:(x + 1) * BANK]
                                         .rearrange("h c n -> (h c) n"), oev[a][row:row + VW, x, :])\
                                .then_inc(sem(f"{n}_stored{a}"), 16)

            pair(0, True, False)
            with sp.Fori(1, PAIRS - 1) as p:
                pair(p, False, False)
            pair(PAIRS - 1, False, True)
            for a in range(2):
                sp.wait_ge(sem(f"{n}_stored{a}"), g(PAIRS, 64, 0))
            for part in range(2):
                skip = P if pl.causal and part else 0
                for i, (row, step) in enumerate(((0, T), (HD, 0))):
                    src = bass.AP(oscr[n], (part * H * VW + row) * T + skip, [[VW * T, H], [step, HD], [1, T - skip]])
                    sp.dma_start(ring[:, 2 * i + part, skip:], src).then_inc(sem(n + "_gathered"), 16)

        def split(dve, ch, src, parts, tmp):
            ch.link(dve.tensor_copy(parts[0], src))
            ch.link(dve.tensor_tensor(tmp, src, parts[0], ALU.subtract))
            ch.link(dve.tensor_copy(parts[1], tmp))
            return dve.tensor_tensor(parts[2], tmp, parts[1], ALU.subtract)

        def queries_pe(pe, n, wq):
            for x in range(HALVES):
                last = pe.matmul(ps[:, x, :], wq[:, :], xT[:, x * BANK:(x + 1) * BANK], start=True, stop=True)
            last.then_inc(sem(n + "_q_projected"), 1)

        def bounds_pe(pe, n):
            for i in range(2):
                pe.wait_ge(sem(n + "_bound_terms"), i + 1)
                for x in range(HALVES):
                    last = pe.matmul(ps[0:H, 2 * i + x, :], hblk[:, :], ring[:, 2 * i, x * BANK:(x + 1) * BANK],
                                     start=True, stop=True)
                last.then_inc(sem(n + "_bounds"), 1)

        def queries_dve(dve, ch, n, bq):
            dve.wait_ge(sem(n + "_q_projected"), 1)
            ch.link(dve.tensor_scalar(qT[n][:, :], flat[:, 0:T], bq[:, :], SCALE, ALU.add, ALU.mult))
            split(dve, ch, qT[n][:, :], [qp[:, i, :] for i in range(3)], ring[:, 1, :]).then_inc(sem(n + "_q_split"), 1)

        def bounds_dve(dve, ch, n):
            q, kmax, kmin = qT[n][:, :], ext[n][:, 0:1], ext[n][:, 1:2]
            ch.link(dve.tensor_scalar(ring[:, 0, :], q, 0.0, kmax, ALU.max, ALU.mult))
            ch.link(dve.tensor_scalar(ring[:, 3, :], q, 0.0, kmin, ALU.min, ALU.mult))
            ch.link(dve.tensor_tensor(ring[:, 0, :], ring[:, 0, :], ring[:, 3, :], ALU.add))
            ch.link(dve.tensor_scalar(ring[:, 2, :], q, 0.0, kmin, ALU.max, ALU.mult))
            ch.link(dve.tensor_scalar(ring[:, 3, :], q, 0.0, kmax, ALU.min, ALU.mult))
            ch.link(dve.tensor_tensor(ring[:, 2, :], ring[:, 2, :], ring[:, 3, :], ALU.add))
            dve.tensor_tensor(ring[:, 2, :], ring[:, 0, :], ring[:, 2, :], ALU.subtract).then_inc(sem(n + "_bound_terms"), 2)
            dve.wait_ge(sem(n + "_bounds"), 1)
            dve.tensor_scalar(shift[:, :], flat[0:H, 0:T], -1.0, None, ALU.mult).then_inc(sem(n + "_shift"), 1)
            for i, (limit, op) in enumerate(((LARGEST, ALU.is_le), (-LARGEST, ALU.is_ge))):
                ch.link(dve.tensor_scalar(inr[:, :], flat[0:H, 0:T], limit, None, op))
                ch.link(dve.tensor_reduce(good[0:H, GOOD[n] + 1 + i:GOOD[n] + 2 + i], inr[:, :], AX.X, ALU.add))
            dve.wait_ge(sem(n + "_bounds"), 2)
            ch.link(dve.tensor_scalar(inr[:, :], flat[0:H, 2 * BANK:2 * BANK + T], SPREAD, None, ALU.is_le))
            dve.tensor_reduce(good[0:H, GOOD[n]:GOOD[n] + 1], inr[:, :], AX.X, ALU.add).then_inc(sem(n + "_ranged"), 1)

        def queries_sp(sp, n):
            sp.wait_ge(sem(n + "_q_split"), 1)
            for part in range(3):
                src = bass.AP(qscr[n], part * HD * T, [[3 * HD * T, H], [T, HD], [1, T]])
                sp.dma_start(src, qp[:, part, :]).then_inc(sem(n + "_q_stored"), 16)
            sp.wait_ge(sem(n + "_q_stored"), 48)
            if n == "self":
                sp.wait_ge(sem("stacks_cleared"), 3)
            for a in range(2):
                row, t = STACK * a, 0
                while t < NTERM:
                    m = 1
                    while t + m < NTERM and QPART[t + m] == QPART[t + m - 1] + 1:
                        m += 1
                    src = qscr[n][a:H:2, 0:m].rearrange("h r d n -> h (r d) n").rearrange("h r n -> r h n")
                    sp.dma_start(qs[row:row + m * HD, a:H:2, :], src).then_inc(sem(n + "_q_loaded"), 16)
                    row, t = row + m * HD, t + m
            sp.wait_ge(sem(n + "_shift"), 1)
            sp.dma_start(sscr[n][:, :], shift[:, :]).then_inc(sem(n + "_shift_stored"), 16)
            sp.wait_ge(sem(n + "_shift_stored"), 16)
            for a in range(2):
                row = STACK * a + SHIFT_ROW
                sp.dma_start(qs[row:row + 1, a:H:2, :], bass.AP(sscr[n], a * T, [[0, 1], [2 * T, PAIRS], [1, T]]))\
                    .then_inc(sem(n + "_q_loaded"), 16)

        QLOADS = 2 * 3 + 2
        LOADED = 4
        GOOD = {"self": 0, "cross": 3, "mask_sign": 6, "mask_rows": 7}
        HOLD = 6 * H * T + T * LC + LP

        def normalise_heads(dve, ch, n):
            dve.wait_ge(sem(n + "_gathered"), 64)
            ch.link(dve.tensor_tensor(ring[:, 2, :], ring[:, 2, :], ring[:, 3, :], ALU.add))
            ch.link(dve.reciprocal(ring[:, 2, :], ring[:, 2, :]))
            ch.link(dve.tensor_tensor(ring[:, 0, :], ring[:, 0, :], ring[:, 1, :], ALU.add))
            dve.tensor_tensor(ring[:, 0, :], ring[:, 0, :], ring[:, 2, :], ALU.mult).then_inc(sem(n + "_heads"), 1)

        def project_out(pe, n, wo, heads):
            pe.wait_ge(sem(n + "_heads"), 1)
            for t in range(QT):
                last = pe.matmul(ps[:, t // 4, t % 4 * P:(t % 4 + 1) * P], heads[:, t * P:(t + 1) * P], wo[:, :],
                                 start=True, stop=True)
            last.then_inc(sem(n + "_y"), 1)

        def norm_dve(dve, ch, n, dst):
            dve.wait_ge(sem(n + "_y"), 1)
            ch.link(dve.tensor_tensor(yn[:, :, :].rearrange("p t c -> p (t c)"), flat[:, 0:T],
                                      xn[:, :, :].rearrange("p t c -> p (t c)"), ALU.add))
            for t in range(QT):
                last = dve.bn_stats(st[:, t, :], yn[:, t, :])
            ch.link(last)
            for t in range(QT):
                last = dve.bn_aggr(mv[:, t, :], st[:, t, :])
            ch.link(last)
            dve.tensor_scalar(rstd[:, :], mv[:, :, 1], EPS, None, ALU.add).then_inc(sem(n + "_var"), 1)
            dve.wait_ge(sem(n + "_std"), 1)
            ch.link(dve.reciprocal(rstd[:, :], rstd[:, :]))
            for t in range(QT):
                dve.tensor_scalar(dst[:, t, :], yn[:, t, :], mv[:, t, 0:1], rstd[:, t:t + 1], ALU.subtract, ALU.mult)\
                    .then_inc(sem(n + "_normed"), 1)

        def norm_act(act, n):
            act.wait_ge(sem(n + "_var"), 1)
            act.activation(rstd[:, :], rstd[:, :], ACT.Sqrt).then_inc(sem(n + "_std"), 1)

        def turn_pe(pe, n, src):
            for t in range(QT):
                pe.wait_ge(sem(n + "_normed"), t + 1)
                last = pe.transpose(ps[:, 2 + t // 4, t % 4 * P:(t % 4 + 1) * P], src[:, t, :], ident[:, :])
            last.then_inc(sem(n + "_turned"), 1)

        def turn_dve(dve, n):
            dve.wait_ge(sem(n + "_turned"), 1)
            dve.tensor_copy(xT[:, :], flat[:, 2 * BANK:2 * BANK + T]).then_inc(sem(n + "_xT"), 1)

        srow = qs[:, :, :].rearrange("p h n -> p (h n)").bitcast(F32)
        mrow = [ring[:, :, :].rearrange("p s n -> p (s n)"), oev[0][:, :, :].rearrange("p x n -> p (x n)")]
        MR = RING * T
        heads_g = oev[1][:, :, :].rearrange("p x n -> p (x n)")
        probT = xT[:, :].rearrange("p (b n) -> p b n", b=2)
        qhead, orow = w["q1"], w["k1"]
        keys_of = {"gself": T, "gcross": LC}

        def key_chunks(n):
            return [(c, min(BANK, keys_of[n] - c)) for c in range(0, keys_of[n], BANK)]

        def key_groups(pl):
            return [list(range(k, min(k + 4, pl.tiles))) for k in range(0, pl.tiles, 4)]

        def general_pe(pe, n, pl, kT, q):
            chunks, groups = key_chunks(n), key_groups(pl)
            with pe.Fori(0, QT) as qt:
                with pe.Fori(0, H) as h:
                    it = qt * H + h
                    pe.wait_ge(sem(n + "_qhead"), it + 1)
                    for c, (k0, m) in enumerate(chunks):
                        if c >= 4:
                            pe.wait_ge(sem(n + "_masked"), it * len(chunks) + c - 3)
                        pe.matmul(ps[:, c % 4, 0:m], qhead[:, :], kT[:, k0:k0 + m], start=True, stop=True)\
                            .then_inc(sem(n + "_scored"), 1)
                    pe.wait_ge(sem(n + "_exped"), it + 1)

                    def turn(i):
                        if i >= 2:
                            pe.wait_ge(sem(n + "_probT"), it * len(groups) + i - 1)
                        for j, kt in enumerate(groups[i]):
                            last = pe.transpose(ps[:, 4 + i % 2, j * P:(j + 1) * P], srow[:, kt * P:(kt + 1) * P], ident[:, :])
                        last.then_inc(sem(n + "_turned_p"), 1)

                    turn(0)
                    for i, kts in enumerate(groups):
                        if i + 1 < len(groups):
                            turn(i + 1)
                        pe.wait_ge(sem(n + "_probT"), it * len(groups) + i + 1)
                        for j, kt in enumerate(kts):
                            last = pe.matmul(ps[:, 6, 0:HD], probT[:, i % 2, j * P:(j + 1) * P],
                                             vx[pl.name][:, bass.ds(h, 1), kt, 0:HD].rearrange("p h d -> p (h d)"),
                                             start=kt == 0, stop=kt == pl.tiles - 1)
                        last.then_inc(sem(n + "_summed"), 1)
                pe.wait_ge(sem(n + "_headed"), (qt + 1) * H)
                pe.transpose(ps[:, 7, 0:P], orow[:, :], ident[:, :]).then_inc(sem(n + "_turned_o"), 1)

        def general_act(act, n, pl):
            groups = key_groups(pl)
            with act.Fori(0, QT) as qt:
                with act.Fori(0, H) as h:
                    it = qt * H + h
                    act.wait_ge(sem(n + "_maxed"), it + 1)
                    act.activation(srow[:, 0:keys_of[n]], srow[:, 0:keys_of[n]], ACT.Exp, bias=stat[:, 1:2],
                                   accum_out=stat[:, 2:3]).then_inc(sem(n + "_exped"), 1)
                    for i, kts in enumerate(groups):
                        act.wait_ge(sem(n + "_turned_p"), it * len(groups) + i + 1)
                        if i >= 2:
                            act.wait_ge(sem(n + "_summed"), it * len(groups) + i - 1)
                        act.activation(probT[:, i % 2, 0:len(kts) * P], ps[:, 4 + i % 2, 0:len(kts) * P], ACT.Copy)\
                            .then_inc(sem(n + "_probT"), 1)

        def general_dve(dve, n, pl, q, factor):
            chunks, groups = key_chunks(n), key_groups(pl)
            with dve.Fori(0, QT) as qt:
                with dve.Fori(0, H) as h:
                    it = qt * H + h
                    dve.tensor_scalar(qhead[:, :], q[:, bass.ds(qt * P, P)], hblk[:, bass.ds(h, 1)], None, ALU.mult)\
                        .then_inc(sem(n + "_qhead"), 1)
                    dve.wait_ge(sem(n + "_mask_in"), (qt + 1) * 32)
                    for c, (k0, m) in enumerate(chunks):
                        mask = mrow[0][:, k0:k0 + m] if k0 < MR else mrow[1][:, k0 - MR:k0 - MR + m]
                        dve.wait_ge(sem(n + "_scored"), it * len(chunks) + c + 1)
                        dve.scalar_tensor_tensor(out=srow[:, k0:k0 + m], in0=mask, scalar=factor, in1=ps[:, c % 4, 0:m],
                                                 op0=ALU.mult, op1=ALU.add).then_inc(sem(n + "_masked"), 1)
                    dve.wait_ge(sem(n + "_masked"), (it + 1) * len(chunks))
                    dve.tensor_reduce(stat[:, 0:1], srow[:, 0:keys_of[n]], AX.X, ALU.max).then_inc(sem(n + "_max"), 1)
                    dve.wait_ge(sem(n + "_max"), it + 1)
                    dve.tensor_scalar(stat[:, 1:2], stat[:, 0:1], -1.0, None, ALU.mult).then_inc(sem(n + "_maxed"), 1)
                    dve.wait_ge(sem(n + "_exped"), it + 1)
                    dve.reciprocal(stat[:, 3:4], stat[:, 2:3]).then_inc(sem(n + "_inverse"), 1)
                    dve.wait_ge(sem(n + "_inverse"), it + 1)
                    dve.wait_ge(sem(n + "_summed"), (it + 1) * len(groups))
                    dve.tensor_scalar(orow[:, bass.ds(h * HD, HD)], ps[:, 6, 0:HD], stat[:, 3:4], None, ALU.mult)\
                        .then_inc(sem(n + "_headed"), 1)
                dve.wait_ge(sem(n + "_turned_o"), qt + 1)
                dve.tensor_copy(heads_g[:, bass.ds(qt * P, P)], ps[:, 7, 0:P]).then_inc(sem(n + "_heads_copied"), 1)
            dve.wait_ge(sem(n + "_heads_copied"), QT)

        def general_sp(sp, n, mask):
            wide = keys_of[n]
            cut = MR if wide > MR else wide // 2

            def load(qt):
                rows = mask[bass.ds(qt * P, P), :]
                second = mrow[1][:, 0:wide - cut] if wide > MR else mrow[0][:, cut:wide]
                sp.dma_start(mrow[0][:, 0:cut], rows[:, 0:cut]).then_inc(sem(n + "_mask_in"), 16)
                sp.dma_start(second, rows[:, cut:wide]).then_inc(sem(n + "_mask_in"), 16)

            load(0)
            with sp.Fori(1, QT) as qt:
                sp.wait_ge(sem(n + "_masked"), qt * H * len(key_chunks(n)))
                load(qt)

        def fast_failed(eng):
            eng.wait_ge(sem("flagged"), 1)
            return eng.value_load(flag[0:1, 0:1], min_val=0, max_val=1) != 0

        w1 = region_m[:, 0:HID]
        w2 = region_m[:, HID:2 * HID]
        w3 = region_m[:, 2 * HID:2 * HID + len(FCH) * D].rearrange("p (j c) -> p j c", c=D)
        wbc = [qs[:, :, :].rearrange("p h n -> p (h n)").bitcast(F32)[:, i * T:(i + 1) * T] for i in range(8)] + \
            [region_k[:, i * T:(i + 1) * T] for i in range(3)]
        WSEGS = sum((c + m - 1) // HE - c // HE + 1 for c, m in FCH[:NEXP])
        UNITS = [(j, x) for j in FORDER for x in range(HALVES)]

        def queries_sp_self(sp):
            sp.wait_ge(sem("self_k_split"), 1)
            for part in range(3):
                sp.dma_start(bass.AP(kscr["self"], part * HD * T, [[3 * HD * T, H], [T, HD], [1, T]]), kp_self[:, part, :])\
                    .then_inc(sem("self_k_stored"), 16)
            sp.wait_ge(sem("self_k_stored"), 48)
            sp.wait_ge(sem("stacks_cleared"), 3)
            for a in range(2):
                for b in range(2):
                    row = STACK * a + SHIFT_ROW
                    sp.dma_start(kst["self"][row:row + 1, b * T:(b + 1) * T], A["c_ones"][:, 0:T]).then_inc(sem("kfix_self"), 16)
            load_keys(sp, SELF, 0)
            queries_sp(sp, "self")

        def hbuf(i):
            return ring[:, i % 4, 0:BANK]

        @block.sync
        def _(sp):
            ld = lambda dst, src, s: sp.dma_start(dst, src).then_inc(sem(s), 16)
            ld(xT[:, :], A["xT"], "ld_xT")
            for n in ("q1", "k1", "v1"):
                ld(w[n][:, :], A["w_" + n], "ld_" + n)
            for n in ("q1", "k1"):
                ld(bcol[n][:, :], A["b_" + n], "ld_bcol")
            ld(brow["v1"][:, :], bass.AP(A["b_v1"].tensor, 0, [[0, P], [1, D]]), "ld_brow1")
            for i, n in enumerate(("hblk", "trib", "identb", "ident")):
                ld({"hblk": hblk, "trib": trib, "identb": identb, "ident": ident}[n][:, :], A["c_" + n], "ld_const")
            for n in ("k2", "v2"):
                ld(w[n][:, :], A["w_" + n], "ld_kv2")
            ld(bcol["k2"][:, :], A["b_k2"], "ld_kv2")
            ld(brow["v2"][:, :], bass.AP(A["b_v2"].tensor, 0, [[0, P], [1, D]]), "ld_kv2")
            queries_sp_self(sp)
            store_heads(sp, SELF)
            sp.wait_ge(sem("mask_split"), 1)
            for i in range(3):
                sp.dma_start(mscr[i, :].rearrange("(p j) -> p j", p=P), mkp[:, i, :]).then_inc(sem("mask_stored"), 16)
            sp.wait_ge(sem("k_stored"), 8 * 48)
            sp.wait_ge(sem("cross_cleared"), 1)
            sp.wait_ge(sem("mask_stored"), 48)
            for b in range(2):
                for a in range(2):
                    row = STACK * a + SHIFT_ROW
                    sp.dma_start(kst["cross"][row:row + 1, b * LP:(b + 1) * LP], A["c_ones"]).then_inc(sem("kfix_cross"), 16)
                    sp.dma_start(kst["cross"][row + 1:row + 4, b * LP:(b + 1) * LP], mscr[:, :]).then_inc(sem("kfix_cross"), 16)
            load_keys(sp, CROSS, 0)
            queries_sp(sp, "cross")
            store_heads(sp, CROSS)
            with sp.If(fast_failed(sp)):
                sp.wait_ge(sem("cross_heads"), 1)
                sp.dma_start(region_k[:, :], kTscr[:, :]).then_inc(sem("general_in"), 16)
                sp.dma_start(xn[:, :, :], A["x"][0].rearrange("(t p) c -> p t c", p=P)).then_inc(sem("general_in"), 16)
                general_sp(sp, "gself", A["c_causal"])
                sp.wait_ge(sem("gself_masked"), QT * H * len(key_chunks("gself")))
                general_sp(sp, "gcross", A["mask"])
            with sp.Else():
                sp.nop()
            sp.wait_ge(sem("wT_ready"), 1)
            sp.dma_start(wscr[:, :], wT[:, :]).then_inc(sem("w_stored"), 16)
            sp.wait_ge(sem("w_stored"), 16)
            for j, (c, m) in enumerate(FCH[:NEXP]):
                r = 0
                while r < m:
                    e = (c + r) // HE
                    k = min(m - r, (e + 1) * HE - c - r)
                    sp.dma_start(wbc[j][r:r + k, :], bass.AP(wscr, e * T, [[0, k], [1, T]])).then_inc(sem("w_spread"), 16)
                    r += k
            sp.wait_ge(sem("ffn_normed"), QT)
            sp.dma_start(out[0].rearrange("(t p) c -> p t c", p=P), yn[:, :, :]).then_inc(sem("stored"), 16)
            sp.wait_ge(sem("stored"), 16)

        @block.gpsimd
        def _(pool):
            ld = lambda dst, src, s: pool.dma_start(dst, src).then_inc(sem(s), 16)
            for i in range(0, len(CH), LOADED):
                c, m = CH[i][0], sum(m for _, m in CH[i:i + LOADED])
                ld(ctxT[:, c:c + m], A["ctxT"][:, c:c + m], f"ld_ctx{i // LOADED}")
            ld(mk[:, :], A["mask"][0, :].rearrange("(p j) -> p j", p=P), "ld_mk")
            ld(xn[:, :, :], A["x"][0].rearrange("(t p) c -> p t c", p=P), "ld_x")
            for n in ("o1", "q2", "o2"):
                ld(w[n][:, :], A["w_" + n], "ld_late")
            ld(bcol["q2"][:, :], A["b_q2"], "ld_late")
            for n in ("o1", "o2"):
                ld(brow[n][:, :], bass.AP(A["b_" + n].tensor, 0, [[0, P], [1, D]]), "ld_late")
            ld(wg[:, :], A["wg"], "ld_late")
            ld(tri8[:, :, :], bass.AP(A["c_tri8"].tensor, 0, [[0, P], [E, E], [1, E]]), "ld_late")
            pool.memset(kst["self"], 0.0).then_inc(sem("stacks_cleared"), 1)
            pool.memset(qs[:, :, :], 0.0).then_inc(sem("q_zeroed"), 1)
            pool.wait_ge(sem("q_zeroed"), 1)
            for a in range(2):
                r = STACK * a + 32
                pool.memset(qs[r:r + 32, a:H:2, :], 1.0).then_inc(sem("stacks_cleared"), 1)
                pool.wait_ge(sem("stacks_cleared"), a + 2)
            for i, n in enumerate(("self", "cross")):
                pool.memset(vx[n][:, :, :, HD:VW], 1.0).then_inc(sem("v_ones"), 1)
                pool.wait_ge(sem("v_ones"), i + 1)
            pool.wait_ge(sem("self_v_ready"), 1)

            pool.wait_ge(sem("k_evicted"), len(CH))
            pool.dma_start(kTscr[:, :], kT_cross[:, :]).then_inc(sem("kT_saved"), 16)

            def store_key_piece(p, first):
                pool.wait_ge(sem("k_split"), g(p, 1, 1))
                for part in range(3):
                    pool.dma_start(bass.AP(kscr["cross"], p * PIECE + part * HD * LP, [[3 * HD * LP, H], [LP, HD], [1, PIECE]]),
                                   kp[:, part, :]).then_inc(sem("k_stored"), 16)

            head_values(pool, SELF, store_key_piece)
            pool.wait_ge(sem("ctx_projected"), len(CH) * 2)
            pool.memset(region_k[:, :], 0.0).then_inc(sem("cross_cleared"), 1)
            pool.wait_ge(sem("k_stored"), PAIRS * 48)
            pool.wait_ge(sem("extrema"), 2 * PAIRS)
            pool.wait_ge(sem("kT_saved"), 16)
            ld(row0, bass.AP(A["mask"].tensor, 0, [[0, P], [1, LC]]), "ld_row0")
            pool.wait_ge(sem("cross_v_ready"), len(CH))
            pool.wait_ge(sem("self_valued"), g(PAIRS, len(SELF.groups), 0))

            def load_mask_rows(p, first):
                for j, (c, m) in enumerate(MPIECES):
                    if j >= 2 or not first:
                        pool.wait_ge(sem("checked"), g(p, MCOLS, j - 1))
                    pool.dma_start(mchk[j % 2][:, 0:m], A["mask"][bass.ds(p * P, P), c:c + m])\
                        .then_inc(sem(f"ld_mask{j % 2}"), 16)

            pool.wait_ge(sem("self_normed"), QT)
            head_values(pool, CROSS, load_mask_rows)
            pool.wait_ge(sem("checked"), MCOLS * PAIRS)
            for dst, src in ((w1, "w1"), (w2, "w2"), (w3, "w3")):
                ld(dst, A[src], "ld_ffn")

        @block.tensor
        def _(pe):
            pe.wait_ge(sem("ld_xT"), 16)
            pe.wait_ge(sem("ld_q1"), 16)
            queries_pe(pe, "self", w["q1"])
            pe.wait_ge(sem("ld_k1"), 16)
            for x in range(HALVES):
                last = pe.matmul(ps[:, 2 + x, :], w["k1"][:, :], xT[:, x * BANK:(x + 1) * BANK], start=True, stop=True)
            last.then_inc(sem("self_k_projected"), 1)
            pe.wait_ge(sem("ld_v1"), 16)
            for t in range(QT):
                last = pe.matmul(ps[:, 4 + t // 4, t % 4 * P:(t % 4 + 1) * P], xT[:, t * P:(t + 1) * P], w["v1"][:, :],
                                 start=True, stop=True)
            last.then_inc(sem("self_v_projected"), 1)
            pe.wait_ge(sem("ld_kv2"), 64)
            pe.wait_ge(sem("self_v_ready"), 1)
            for i, (c, m) in enumerate(CH):
                if i == 1:
                    pe.wait_ge(sem("ld_const"), 64)
                    bounds_pe(pe, "self")
                pe.wait_ge(sem(f"ld_ctx{i // LOADED}"), 16)
                if i:
                    pe.wait_ge(sem("k_evicted"), i)
                pe.matmul(ps[:, 4, 0:m], w["k2"][:, :], ctxT[:, c:c + m], start=True, stop=True).then_inc(sem("ctx_projected"), 1)
                if i:
                    pe.wait_ge(sem("cross_v_ready"), i)
                for t in range(m // P):
                    last = pe.matmul(ps[:, 5, t * P:(t + 1) * P], ctxT[:, c + t * P:c + (t + 1) * P], w["v2"][:, :],
                                     start=True, stop=True)
                last.then_inc(sem("ctx_projected"), 1)
            pe.wait_ge(sem("sums_cleared"), 1)
            pe.wait_ge(sem("self_q_loaded"), 16 * QLOADS)
            pe.wait_ge(sem("kfix_self"), 64)
            pe.wait_ge(sem("self_ranged"), 1)
            scores_and_values(pe, SELF)
            pe.wait_ge(sem("ld_late"), 16 * 8)
            project_out(pe, "self", w["o1"], ring[:, 0, :])
            turn_pe(pe, "self", xn)
            pe.wait_ge(sem("self_xT"), 1)
            queries_pe(pe, "cross", w["q2"])
            bounds_pe(pe, "cross")
            pe.wait_ge(sem("cross_q_loaded"), 16 * QLOADS)
            pe.wait_ge(sem("kfix_cross"), 128)
            pe.wait_ge(sem("cross_ranged"), 1)
            scores_and_values(pe, CROSS)
            pe.wait_ge(sem("goods_summed"), 2)
            pe.matmul(ps[0:1, 0, 0:2], ones[:, :], goods[:, :], start=True, stop=True).then_inc(sem("goods_counted"), 1)
            with pe.If(fast_failed(pe)):
                general_pe(pe, "gself", SELF, kT_self[:, :], qT["self"])
                project_out(pe, "gself", w["o1"], heads_g)
                turn_pe(pe, "gself", xn)
                pe.wait_ge(sem("gself_xT"), 1)
                queries_pe(pe, "gcross", w["q2"])
                general_pe(pe, "gcross", CROSS, region_k[:, :], qT["cross"])
                pe.wait_ge(sem("general_done"), 1)
            with pe.Else():
                pe.nop()
            project_out(pe, "cross", w["o2"], ring[:, 0, :])
            turn_pe(pe, "cross", xn)
            pe.wait_ge(sem("cross_xT"), 1)
            for t in range(QT):
                last = pe.matmul(ps[:, 4, t * E:(t + 1) * E], xT[:, t * P:(t + 1) * P], wg[:, :], start=True, stop=True)
            last.then_inc(sem("routed"), 1)
            pe.wait_ge(sem("ld_ffn"), 48)

            def hidden(i):
                j, x = UNITS[i]
                c, m = FCH[j]
                if i >= 3:
                    pe.wait_ge(sem("gated"), i - 2)
                if i == 2:
                    pe.wait_ge(sem("wT_ready"), 1)
                for k, wk in enumerate((w1, w2)):
                    last = pe.matmul(ps[0:m, 2 * (i % 3) + k, :], wk[:, c:c + m], xT[:, x * BANK:(x + 1) * BANK],
                                     start=True, stop=True)
                last.then_inc(sem("hidden"), 1)

            def down(i):
                j, x = UNITS[i]
                c, m = FCH[j]
                if j >= NEXP:
                    pe.wait_ge(sem("gated"), i + 1)
                else:
                    pe.wait_ge(sem("activated"), i + 1 - 2 * (len(FCH) - NEXP))
                pe.matmul(ps[:, 6 + x, :], w3[0:m, j, :], hbuf(i)[0:m, :], start=j == FORDER[0],
                          stop=j == FORDER[-1]).then_inc(sem("down"), 1)

            hidden(0)
            hidden(1)
            pe.wait_ge(sem("sel_ready"), 1)
            for t in range(QT):
                last = pe.transpose(ps[0:E, 4 + t // 4, t % 4 * P:(t % 4 + 1) * P], sel[:, t, :], ident[:, :])
            last.then_inc(sem("wT_turned"), 1)
            for i in range(2, len(UNITS) + 2):
                if i < len(UNITS):
                    hidden(i)
                down(i - 2)
            pe.wait_ge(sem("yT_copied"), 1)
            for t in range(QT):
                last = pe.transpose(ps[:, t // 4, t % 4 * P:(t % 4 + 1) * P], ring[:, 5, t * P:(t + 1) * P], ident[:, :])
            last.then_inc(sem("ffn_y"), 1)

        @block.scalar
        def _(act):
            exponentials(act, SELF)
            norm_act(act, "self")
            exponentials(act, CROSS)
            with act.If(fast_failed(act)):
                general_act(act, "gself", SELF)
                norm_act(act, "gself")
                general_act(act, "gcross", CROSS)
            with act.Else():
                act.nop()
            norm_act(act, "cross")
            act.wait_ge(sem("logits_shifted"), 1)
            act.activation(lg[:, :, :], lg[:, :, :], ACT.Exp).then_inc(sem("logits_exped"), 1)
            for i, (j, x) in enumerate(UNITS):
                m = FCH[j][1]
                act.wait_ge(sem("hidden"), i + 1)
                if i >= 4:
                    act.wait_ge(sem("down"), i - 3)
                act.activation(hbuf(i)[0:m, :], ps[0:m, 2 * (i % 3), :], ACT.Silu).then_inc(sem("silued"), 1)
            norm_act(act, "ffn")

        @block.vector
        def _(dve):
            ch = Chain(dve, "dve_chain")
            ch.link(dve.memset(good[:, :], 0.0))
            dve.memset(ps[:, 6:8, :], 0.0).then_inc(sem("sums_cleared"), 1)
            dve.wait_ge(sem("ld_bcol"), 32)
            queries_dve(dve, ch, "self", bcol["q1"])
            dve.wait_ge(sem("self_k_projected"), 1)
            ch.link(dve.tensor_scalar(kT_self[:, :], flat[:, 2 * BANK:2 * BANK + T], bcol["k1"][:, :], None, ALU.add))
            split(dve, ch, kT_self[:, :], [kp_self[:, i, :] for i in range(3)], ring[:, 1, :]).then_inc(sem("self_k_split"), 1)
            dve.wait_ge(sem("self_v_projected"), 1)
            dve.wait_ge(sem("ld_brow1"), 16)
            dve.wait_ge(sem("v_ones"), 2)
            for t in range(QT):
                last = dve.tensor_tensor(vx["self"][:, :, t, 0:HD],
                                         ps[:, 4 + t // 4, t % 4 * P:(t % 4 + 1) * P].rearrange("p (h d) -> p h d", d=HD),
                                         brow["v1"][:, :].rearrange("p (h d) -> p h d", d=HD), ALU.add)
            last.then_inc(sem("self_v_ready"), 1)
            ch.link(dve.tensor_reduce(ext["self"][:, 0:1], kT_self[:, :], AX.X, ALU.max))
            ch.link(dve.tensor_reduce(ext["self"][:, 1:2], kT_self[:, :], AX.X, ALU.min))
            bounds_dve(dve, ch, "self")
            dve.wait_ge(sem("ld_kv2"), 64)
            for i, (c, m) in enumerate(CH):
                dve.wait_ge(sem("ctx_projected"), 2 * i + 1)
                dve.tensor_scalar(kT_cross[:, c:c + m], ps[:, 4, 0:m], bcol["k2"][:, :], None, ALU.add).then_inc(sem("k_evicted"), 1)
                dve.wait_ge(sem("ctx_projected"), 2 * i + 2)
                n = m // P
                for t in range(n):
                    last = dve.tensor_tensor(vx["cross"][:, :, 4 * i + t, 0:HD],
                                             ps[:, 5, t * P:(t + 1) * P].rearrange("p (h d) -> p h d", d=HD),
                                             brow["v2"][:, :].rearrange("p (h d) -> p h d", d=HD), ALU.add)
                last.then_inc(sem("cross_v_ready"), 1)
            dve.wait_ge(sem("ld_mk"), 16)
            ch.link(dve.tensor_scalar(mku[:, :], mk[:, :], MASKED, None, ALU.mult))
            split(dve, ch, mku[:, :], [mkp[:, i, :] for i in range(3)], mku[:, :]).then_inc(sem("mask_split"), 1)
            W = LP // 8
            dve.wait_ge(sem("k_evicted"), len(CH))
            for p in range(PAIRS):
                c = p * W
                if p:
                    dve.wait_ge(sem("k_stored"), 48 * p)
                else:
                    dve.wait_ge(sem("self_k_stored"), 48)
                src, parts, tmp = kT_cross[:, c:c + W], [kp[:, i, :] for i in range(3)], kp_tmp
                ch.link(dve.tensor_copy(parts[0], src))
                ch.link(dve.tensor_tensor(tmp, src, parts[0], ALU.subtract))
                evict(dve, SELF, p, p == 0, 0)
                ch.link(dve.tensor_copy(parts[1], tmp))
                dve.tensor_tensor(parts[2], tmp, parts[1], ALU.subtract).then_inc(sem("k_split"), 1)
                n = min(W, LC - c)
                dve.tensor_reduce(extc[:, 0, p:p + 1], kT_cross[:, c:c + n], AX.X, ALU.max).then_inc(sem("extrema"), 1)
                dve.tensor_reduce(extc[:, 1, p:p + 1], kT_cross[:, c:c + n], AX.X, ALU.min).then_inc(sem("extrema"), 1)
                evict(dve, SELF, p, p == 0, 1)
            dve.wait_ge(sem("extrema"), 2 * PAIRS)
            ch.link(dve.tensor_reduce(ext["cross"][:, 0:1], extc[:, 0, :], AX.X, ALU.max))
            ch.link(dve.tensor_reduce(ext["cross"][:, 1:2], extc[:, 1, :], AX.X, ALU.min))
            dve.wait_ge(sem("ld_x"), 16)
            dve.wait_ge(sem("ld_late"), 16 * 8)
            for t in range(QT):
                last = dve.tensor_tensor(xn[:, t, :], xn[:, t, :], brow["o1"][:, :], ALU.add)
            ch.link(last)
            dve.wait_ge(sem("self_valued"), g(PAIRS, len(SELF.groups), 0))
            dve.memset(ring[:, 1, 0:P], 0.0)
            ch.link(dve.memset(ring[:, 3, 0:P], 0.0))
            normalise_heads(dve, ch, "self")
            norm_dve(dve, ch, "self", xn)
            turn_dve(dve, "self")
            queries_dve(dve, ch, "cross", bcol["q2"])
            bounds_dve(dve, ch, "cross")
            for t in range(QT):
                last = dve.tensor_tensor(xn[:, t, :], xn[:, t, :], brow["o2"][:, :], ALU.add)
            ch.link(last)
            ch.link(dve.memset(ones[:, :], 1.0))
            ch.link(dve.tensor_scalar(mku[:, :], mk[:, :], 0.0, None, ALU.is_ge))
            ch.link(dve.tensor_reduce(good[:, GOOD["mask_sign"]:GOOD["mask_sign"] + 1], mku[:, :], AX.X, ALU.add))
            ch.link(dve.tensor_scalar(mku[:, :], mk[:, :], 0.0, None, ALU.is_equal))
            dve.tensor_reduce(goods[:, 1:2], mku[:, :], AX.X, ALU.add).then_inc(sem("goods_summed"), 1)
            dve.wait_ge(sem("ld_row0"), 16)

            def check_mask(p, j):
                c, m = MPIECES[j]
                piece = mchk[j % 2][:, 0:m]
                dve.wait_ge(sem(f"ld_mask{j % 2}"), g(p, 8 * MCOLS, 16 * (j // 2 + 1)))
                dve.tensor_tensor(piece, piece, row0[:, c:c + m], ALU.is_equal).then_inc(sem("compared"), 1)
                dve.wait_ge(sem("compared"), g(p, MCOLS, j + 1))
                dve.tensor_reduce(good[:, bass.ds(p * MCOLS + GOOD["mask_rows"] + j, 1)], piece, AX.X, ALU.add)\
                    .then_inc(sem("checked"), 1)

            def cross_pair(p, first):
                for a in range(2):
                    for j in range(a * MCOLS // 2, (a + 1) * MCOLS // 2):
                        check_mask(p, j)
                    evict(dve, CROSS, p, first, a)

            cross_pair(0, True)
            with dve.Fori(1, PAIRS) as p:
                cross_pair(p, False)
            dve.wait_ge(sem("checked"), MCOLS * PAIRS)
            dve.tensor_reduce(goods[:, 0:1], good[:, :], AX.X, ALU.add).then_inc(sem("goods_summed"), 1)
            dve.wait_ge(sem("goods_counted"), 1)
            ch.link(dve.tensor_scalar(held[:, 0:1], ps[0:1, 0, 0:1], float(HOLD), None, ALU.not_equal))
            ch.link(dve.tensor_scalar(held[:, 1:2], ps[0:1, 0, 1:2], 0.5, None, ALU.is_lt))
            dve.tensor_tensor(flag[:, :], held[:, 0:1], held[:, 1:2], ALU.max).then_inc(sem("flagged"), 1)
            normalise_heads(dve, ch, "cross")
            with dve.If(fast_failed(dve)):
                gch = Chain(dve, "dve_general_chain")
                dve.wait_ge(sem("general_in"), 32)
                dve.wait_ge(sem("cross_heads"), 1)
                general_dve(dve, "gself", SELF, qT["self"], -float(np.finfo(np.float32).max))
                for t in range(QT):
                    last = dve.tensor_tensor(xn[:, t, :], xn[:, t, :], brow["o1"][:, :], ALU.add)
                last.then_inc(sem("gself_heads"), 1)
                dve.wait_ge(sem("gself_heads"), 1)
                norm_dve(dve, gch, "gself", xn)
                turn_dve(dve, "gself")
                dve.wait_ge(sem("gcross_q_projected"), 1)
                gch.link(dve.tensor_scalar(qT["cross"][:, :], flat[:, 0:T], bcol["q2"][:, :], SCALE, ALU.add, ALU.mult))
                for t in range(QT):
                    last = dve.tensor_tensor(xn[:, t, :], xn[:, t, :], brow["o2"][:, :], ALU.add)
                gch.link(last)
                gch.link(dve.memset(srow[:, LC:LP], 0.0))
                general_dve(dve, "gcross", CROSS, qT["cross"], MASKED)
                dve.tensor_copy(ring[:, 0, :], heads_g).then_inc(sem("general_done"), 1)
                dve.wait_ge(sem("general_done"), 1)
            with dve.Else():
                dve.nop()
            norm_dve(dve, ch, "cross", xn)
            turn_dve(dve, "cross")
            dve.wait_ge(sem("routed"), 1)
            ch.link(dve.tensor_copy(lg[:, :, :].rearrange("p t e -> p (t e)"), ps[:, 4, 0:QT * E]))
            lj = bass.AP(lg, 0, [[QT * E, P], [E, QT], [0, E], [1, E]])
            le = bass.AP(lg, 0, [[QT * E, P], [E, QT], [1, E], [0, E]])
            low = bass.AP(tri8, 0, [[E * E, P], [0, QT], [E, E], [1, E]])
            ch.link(dve.tensor_tensor(rk[0], lj, le, ALU.is_ge))
            ch.link(dve.tensor_tensor(rk[0], rk[0], low, ALU.mult))
            ch.link(dve.tensor_tensor(rk[1], lj, le, ALU.is_gt))
            ch.link(dve.tensor_tensor(rk[0], rk[0], rk[1], ALU.max))
            ch.link(dve.tensor_reduce(sel[:, :, :], rk[0], AX.X, ALU.add))
            ch.link(dve.tensor_reduce(mx8[:, :], lg[:, :, :], AX.X, ALU.max))
            ch.link(dve.tensor_scalar(sel[:, :, :], sel[:, :, :], 2.0, None, ALU.is_lt))
            dve.tensor_tensor(lg[:, :, :], lg[:, :, :], bass.AP(mx8, 0, [[QT, P], [1, QT], [0, E]]), ALU.subtract)\
                .then_inc(sem("logits_shifted"), 1)
            dve.wait_ge(sem("logits_exped"), 1)
            ch.link(dve.tensor_tensor(sel[:, :, :], sel[:, :, :], lg[:, :, :], ALU.mult))
            ch.link(dve.tensor_reduce(mx8[:, :], sel[:, :, :], AX.X, ALU.add))
            ch.link(dve.reciprocal(mx8[:, :], mx8[:, :]))
            dve.tensor_tensor(sel[:, :, :], sel[:, :, :], bass.AP(mx8, 0, [[QT, P], [1, QT], [0, E]]), ALU.mult)\
                .then_inc(sem("sel_ready"), 1)
            dve.wait_ge(sem("wT_turned"), 1)
            dve.tensor_copy(wT[:, :], flat[0:E, 4 * BANK:4 * BANK + T]).then_inc(sem("wT_ready"), 1)
            for i, (j, x) in enumerate(UNITS):
                m = FCH[j][1]
                h = hbuf(i)[0:m, :]
                dve.wait_ge(sem("silued"), i + 1)
                if j >= NEXP:
                    dve.tensor_tensor(h, ps[0:m, 2 * (i % 3) + 1, :], h, ALU.mult).then_inc(sem("gated"), 1)
                else:
                    dve.tensor_tensor(h, ps[0:m, 2 * (i % 3) + 1, :], h, ALU.mult).then_inc(sem("gated"), 1)
                    dve.wait_ge(sem("gated"), i + 1)
                    dve.wait_ge(sem("w_spread"), 16 * WSEGS)
                    dve.tensor_tensor(h, h, wbc[j][0:m, x * BANK:(x + 1) * BANK], ALU.mult).then_inc(sem("activated"), 1)
            dve.wait_ge(sem("down"), len(UNITS))
            dve.tensor_copy(ring[:, 5, :], flat[:, 6 * BANK:8 * BANK]).then_inc(sem("yT_copied"), 1)
            norm_dve(dve, ch, "ffn", yn)



def kernel(**inputs):
    import numpy as _np
    import ml_dtypes as _ml
    import concourse.bacc as _bacc
    from concourse import mybir as _mybir
    from concourse.bass_utils import run_bass_kernel_spmd as _run

    i = {k: _np.asarray(v) for k, v in inputs.items()}
    bf = _ml.bfloat16
    f = _np.float32
    ctx = _np.zeros((LP, D), f)
    ctx[:LC] = i["ctx_1024"][0]
    mask = _np.ones((T, LP), f)
    mask[:, :LC] = i["mask_Bx1xSxS2_fk0"][0, 0]
    cat = lambda a, s: _np.concatenate([_np.transpose(i[a], (1, 0, 2)).reshape(D, E * HE), i[s]], 1)
    w3 = _np.zeros((len(FCH) * P, D), f)
    w3[:HID] = _np.concatenate([i["L0_ffn_W3"].reshape(E * HE, D), i["L0_ffn_Ws3"]], 0)
    arrays = {
        "x": i["x"], "xT": i["x"][0].T, "ctxT": ctx.T, "mask": mask,
        "w_q1": i["L0_attn_wq"], "w_k1": i["L0_attn_wk"], "w_v1": i["L0_attn_wv"], "w_o1": i["L0_attn_wo"],
        "w_q2": i["L0_xattn_Wq"].T, "w_k2": i["L0_xattn_Wk"].T, "w_v2": i["L0_xattn_Wv"].T, "w_o2": i["L0_xattn_Wo"].T,
        "b_q1": i["L0_attn_bq"][:, None], "b_k1": i["L0_attn_bk"][:, None],
        "b_q2": i["L0_xattn_bq"][:, None], "b_k2": i["L0_xattn_bk"][:, None],
        "b_v1": i["L0_attn_bv"][None], "b_o1": i["L0_attn_bo"][None],
        "b_v2": i["L0_xattn_bv"][None], "b_o2": i["L0_xattn_bo"][None],
        "wg": i["L0_ffn_Wg"], "w1": cat("L0_ffn_W1", "L0_ffn_Ws1"), "w2": cat("L0_ffn_W2", "L0_ffn_Ws2"),
        "w3": w3.reshape(len(FCH), P, D).transpose(1, 0, 2),
        "c_ones": _np.ones((1, LP), bf), "c_ident": _np.eye(P, dtype=f), "c_identb": _np.eye(P).astype(bf),
        "c_trib": _np.where(_np.arange(P)[None, :] < _np.arange(P)[:, None], -1e30, 0.0).astype(bf),
        "c_hblk": (_np.arange(P)[:, None] // HD == _np.arange(H)[None, :]).astype(f),
        "c_causal": (_np.arange(T)[None, :] > _np.arange(T)[:, None]).astype(f),
        "c_tri8": (_np.arange(E)[None, :] < _np.arange(E)[:, None]).astype(f),
    }
    nc = _bacc.Bacc("TRN2", target_bir_lowering=False, num_devices=1)
    sent, args = {}, {}
    for name, a in arrays.items():
        a = _np.ascontiguousarray(a)
        sent[f"in_{name}"] = a
        args[name] = nc.dram_tensor(f"in_{name}", a.shape, _mybir.dt.from_np(a.dtype), kind="ExternalInput").ap()
    out = nc.dram_tensor("out_0", (1, T, D), _mybir.dt.float32, kind="ExternalOutput").ap()
    nc.disable_value_cache = True
    build(nc, args, out)
    r = _run(nc, [sent], core_ids=[0])
    return r.results[0]["out_0"]
```

```python
from contextlib import ExitStack

import numpy as np

import concourse.bass as bass
from concourse import mybir

F32 = mybir.dt.float32
BF16 = mybir.dt.bfloat16
I32 = mybir.dt.int32
ALU = mybir.AluOpType
ACT = mybir.ActivationFunctionType
AX = mybir.AxisListType

P = 128
BANK = 512
T = 1024
D = 128
H = 16
HD = D // H
PAIRS = H // 2
QT = T // P
HALVES = T // BANK
LC = 6404
NC_ = -(-LC // P)
LP = NC_ * P
CH = [(c, min(BANK, LP - c)) for c in range(0, LP, BANK)]
E, HE, HS = 8, 176, 352
HID = E * HE + HS
FCH = [(c, min(P, HID - c)) for c in range(0, HID, P)]
FORDER = [j for j, (c, _) in enumerate(FCH) if c >= E * HE] + [j for j, (c, _) in enumerate(FCH) if c < E * HE]
NEXP = sum(c < E * HE for c, _ in FCH)
SCALE = float(1.0 / np.sqrt(np.float32(HD)))
MASKED = -1.0e9
EPS = 1e-5
SPREAD = 60.0
LARGEST = 1024.0
VW = HD + 1

QPART = (0, 1, 2, 0, 1, 0)
KPART = (0, 0, 0, 1, 1, 2)
NTERM = len(QPART)
STACK = 64
ONES_PAIR = float(np.array([0x3F803F80], np.uint32).view(np.float32)[0])
SHIFT_ROW = NTERM * HD
MASK_ROW = SHIFT_ROW + 1
RING = 6
SLOTS = 3
LAG = SLOTS - 1


class Plan:

    def __init__(self, name, tiles, ring, causal):
        self.name, self.tiles, self.ring, self.causal = name, tiles, ring, causal
        self.width = tiles * P
        packed = [k for k in range(tiles) if causal and k * P >= BANK]
        self.steps = []
        for a in range(2):
            for kt in range(tiles - len(packed)):
                pieces = [(kt, x, self.first_query(kt, x), self.first_query(kt, x)) for x in range(HALVES)]
                self.steps.append((a, [q for q in pieces if q[2] < (q[1] + 1) * BANK]))
            for kt in packed[::2]:
                q = [self.first_query(k, 1) for k in (kt, kt + 1)]
                self.steps.append((a, [(kt, 1, q[0], BANK), (kt + 1, 1, q[1], q[1] - BANK)]))
        self.n = len(self.steps)
        assert self.n % SLOTS == 0 and self.n % self.ring == 0
        self.groups = [(a, list(range(k, min(k + 2, tiles)))) for a in range(2) for k in range(0, tiles, 2)]
        self.per_head = len(self.groups) // 2

    def group_of(self, s):
        a, pieces = self.steps[s]
        return a * self.per_head + pieces[0][0] // 2

    def last_step(self, g):
        return max(s for s in range(self.n) if self.group_of(s) == g)

    def span(self, s):
        pieces = self.steps[s][1]
        return min(at for _, _, _, at in pieces), max(at + (x + 1) * BANK - q0 for _, x, q0, at in pieces)

    def first_query(self, kt, half):
        return max(half * BANK, kt * P if self.causal else 0)

    def pieces_of(self, g):
        a, kts = self.groups[g]
        return sorted(((s, q) for s, (b, pieces) in enumerate(self.steps) if b == a for q in pieces if q[0] in kts),
                      key=lambda i: i[1][:2])


SELF = Plan("self", T // P, 4, True)
CROSS = Plan("cross", NC_, RING, False)


def build(nc, A, out):
    ctx = ExitStack()
    with ctx:
        def sb(name, shape, dt=F32):
            return ctx.enter_context(nc.sbuf_tensor(name, shape, dt))

        def dram(name, shape, dt):
            return nc.dram_tensor(name, shape, dt)

        sems = {}

        def sem(name):
            if name not in sems:
                sems[name] = ctx.enter_context(nc.semaphore(name))
            return sems[name]

        class Chain:

            def __init__(self, eng, name):
                self.eng, self.sem, self.n = eng, sem(name), 0

            def link(self, ins):
                self.n += 1
                ins.then_inc(self.sem, 1)
                self.eng.wait_ge(self.sem, self.n)

        ps = ctx.enter_context(nc.psum_tensor("ps", [P, 8, BANK], F32))
        flat = ps[:, :, :].rearrange("p b n -> p (b n)")
        region_k = sb("region_k", [P, LP])
        region_m = sb("region_m", [P, LP])
        ctxT = region_k
        kT_cross = region_m
        kst = {"cross": region_k[:, :].bitcast(BF16), "self": sb("kst_self", [P, 2 * T], BF16)[:, :]}
        qs = sb("qs", [P, H, T], BF16)
        ring = sb("ring", [P, RING, T])
        vx = {"self": sb("vx_self", [P, H, SELF.tiles, VW]), "cross": sb("vx_cross", [P, H, CROSS.tiles, VW])}
        vh = [sb(f"vh{a}", [P, NC_, VW]) for a in range(2)]
        oev = [sb(f"oev{a}", [P, HALVES, BANK]) for a in range(2)]
        PIECE = LP // PAIRS
        spare = ring[:, 4:6, :].rearrange("p s n -> p (s n)")
        kp_tmp = spare[:, 0:PIECE]
        kp = spare[:, PIECE:PIECE + 3 * PIECE // 2].bitcast(BF16).rearrange("p (i n) -> p i n", i=3)
        qp = sb("qp", [P, 3, T], BF16)
        kp_self = spare[:, 0:3 * T // 2].bitcast(BF16).rearrange("p (i n) -> p i n", i=3)
        qT = {"self": sb("qT_self", [P, T]), "cross": sb("qT_cross", [P, T])}
        kT_self = sb("kT_self", [P, T])
        xT = sb("xT", [P, T])
        xn = sb("xn", [P, QT, D])
        yn = sb("yn", [P, QT, D])
        w = {n: sb("w_" + n, [P, D]) for n in ("q1", "k1", "v1", "o1", "q2", "k2", "v2", "o2")}
        bcol = {n: sb("b_" + n, [P, 1]) for n in ("q1", "k1", "q2", "k2")}
        brow = {n: sb("b_" + n, [P, D]) for n in ("v1", "o1", "v2", "o2")}
        ident = sb("ident", [P, P])
        qs32 = qs[:, :, :].rearrange("p h n -> p (h n)").bitcast(F32).rearrange("p (h n) -> p h n", h=H)
        identb = sb("identb", [P, P], BF16)
        trib = sb("trib", [P, P], BF16)
        hblk = sb("hblk", [P, H])
        ext = {n: sb("ext_" + n, [P, 2]) for n in ("self", "cross")}
        extent = sb("extent", [P, 1])
        extc = sb("extc", [P, 2, 8])
        shift = sb("shift", [H, T], BF16)
        inr = sb("inr", [H, T])
        good = sb("good", [P, 72])
        mk = sb("mk", [P, NC_])
        mku = sb("mku", [P, NC_])
        mkp = sb("mkp", [P, 3, NC_], BF16)
        st = sb("st", [P, QT, 6])
        mv = sb("mv", [P, QT, 2])
        rstd = sb("rstd", [P, QT])
        wg = sb("wg", [P, E])
        tri8 = sb("tri8", [P, E, E])
        lg = sb("lg", [P, QT, E])
        mx8 = sb("mx8", [P, QT])
        rk = [spare[:, i * QT * E * E:(i + 1) * QT * E * E].rearrange("p (t e j) -> p t e j", e=E, j=E) for i in range(2)]
        sel = sb("sel", [P, QT, E])
        wT = sb("wT", [E, T])
        ones = sb("ones", [P, 1])
        goods = sb("goods", [P, 2])
        held = sb("held", [1, 4])
        flag = sb("flag", [1, 1], I32)
        stat = sb("stat", [P, 4])
        MW = -(-LC // 8)
        MPIECES = [(c, min(MW, LC - c)) for c in range(0, LC, MW)]
        MCOLS = len(MPIECES)
        mchk = [kst["self"].bitcast(F32), yn[:, :, :].rearrange("p t c -> p (t c)")]
        row0 = region_m[:, 0:LC]

        qscr = {n: dram("qscr_" + n, [H, 3, HD, T], BF16) for n in ("self", "cross")}
        kscr = {"self": dram("kscr_self", [H, 3, HD, T], BF16), "cross": dram("kscr_cross", [H, 3, HD, LP], BF16)}
        sscr = {n: dram("sscr_" + n, [H, T], BF16) for n in ("self", "cross")}
        mscr = dram("mscr", [3, LP], BF16)
        oscr = {n: dram("oscr_" + n, [2, H, VW, T], F32) for n in ("self", "cross")}
        wscr = dram("wscr", [E, T], F32)
        kTscr = dram("kTscr", [P, LP], F32)

        block = ctx.enter_context(nc.Block())
        g = lambda pair, per, off: pair * per + off

        def scores_and_values(pe, pl):
            n = pl.name
            scored, exped, valued = sem(n + "_scored"), sem(n + "_exped"), sem(n + "_valued")
            evicted, vh_ready, k_loaded = sem(n + "_evicted"), sem(n + "_vh_ready"), sem(n + "_k_loaded")

            def scores(p, first, s):
                a, pieces = pl.steps[s]
                if not (first and s < SLOTS):
                    pe.wait_ge(exped, g(p, pl.n, s - SLOTS + 1))
                if s == 0:
                    pe.wait_ge(k_loaded, g(p, 16 * NTERM, 16 * NTERM))
                for kt, x, q0, at in pieces:
                    keys = kst[n][:, bass.ds((p % 2) * pl.width + kt * P, P)]
                    queries = lambda lo, hi: qs[:, bass.ds(2 * p + a, 1), lo:hi].rearrange("p h n -> p (h n)")
                    at += 2 * (s % SLOTS) * BANK
                    if pl.causal and q0 == kt * P:
                        pe.matmul(flat[:, at:at + P], identb[:, :], trib[:, :], start=True, stop=False)
                        last = pe.matmul(flat[:, at:at + P], keys, queries(q0, q0 + P), start=False, stop=True)
                        q0, at = q0 + P, at + P
                    m = (x + 1) * BANK - q0
                    if m:
                        last = pe.matmul(flat[:, at:at + m], keys, queries(q0, q0 + m), start=True, stop=True)
                last.then_inc(scored, 1)

            def values(p, first, gi):
                a, kts = pl.groups[gi]
                pe.wait_ge(exped, g(p, pl.n, pl.last_step(gi) + 1))
                if gi % pl.per_head == 0:
                    pe.wait_ge(vh_ready, g(p, 2, a + 1))
                    if not (first and a == 0):
                        pe.wait_ge(evicted, g(p, 4, 2 * a))
                if first and gi == 0:
                    pe.wait_ge(sem(n + "_ranged"), 1)
                for s, (kt, x, q0, at) in pl.pieces_of(gi):
                    row = 32 * (2 * (kt % 2) + x)
                    last = pe.matmul(ps[row:row + VW, 6 + x, q0 - x * BANK:BANK], vh[a][:, kt, :],
                                     ring[:, s % pl.ring, at:at + (x + 1) * BANK - q0],
                                     start=kt < 2, stop=pl.causal or kt + 2 >= pl.tiles, skip_group_check=True)
                last.then_inc(valued, 1)

            def pair(p, first):
                for s in range(pl.n):
                    scores(p, first, s)
                    for gi in range(len(pl.groups)):
                        at = pl.last_step(gi) + LAG
                        if at == s:
                            values(p, first, gi)
                        elif at == s + pl.n and not first:
                            values(p - 1, False, gi)

            pair(0, True)
            pe.wait_ge(sem(n + "_q_loaded1"), 16 * QLOADS)
            with pe.Fori(1, PAIRS) as p:
                pair(p, False)
            for gi in range(len(pl.groups)):
                if pl.last_step(gi) + LAG >= pl.n:
                    values(PAIRS - 1, False, gi)

        def exponentials(act, pl):
            n = pl.name
            scored, exped, valued = sem(n + "_scored"), sem(n + "_exped"), sem(n + "_valued")

            def pair(p, first):
                for s in range(pl.n):
                    at = 2 * (s % SLOTS) * BANK
                    lo, hi = pl.span(s)
                    before = s - pl.ring
                    if before >= 0:
                        act.wait_ge(valued, g(p, len(pl.groups), pl.group_of(before) + 1))
                    elif not first:
                        act.wait_ge(valued, g(p - 1, len(pl.groups), pl.group_of(before + pl.n) + 1))
                    act.wait_ge(scored, g(p, pl.n, s + 1))
                    act.activation(ring[:, s % pl.ring, lo:hi], flat[:, at + lo:at + hi], ACT.Exp).then_inc(exped, 1)

            pair(0, True)
            with act.Fori(1, PAIRS) as p:
                pair(p, False)

        def evict(dve, pl, p, first, a):
            n = pl.name
            dve.wait_ge(sem(n + "_valued"), g(p, len(pl.groups), (a + 1) * pl.per_head))
            if not first:
                dve.wait_ge(sem(f"{n}_stored{a}"), g(p, 64, 0))
            for x in range(HALVES):
                dve.tensor_copy(oev[a][:, x, :], ps[:, 6 + x, :]).then_inc(sem(n + "_evicted"), 1)

        def head_values(pool, pl, then):
            n = pl.name

            def pair(p, first):
                for a in range(2):
                    if not first:
                        pool.wait_ge(sem(n + "_valued"), g(p - 1, len(pl.groups), (a + 1) * pl.per_head))
                    pool.tensor_copy(vh[a][:, 0:pl.tiles, :],
                                     vx[n][:, bass.ds(2 * p + a, 1), :, :].rearrange("p h t c -> p (h t) c"))\
                        .then_inc(sem(n + "_vh_ready"), 1)
                then(p, first)

            pair(0, True)
            with pool.Fori(1, PAIRS) as p:
                pair(p, False)

        def load_keys(sp, pl, p):
            n = pl.name
            for a in range(2):
                row = STACK * a
                for part in range(3):
                    terms = [i for i in range(NTERM) if KPART[i] == part]
                    src = kscr[n][bass.ds(2 * p + a, 1), part]
                    src = bass.AP(src.tensor, src.offset, [[0, len(terms)], [pl.width, HD], [1, pl.width]])
                    sp.dma_start(kst[n][row:row + HD * len(terms), bass.ds((p % 2) * pl.width, pl.width)], src)\
                        .then_inc(sem(n + "_k_loaded"), 16)
                    row += HD * len(terms)

        def store_heads(sp, pl):
            n = pl.name

            def pair(p, first, last):
                if not last:
                    if not first:
                        sp.wait_ge(sem(n + "_scored"), g(p, pl.n, 0))
                    sp.wait_ge(sem(n + "_k_loaded"), g(p, 16 * NTERM, 16 * NTERM))
                    load_keys(sp, pl, p + 1)
                for a in range(2):
                    sp.wait_ge(sem(n + "_evicted"), g(p, 4, 2 * a + 2))
                    for part in range(2):
                        for x in range(HALVES):
                            row = 32 * (2 * part + x)
                            sp.dma_start(oscr[n][part, bass.ds(2 * p + a, 1), :, x * BANK:(x + 1) * BANK]
                                         .rearrange("h c n -> (h c) n"), oev[a][row:row + VW, x, :])\
                                .then_inc(sem(f"{n}_stored{a}"), 16)

            pair(0, True, False)
            with sp.Fori(1, PAIRS - 1) as p:
                pair(p, False, False)
            pair(PAIRS - 1, False, True)
            for a in range(2):
                sp.wait_ge(sem(f"{n}_stored{a}"), g(PAIRS, 64, 0))
            for part in range(2):
                skip = P if pl.causal and part else 0
                for i, (row, step) in enumerate(((0, T), (HD, 0))):
                    src = bass.AP(oscr[n], (part * H * VW + row) * T + skip, [[VW * T, H], [step, HD], [1, T - skip]])
                    sp.dma_start(ring[:, 2 * i + part, skip:], src).then_inc(sem(n + "_gathered"), 16)

        def split(dve, ch, src, parts, tmp):
            ch.link(dve.tensor_copy(parts[0], src))
            ch.link(dve.tensor_tensor(tmp, src, parts[0], ALU.subtract))
            ch.link(dve.tensor_copy(parts[1], tmp))
            return dve.tensor_tensor(parts[2], tmp, parts[1], ALU.subtract)

        def queries_pe(pe, n, wq):
            for x in range(HALVES):
                last = pe.matmul(ps[:, x, :], wq[:, :], xT[:, x * BANK:(x + 1) * BANK], start=True, stop=True)
            last.then_inc(sem(n + "_q_projected"), 1)

        def bounds_pe(pe, n):
            pe.wait_ge(sem(n + "_bound_terms"), 2)
            for x in range(HALVES):
                for i in (0, 3):
                    last = pe.matmul(ps[0:H, x, :], hblk[:, :], ring[:, i, x * BANK:(x + 1) * BANK], start=i == 0, stop=i == 3)
            last.then_inc(sem(n + "_bounds"), 1)
            pe.wait_ge(sem(n + "_width_terms"), 1)
            for x in range(HALVES):
                last = pe.matmul(ps[0:H, 6 + x, :], hblk[:, :], ring[:, 1, x * BANK:(x + 1) * BANK], start=True, stop=True)
            last.then_inc(sem(n + "_bounds"), 1)

        def widths_act(act, n):
            act.wait_ge(sem(n + "_q_split"), 1)
            act.wait_ge(sem(n + "_bound_terms"), 3)
            act.activation(ring[:, 1, :], qT[n][:, :], ACT.Abs, scale=extent[:, :]).then_inc(sem(n + "_width_terms"), 1)

        def queries_dve(dve, ch, n, bq):
            dve.wait_ge(sem(n + "_q_projected"), 1)
            ch.link(dve.tensor_scalar(qT[n][:, :], flat[:, 0:T], bq[:, :], SCALE, ALU.add, ALU.mult))
            split(dve, ch, qT[n][:, :], [qp[:, i, :] for i in range(3)], ring[:, 1, :]).then_inc(sem(n + "_q_split"), 1)

        def bounds_dve(dve, n):
            q, kmax, kmin = qT[n][:, :], ext[n][:, 0:1], ext[n][:, 1:2]
            dve.tensor_scalar(ring[:, 0, :], q, 0.0, kmax, ALU.max, ALU.mult).then_inc(sem(n + "_bound_terms"), 1)
            dve.tensor_scalar(ring[:, 3, :], q, 0.0, kmin, ALU.min, ALU.mult).then_inc(sem(n + "_bound_terms"), 1)
            dve.tensor_tensor(extent[:, :], kmax, kmin, ALU.subtract).then_inc(sem(n + "_bound_terms"), 1)
            dve.wait_ge(sem(n + "_bounds"), 1)
            dve.tensor_scalar(shift[:, :], flat[0:H, 0:T], -1.0, None, ALU.mult).then_inc(sem(n + "_shift"), 1)

        def ranges_dve(dve, ch, n):
            dve.wait_ge(sem(n + "_shift"), 1)
            for i, (limit, op) in enumerate(((LARGEST, ALU.is_le), (-LARGEST, ALU.is_ge))):
                ch.link(dve.tensor_scalar(inr[:, :], shift[:, :], limit, None, op))
                ch.link(dve.tensor_reduce(good[0:H, GOOD[n] + 1 + i:GOOD[n] + 2 + i], inr[:, :], AX.X, ALU.add))
            dve.wait_ge(sem(n + "_bounds"), 2)
            dve.tensor_scalar(inr[:, :], flat[0:H, 6 * BANK:8 * BANK], SPREAD, None, ALU.is_le).then_inc(sem(n + "_ranged"), 1)
            dve.wait_ge(sem(n + "_ranged"), 1)
            ch.link(dve.tensor_reduce(good[0:H, GOOD[n]:GOOD[n] + 1], inr[:, :], AX.X, ALU.add))

        def queries_sp(sp, n):
            sp.wait_ge(sem(n + "_q_split"), 1)
            for part in range(3):
                src = bass.AP(qscr[n], part * HD * T, [[3 * HD * T, H], [T, HD], [1, T]])
                sp.dma_start(src, qp[:, part, :]).then_inc(sem(n + "_q_stored"), 16)
            sp.wait_ge(sem(n + "_q_stored"), 48)
            if n == "self":
                sp.wait_ge(sem("q_cleared"), 4)
            for wave, (lo, hi) in enumerate(WAVES):
                for a in range(2):
                    row, t = STACK * a, 0
                    while t < NTERM:
                        m = 1
                        while t + m < NTERM and QPART[t + m] == QPART[t + m - 1] + 1:
                            m += 1
                        src = qscr[n][2 * lo + a:2 * hi:2, 0:m].rearrange("h r d n -> h (r d) n").rearrange("h r n -> r h n")
                        sp.dma_start(qs[row:row + m * HD, 2 * lo + a:2 * hi:2, :], src)\
                            .then_inc(sem(f"{n}_q_loaded{wave}"), 16)
                        row, t = row + m * HD, t + m
                if wave == 0:
                    sp.wait_ge(sem(n + "_shift"), 1)
                    sp.dma_start(sscr[n][:, :], shift[:, :]).then_inc(sem(n + "_shift_stored"), 16)
                    sp.wait_ge(sem(n + "_shift_stored"), 16)
                for a in range(2):
                    row = STACK * a + SHIFT_ROW
                    sp.dma_start(qs[row:row + 1, 2 * lo + a:2 * hi:2, :],
                                 bass.AP(sscr[n], (2 * lo + a) * T, [[0, 1], [2 * T, hi - lo], [1, T]]))\
                        .then_inc(sem(f"{n}_q_loaded{wave}"), 16)

        WAVES = ((0, 1), (1, PAIRS))
        QLOADS = 2 * 3 + 2
        BOUNDS_AT = 6
        LOADED = 4
        GOOD = {"self": 0, "cross": 3, "mask_sign": 6, "mask_rows": 7}
        HOLD = 6 * H * T + T * LC + LP

        def normalise_heads(dve, ch, n):
            dve.wait_ge(sem(n + "_gathered"), 64)
            ch.link(dve.tensor_tensor(ring[:, 2, :], ring[:, 2, :], ring[:, 3, :], ALU.add))
            ch.link(dve.reciprocal(ring[:, 2, :], ring[:, 2, :]))
            ch.link(dve.tensor_tensor(ring[:, 0, :], ring[:, 0, :], ring[:, 1, :], ALU.add))
            dve.tensor_tensor(ring[:, 0, :], ring[:, 0, :], ring[:, 2, :], ALU.mult).then_inc(sem(n + "_heads"), 1)

        def project_out(pe, n, wo, heads):
            pe.wait_ge(sem(n + "_heads"), 1)
            for t in range(QT):
                last = pe.matmul(ps[:, t // 4, t % 4 * P:(t % 4 + 1) * P], heads[:, t * P:(t + 1) * P], wo[:, :],
                                 start=True, stop=True)
            last.then_inc(sem(n + "_y"), 1)

        def norm_dve(dve, ch, n, dst):
            dve.wait_ge(sem(n + "_y"), 1)
            ch.link(dve.tensor_tensor(yn[:, :, :].rearrange("p t c -> p (t c)"), flat[:, 0:T],
                                      xn[:, :, :].rearrange("p t c -> p (t c)"), ALU.add))
            for t in range(QT):
                last = dve.bn_stats(st[:, t, :], yn[:, t, :])
            ch.link(last)
            for t in range(QT):
                last = dve.bn_aggr(mv[:, t, :], st[:, t, :])
            ch.link(last)
            dve.tensor_scalar(rstd[:, :], mv[:, :, 1], EPS, None, ALU.add).then_inc(sem(n + "_var"), 1)
            dve.wait_ge(sem(n + "_std"), 1)
            ch.link(dve.reciprocal(rstd[:, :], rstd[:, :]))
            for t in range(QT):
                dve.tensor_scalar(dst[:, t, :], yn[:, t, :], mv[:, t, 0:1], rstd[:, t:t + 1], ALU.subtract, ALU.mult)\
                    .then_inc(sem(n + "_normed"), 1)

        def norm_act(act, n):
            act.wait_ge(sem(n + "_var"), 1)
            act.activation(rstd[:, :], rstd[:, :], ACT.Sqrt).then_inc(sem(n + "_std"), 1)

        def turn_pe(pe, n, src):
            for t in range(QT):
                pe.wait_ge(sem(n + "_normed"), t + 1)
                last = pe.transpose(ps[:, 2 + t // 4, t % 4 * P:(t % 4 + 1) * P], src[:, t, :], ident[:, :])
            last.then_inc(sem(n + "_turned"), 1)

        def turn_dve(dve, n):
            dve.wait_ge(sem(n + "_turned"), 1)
            dve.tensor_copy(xT[:, :], flat[:, 2 * BANK:2 * BANK + T]).then_inc(sem(n + "_xT"), 1)

        srow = qs[:, :, :].rearrange("p h n -> p (h n)").bitcast(F32)
        mrow = [ring[:, :, :].rearrange("p s n -> p (s n)"), oev[0][:, :, :].rearrange("p x n -> p (x n)")]
        MR = RING * T
        heads_g = oev[1][:, :, :].rearrange("p x n -> p (x n)")
        probT = xT[:, :].rearrange("p (b n) -> p b n", b=2)
        qhead, orow = w["q1"], w["k1"]
        keys_of = {"gself": T, "gcross": LC}

        def key_chunks(n):
            return [(c, min(BANK, keys_of[n] - c)) for c in range(0, keys_of[n], BANK)]

        def key_groups(pl):
            return [list(range(k, min(k + 4, pl.tiles))) for k in range(0, pl.tiles, 4)]

        def general_pe(pe, n, pl, kT, q):
            chunks, groups = key_chunks(n), key_groups(pl)
            with pe.Fori(0, QT) as qt:
                with pe.Fori(0, H) as h:
                    it = qt * H + h
                    pe.wait_ge(sem(n + "_qhead"), it + 1)
                    for c, (k0, m) in enumerate(chunks):
                        if c >= 4:
                            pe.wait_ge(sem(n + "_masked"), it * len(chunks) + c - 3)
                        pe.matmul(ps[:, c % 4, 0:m], qhead[:, :], kT[:, k0:k0 + m], start=True, stop=True)\
                            .then_inc(sem(n + "_scored"), 1)
                    pe.wait_ge(sem(n + "_exped"), it + 1)

                    def turn(i):
                        if i >= 2:
                            pe.wait_ge(sem(n + "_probT"), it * len(groups) + i - 1)
                        for j, kt in enumerate(groups[i]):
                            last = pe.transpose(ps[:, 4 + i % 2, j * P:(j + 1) * P], srow[:, kt * P:(kt + 1) * P], ident[:, :])
                        last.then_inc(sem(n + "_turned_p"), 1)

                    turn(0)
                    for i, kts in enumerate(groups):
                        if i + 1 < len(groups):
                            turn(i + 1)
                        pe.wait_ge(sem(n + "_probT"), it * len(groups) + i + 1)
                        for j, kt in enumerate(kts):
                            last = pe.matmul(ps[:, 6, 0:HD], probT[:, i % 2, j * P:(j + 1) * P],
                                             vx[pl.name][:, bass.ds(h, 1), kt, 0:HD].rearrange("p h d -> p (h d)"),
                                             start=kt == 0, stop=kt == pl.tiles - 1)
                        last.then_inc(sem(n + "_summed"), 1)
                pe.wait_ge(sem(n + "_headed"), (qt + 1) * H)
                pe.transpose(ps[:, 7, 0:P], orow[:, :], ident[:, :]).then_inc(sem(n + "_turned_o"), 1)

        def general_act(act, n, pl):
            groups = key_groups(pl)
            with act.Fori(0, QT) as qt:
                with act.Fori(0, H) as h:
                    it = qt * H + h
                    act.wait_ge(sem(n + "_maxed"), it + 1)
                    act.activation(srow[:, 0:keys_of[n]], srow[:, 0:keys_of[n]], ACT.Exp, bias=stat[:, 1:2],
                                   accum_out=stat[:, 2:3]).then_inc(sem(n + "_exped"), 1)
                    for i, kts in enumerate(groups):
                        act.wait_ge(sem(n + "_turned_p"), it * len(groups) + i + 1)
                        if i >= 2:
                            act.wait_ge(sem(n + "_summed"), it * len(groups) + i - 1)
                        act.activation(probT[:, i % 2, 0:len(kts) * P], ps[:, 4 + i % 2, 0:len(kts) * P], ACT.Copy)\
                            .then_inc(sem(n + "_probT"), 1)

        def general_dve(dve, n, pl, q, factor):
            chunks, groups = key_chunks(n), key_groups(pl)
            with dve.Fori(0, QT) as qt:
                with dve.Fori(0, H) as h:
                    it = qt * H + h
                    dve.tensor_scalar(qhead[:, :], q[:, bass.ds(qt * P, P)], hblk[:, bass.ds(h, 1)], None, ALU.mult)\
                        .then_inc(sem(n + "_qhead"), 1)
                    dve.wait_ge(sem(n + "_mask_in"), (qt + 1) * 32)
                    for c, (k0, m) in enumerate(chunks):
                        mask = mrow[0][:, k0:k0 + m] if k0 < MR else mrow[1][:, k0 - MR:k0 - MR + m]
                        dve.wait_ge(sem(n + "_scored"), it * len(chunks) + c + 1)
                        dve.scalar_tensor_tensor(out=srow[:, k0:k0 + m], in0=mask, scalar=factor, in1=ps[:, c % 4, 0:m],
                                                 op0=ALU.mult, op1=ALU.add).then_inc(sem(n + "_masked"), 1)
                    dve.wait_ge(sem(n + "_masked"), (it + 1) * len(chunks))
                    dve.tensor_reduce(stat[:, 0:1], srow[:, 0:keys_of[n]], AX.X, ALU.max).then_inc(sem(n + "_stat"), 1)
                    dve.wait_ge(sem(n + "_stat"), 2 * it + 1)
                    dve.tensor_scalar(stat[:, 1:2], stat[:, 0:1], -1.0, None, ALU.mult).then_inc(sem(n + "_maxed"), 1)
                    dve.wait_ge(sem(n + "_exped"), it + 1)
                    dve.reciprocal(stat[:, 3:4], stat[:, 2:3]).then_inc(sem(n + "_stat"), 1)
                    dve.wait_ge(sem(n + "_stat"), 2 * it + 2)
                    dve.wait_ge(sem(n + "_summed"), (it + 1) * len(groups))
                    dve.tensor_scalar(orow[:, bass.ds(h * HD, HD)], ps[:, 6, 0:HD], stat[:, 3:4], None, ALU.mult)\
                        .then_inc(sem(n + "_headed"), 1)
                dve.wait_ge(sem(n + "_turned_o"), qt + 1)
                dve.tensor_copy(heads_g[:, bass.ds(qt * P, P)], ps[:, 7, 0:P]).then_inc(sem(n + "_heads_copied"), 1)
            dve.wait_ge(sem(n + "_heads_copied"), QT)

        def general_sp(sp, n, mask):
            wide = keys_of[n]
            cut = MR if wide > MR else wide // 2

            def load(qt):
                rows = mask[bass.ds(qt * P, P), :]
                second = mrow[1][:, 0:wide - cut] if wide > MR else mrow[0][:, cut:wide]
                sp.dma_start(mrow[0][:, 0:cut], rows[:, 0:cut]).then_inc(sem(n + "_mask_in"), 16)
                sp.dma_start(second, rows[:, cut:wide]).then_inc(sem(n + "_mask_in"), 16)

            load(0)
            with sp.Fori(1, QT) as qt:
                sp.wait_ge(sem(n + "_masked"), qt * H * len(key_chunks(n)))
                load(qt)

        def fast_failed(eng):
            eng.wait_ge(sem("flagged"), 1)
            return eng.value_load(flag[0:1, 0:1], min_val=0, max_val=1) != 0

        w1 = region_m[:, 0:HID]
        w2 = region_m[:, HID:2 * HID]
        w3 = region_m[:, 2 * HID:2 * HID + len(FCH) * D].rearrange("p (j c) -> p j c", c=D)
        wbc = [qs[:, :, :].rearrange("p h n -> p (h n)").bitcast(F32)[:, i * T:(i + 1) * T] for i in range(8)] + \
            [region_k[:, i * T:(i + 1) * T] for i in range(3)]
        SPREADS = 4
        segments = lambda j: (FCH[j][0] + FCH[j][1] - 1) // HE - FCH[j][0] // HE + 1
        UNITS = [(j, x) for j in FORDER for x in range(HALVES)]

        def queries_sp_self(sp):
            sp.wait_ge(sem("self_k_split"), 1)
            for part in range(3):
                sp.dma_start(bass.AP(kscr["self"], part * HD * T, [[3 * HD * T, H], [T, HD], [1, T]]), kp_self[:, part, :])\
                    .then_inc(sem("self_k_stored"), 16)
            sp.wait_ge(sem("self_k_stored"), 48)
            sp.wait_ge(sem("k_cleared"), 2)
            for a in range(2):
                for b in range(2):
                    row = STACK * a + SHIFT_ROW
                    sp.dma_start(kst["self"][row:row + 1, b * T:(b + 1) * T], A["c_ones"][:, 0:T]).then_inc(sem("kfix_self"), 16)
            load_keys(sp, SELF, 0)
            queries_sp(sp, "self")

        def hbuf(i):
            return ring[:, i % 4, 0:BANK]

        @block.sync
        def _(sp):
            ld = lambda dst, src, s: sp.dma_start(dst, src).then_inc(sem(s), 16)
            ld(xT[:, :], A["xT"], "ld_q1")
            for n in ("q1", "v1"):
                ld(w[n][:, :], A["w_" + n], "ld_" + n)
            for n in ("q1", "k1"):
                ld(bcol[n][:, :], A["b_" + n], "ld_bcol")
            ld(brow["v1"][:, :], bass.AP(A["b_v1"].tensor, 0, [[0, P], [1, D]]), "ld_v1")
            for i, n in enumerate(("hblk", "trib", "identb", "ident")):
                ld({"hblk": hblk, "trib": trib, "identb": identb, "ident": ident}[n][:, :], A["c_" + n], "ld_const")
            for n in ("k2", "v2"):
                ld(w[n][:, :], A["w_" + n], "ld_kv2")
            ld(bcol["k2"][:, :], A["b_k2"], "ld_kv2")
            ld(brow["v2"][:, :], bass.AP(A["b_v2"].tensor, 0, [[0, P], [1, D]]), "ld_kv2")
            queries_sp_self(sp)
            store_heads(sp, SELF)
            sp.wait_ge(sem("mask_split"), 1)
            for i in range(3):
                sp.dma_start(mscr[i, :].rearrange("(p j) -> p j", p=P), mkp[:, i, :]).then_inc(sem("mask_stored"), 16)
            sp.wait_ge(sem("k_stored"), 8 * 48)
            sp.wait_ge(sem("cross_cleared"), 1)
            sp.wait_ge(sem("mask_stored"), 48)
            for b in range(2):
                for a in range(2):
                    row = STACK * a + SHIFT_ROW
                    sp.dma_start(kst["cross"][row:row + 1, b * LP:(b + 1) * LP], A["c_ones"]).then_inc(sem("kfix_cross"), 16)
                    sp.dma_start(kst["cross"][row + 1:row + 4, b * LP:(b + 1) * LP], mscr[:, :]).then_inc(sem("kfix_cross"), 16)
            load_keys(sp, CROSS, 0)
            queries_sp(sp, "cross")
            store_heads(sp, CROSS)
            with sp.If(fast_failed(sp)):
                sp.wait_ge(sem("cross_heads"), 1)
                sp.dma_start(region_k[:, :], kTscr[:, :]).then_inc(sem("general_in"), 16)
                sp.dma_start(xn[:, :, :], A["x"][0].rearrange("(t p) c -> p t c", p=P)).then_inc(sem("general_in"), 16)
                general_sp(sp, "gself", A["c_causal"])
                sp.wait_ge(sem("gself_masked"), QT * H * len(key_chunks("gself")))
                general_sp(sp, "gcross", A["mask"])
            with sp.Else():
                sp.nop()
            sp.wait_ge(sem("wT_ready"), 1)
            sp.dma_start(wscr[:, :], wT[:, :]).then_inc(sem("w_stored"), 16)
            sp.wait_ge(sem("w_stored"), 16)
            for j, (c, m) in enumerate(FCH[:NEXP]):
                r = 0
                while r < m:
                    e = (c + r) // HE
                    k = min(m - r, (e + 1) * HE - c - r)
                    sp.dma_start(wbc[j][r:r + k, :], bass.AP(wscr, e * T, [[0, k], [1, T]])).then_inc(sem(f"w_spread{j // SPREADS}"), 16)
                    r += k
            sp.wait_ge(sem("ffn_normed"), QT)
            sp.dma_start(out[0].rearrange("(t p) c -> p t c", p=P), yn[:, :, :]).then_inc(sem("stored"), 16)
            sp.wait_ge(sem("stored"), 16)

        @block.gpsimd
        def _(pool):
            ld = lambda dst, src, s: pool.dma_start(dst, src).then_inc(sem(s), 16)
            for a in range(2):
                r = STACK * a + 32
                pool.memset(kst["self"][r:r + 32, :].bitcast(F32), 0.0).then_inc(sem("k_cleared"), 1)
            pool.wait_ge(sem("k_cleared"), 2)
            for a in range(2):
                r = STACK * a + 32
                pool.memset(qs32[r:r + 32, a:H:2, :], ONES_PAIR).then_inc(sem("q_cleared"), 1)
            pool.wait_ge(sem("q_cleared"), 4)
            for i, n in enumerate(("self", "cross")):
                pool.memset(vx[n][:, :, :, HD:VW], 1.0).then_inc(sem("v_ones"), 1)
                pool.wait_ge(sem("v_ones"), i + 1)
            pool.wait_ge(sem("self_v_ready"), 1)
            pool.wait_ge(sem("ctx_v_projected"), len(CH))
            pool.wait_ge(sem("v_ones"), 2)

            pool.wait_ge(sem("k_evicted"), len(CH))
            pool.dma_start(kTscr[:, :], kT_cross[:, :]).then_inc(sem("kT_saved"), 16)

            def store_key_piece(p, first):
                pool.wait_ge(sem("k_split"), g(p, 1, 1))
                for part in range(3):
                    pool.dma_start(bass.AP(kscr["cross"], p * PIECE + part * HD * LP, [[3 * HD * LP, H], [LP, HD], [1, PIECE]]),
                                   kp[:, part, :]).then_inc(sem("k_stored"), 16)
                if first:
                    pool.memset(region_k[:, :], 0.0).then_inc(sem("cross_cleared"), 1)

            head_values(pool, SELF, store_key_piece)
            pool.wait_ge(sem("k_stored"), PAIRS * 48)
            pool.wait_ge(sem("extrema"), 2 * PAIRS)
            pool.wait_ge(sem("cross_v_ready"), len(CH))
            pool.wait_ge(sem("self_valued"), g(PAIRS, len(SELF.groups), 0))

            def load_mask_rows(p, first):
                for j, (c, m) in enumerate(MPIECES):
                    if j >= 2 or not first:
                        pool.wait_ge(sem("checked"), g(p, MCOLS, j - 1))
                    pool.dma_start(mchk[j % 2][:, 0:m], A["mask"][bass.ds(p * P, P), c:c + m])\
                        .then_inc(sem(f"ld_mask{j % 2}"), 16)

            def mask_rows(p, first):
                if first:
                    pool.wait_ge(sem("self_normed"), QT)
                    pool.wait_ge(sem("kT_saved"), 16)
                    pool.wait_ge(sem("cross_q_loaded1"), 16 * QLOADS)
                    ld(row0, bass.AP(A["mask"].tensor, 0, [[0, P], [1, LC]]), "ld_row0")
                load_mask_rows(p, first)

            head_values(pool, CROSS, mask_rows)
            pool.wait_ge(sem("checked"), MCOLS * PAIRS)
            for dst, src in ((w1, "w1"), (w2, "w2"), (w3, "w3")):
                ld(dst, A[src], "ld_ffn")

        @block.tensor
        def _(pe):
            pe.wait_ge(sem("ld_q1"), 32)
            queries_pe(pe, "self", w["q1"])
            pe.wait_ge(sem("ld_k1"), 16)
            for x in range(HALVES):
                last = pe.matmul(ps[:, 2 + x, :], w["k1"][:, :], xT[:, x * BANK:(x + 1) * BANK], start=True, stop=True)
            last.then_inc(sem("self_k_projected"), 1)
            pe.wait_ge(sem("ld_v1"), 32)
            for t in range(QT):
                last = pe.matmul(ps[:, 4 + t // 4, t % 4 * P:(t % 4 + 1) * P], xT[:, t * P:(t + 1) * P], w["v1"][:, :],
                                 start=True, stop=True)
            last.then_inc(sem("self_v_projected"), 1)
            pe.wait_ge(sem("ld_kv2"), 64)
            pe.wait_ge(sem("self_v_ready"), 1)
            for i, (c, m) in enumerate(CH):
                if i == BOUNDS_AT:
                    pe.wait_ge(sem("ld_const"), 64)
                    pe.wait_ge(sem("sums_cleared"), 1)
                    bounds_pe(pe, "self")
                pe.wait_ge(sem(f"ld_ctx{i // LOADED}"), 16)
                if i >= 2:
                    pe.wait_ge(sem("k_evicted"), i - 1)
                pe.matmul(ps[:, 4 + i % 2, 0:m], w["k2"][:, :], ctxT[:, c:c + m], start=True, stop=True)\
                    .then_inc(sem("ctx_k_projected"), 1)
            for i, (c, m) in enumerate(CH):
                if i == 0:
                    pe.wait_ge(sem("k_evicted"), len(CH))
                elif i >= 2:
                    pe.wait_ge(sem("cross_v_ready"), i - 1)
                for t in range(m // P):
                    last = pe.matmul(ps[:, 4 + i % 2, t * P:(t + 1) * P], ctxT[:, c + t * P:c + (t + 1) * P], w["v2"][:, :],
                                     start=True, stop=True)
                last.then_inc(sem("ctx_v_projected"), 1)
            pe.wait_ge(sem("cross_v_ready"), len(CH))
            pe.wait_ge(sem("self_q_loaded0"), 16 * QLOADS)
            pe.wait_ge(sem("kfix_self"), 64)
            pe.wait_ge(sem("self_shift"), 1)
            scores_and_values(pe, SELF)
            pe.wait_ge(sem("ld_late"), 16 * 9)
            project_out(pe, "self", w["o1"], ring[:, 0, :])
            turn_pe(pe, "self", xn)
            pe.wait_ge(sem("self_xT"), 1)
            queries_pe(pe, "cross", w["q2"])
            bounds_pe(pe, "cross")
            pe.wait_ge(sem("cross_q_loaded0"), 16 * QLOADS)
            pe.wait_ge(sem("kfix_cross"), 128)
            scores_and_values(pe, CROSS)
            pe.wait_ge(sem("goods_summed"), 2)
            pe.matmul(ps[0:1, 0, 0:2], ones[:, :], goods[:, :], start=True, stop=True).then_inc(sem("goods_counted"), 1)
            with pe.If(fast_failed(pe)):
                general_pe(pe, "gself", SELF, kT_self[:, :], qT["self"])
                project_out(pe, "gself", w["o1"], heads_g)
                turn_pe(pe, "gself", xn)
                pe.wait_ge(sem("gself_xT"), 1)
                queries_pe(pe, "gcross", w["q2"])
                general_pe(pe, "gcross", CROSS, region_k[:, :], qT["cross"])
                pe.wait_ge(sem("general_done"), 1)
            with pe.Else():
                pe.nop()
            project_out(pe, "cross", w["o2"], ring[:, 0, :])
            turn_pe(pe, "cross", xn)
            pe.wait_ge(sem("cross_xT"), 1)
            for t in range(QT):
                last = pe.matmul(ps[:, 4, t * E:(t + 1) * E], xT[:, t * P:(t + 1) * P], wg[:, :], start=True, stop=True)
            last.then_inc(sem("routed"), 1)
            pe.wait_ge(sem("ld_ffn"), 48)

            def hidden(i):
                j, x = UNITS[i]
                c, m = FCH[j]
                if i >= 3:
                    pe.wait_ge(sem("gated"), i - 2)
                if i == 2:
                    pe.wait_ge(sem("wT_ready"), 1)
                for k, wk in enumerate((w1, w2)):
                    last = pe.matmul(ps[0:m, 2 * (i % 3) + k, :], wk[:, c:c + m], xT[:, x * BANK:(x + 1) * BANK],
                                     start=True, stop=True)
                last.then_inc(sem("hidden"), 1)

            def down(i):
                j, x = UNITS[i]
                c, m = FCH[j]
                if j >= NEXP:
                    pe.wait_ge(sem("gated"), i + 1)
                else:
                    pe.wait_ge(sem("activated"), i + 1 - 2 * (len(FCH) - NEXP))
                pe.matmul(ps[:, 6 + x, :], w3[0:m, j, :], hbuf(i)[0:m, :], start=j == FORDER[0],
                          stop=j == FORDER[-1]).then_inc(sem("down"), 1)

            hidden(0)
            hidden(1)
            pe.wait_ge(sem("sel_ready"), 1)
            for t in range(QT):
                last = pe.transpose(ps[0:E, 4 + t // 4, t % 4 * P:(t % 4 + 1) * P], sel[:, t, :], ident[:, :])
            last.then_inc(sem("wT_turned"), 1)
            for i in range(2, len(UNITS) + 2):
                if i < len(UNITS):
                    hidden(i)
                down(i - 2)
            pe.wait_ge(sem("yT_copied"), 1)
            for t in range(QT):
                last = pe.transpose(ps[:, t // 4, t % 4 * P:(t % 4 + 1) * P], ring[:, 5, t * P:(t + 1) * P], ident[:, :])
            last.then_inc(sem("ffn_y"), 1)

        @block.scalar
        def _(act):
            ld = lambda dst, src, s: act.dma_start(dst, src).then_inc(sem(s), 16)
            ld(w["k1"][:, :], A["w_k1"], "ld_k1")
            for i in range(0, len(CH), LOADED):
                c, m = CH[i][0], sum(m for _, m in CH[i:i + LOADED])
                ld(ctxT[:, c:c + m], A["ctxT"][:, c:c + m], f"ld_ctx{i // LOADED}")
            ld(mk[:, :], A["mask"][0, :].rearrange("(p j) -> p j", p=P), "ld_mk")
            ld(xn[:, :, :], A["x"][0].rearrange("(t p) c -> p t c", p=P), "ld_late")
            for n in ("o1", "q2", "o2"):
                ld(w[n][:, :], A["w_" + n], "ld_late")
            ld(bcol["q2"][:, :], A["b_q2"], "ld_late")
            for n in ("o1", "o2"):
                ld(brow[n][:, :], bass.AP(A["b_" + n].tensor, 0, [[0, P], [1, D]]), "ld_late")
            ld(wg[:, :], A["wg"], "ld_late")
            ld(tri8[:, :, :], bass.AP(A["c_tri8"].tensor, 0, [[0, P], [E, E], [1, E]]), "ld_late")
            act.wait_ge(sem("ld_bcol"), 32)
            act.wait_ge(sem("self_k_projected"), 1)
            act.activation(kT_self[:, :], flat[:, 2 * BANK:2 * BANK + T], ACT.Identity, bias=bcol["k1"][:, :])\
                .then_inc(sem("self_k_out"), 1)
            act.wait_ge(sem("self_k_out"), 1)
            act.activation(kp_self[:, 0, :], kT_self[:, :], ACT.Copy).then_inc(sem("self_k_out"), 1)
            act.wait_ge(sem("ld_kv2"), 64)
            for i, (c, m) in enumerate(CH):
                if i == BOUNDS_AT - 1:
                    widths_act(act, "self")
                act.wait_ge(sem("ctx_k_projected"), i + 1)
                act.activation(kT_cross[:, c:c + m], ps[:, 4 + i % 2, 0:m], ACT.Identity, bias=bcol["k2"][:, :])\
                    .then_inc(sem("k_evicted"), 1)
            exponentials(act, SELF)
            norm_act(act, "self")
            widths_act(act, "cross")
            exponentials(act, CROSS)
            with act.If(fast_failed(act)):
                general_act(act, "gself", SELF)
                norm_act(act, "gself")
                general_act(act, "gcross", CROSS)
            with act.Else():
                act.nop()
            norm_act(act, "cross")
            act.wait_ge(sem("logits_shifted"), 1)
            act.activation(lg[:, :, :], lg[:, :, :], ACT.Exp).then_inc(sem("logits_exped"), 1)
            for i, (j, x) in enumerate(UNITS):
                m = FCH[j][1]
                act.wait_ge(sem("hidden"), i + 1)
                if i >= 4:
                    act.wait_ge(sem("down"), i - 3)
                act.activation(hbuf(i)[0:m, :], ps[0:m, 2 * (i % 3), :], ACT.Silu).then_inc(sem("silued"), 1)
            norm_act(act, "ffn")

        @block.vector
        def _(dve):
            ch = Chain(dve, "dve_chain")
            for a in range(2):
                r = STACK * (1 - a)
                dve.memset(qs32[r:r + STACK, a:H:2, :], 0.0).then_inc(sem("q_cleared"), 1)
            ch.link(dve.memset(good[:, :], 0.0))
            dve.wait_ge(sem("ld_bcol"), 32)
            queries_dve(dve, ch, "self", bcol["q1"])
            dve.wait_ge(sem("self_k_out"), 2)
            tmp, parts = ring[:, 2, :], [kp_self[:, i, :] for i in range(3)]
            ch.link(dve.tensor_tensor(tmp, kT_self[:, :], parts[0], ALU.subtract))
            ch.link(dve.tensor_copy(parts[1], tmp))
            dve.tensor_tensor(parts[2], tmp, parts[1], ALU.subtract).then_inc(sem("self_k_split"), 1)
            by_head = lambda v: v.rearrange("p (t h d) -> p t h d", h=H, d=HD)
            rows = lambda b, n: bass.AP(b, 0, [[D, P], [0, n], [HD, H], [1, HD]])
            dve.wait_ge(sem("self_v_projected"), 1)
            dve.wait_ge(sem("ld_v1"), 32)
            for x in range(HALVES):
                n = QT // HALVES
                last = dve.tensor_tensor(vx["self"][:, :, x * n:(x + 1) * n, 0:HD].rearrange("p h t d -> p t h d"),
                                         by_head(ps[:, 4 + x, :]), rows(brow["v1"], n), ALU.add)
            last.then_inc(sem("self_v_ready"), 1)
            ch.link(dve.tensor_reduce(ext["self"][:, 0:1], kT_self[:, :], AX.X, ALU.max))
            ch.link(dve.tensor_reduce(ext["self"][:, 1:2], kT_self[:, :], AX.X, ALU.min))
            dve.memset(ps[:, 6:8, :], 0.0).then_inc(sem("sums_cleared"), 1)
            bounds_dve(dve, "self")
            dve.wait_ge(sem("ld_kv2"), 64)
            for i, (c, m) in enumerate(CH):
                n = m // P
                dve.wait_ge(sem("ctx_v_projected"), i + 1)
                dve.tensor_tensor(vx["cross"][:, :, 4 * i:4 * i + n, 0:HD].rearrange("p h t d -> p t h d"),
                                  by_head(ps[:, 4 + i % 2, 0:m]), rows(brow["v2"], n), ALU.add)\
                    .then_inc(sem("cross_v_ready"), 1)
            ranges_dve(dve, ch, "self")
            dve.wait_ge(sem("ld_mk"), 16)
            ch.link(dve.tensor_scalar(mku[:, :], mk[:, :], MASKED, None, ALU.mult))
            split(dve, ch, mku[:, :], [mkp[:, i, :] for i in range(3)], mku[:, :]).then_inc(sem("mask_split"), 1)
            W = LP // 8
            dve.wait_ge(sem("k_evicted"), len(CH))
            for p in range(PAIRS):
                c = p * W
                if p:
                    dve.wait_ge(sem("k_stored"), 48 * p)
                else:
                    dve.wait_ge(sem("self_k_stored"), 48)
                src, parts, tmp = kT_cross[:, c:c + W], [kp[:, i, :] for i in range(3)], kp_tmp
                ch.link(dve.tensor_copy(parts[0], src))
                ch.link(dve.tensor_tensor(tmp, src, parts[0], ALU.subtract))
                evict(dve, SELF, p, p == 0, 0)
                ch.link(dve.tensor_copy(parts[1], tmp))
                dve.tensor_tensor(parts[2], tmp, parts[1], ALU.subtract).then_inc(sem("k_split"), 1)
                n = min(W, LC - c)
                dve.tensor_reduce(extc[:, 0, p:p + 1], kT_cross[:, c:c + n], AX.X, ALU.max).then_inc(sem("extrema"), 1)
                dve.tensor_reduce(extc[:, 1, p:p + 1], kT_cross[:, c:c + n], AX.X, ALU.min).then_inc(sem("extrema"), 1)
                evict(dve, SELF, p, p == 0, 1)
            dve.wait_ge(sem("extrema"), 2 * PAIRS)
            ch.link(dve.tensor_reduce(ext["cross"][:, 0:1], extc[:, 0, :], AX.X, ALU.max))
            ch.link(dve.tensor_reduce(ext["cross"][:, 1:2], extc[:, 1, :], AX.X, ALU.min))
            dve.wait_ge(sem("ld_late"), 16 * 9)
            for t in range(QT):
                last = dve.tensor_tensor(xn[:, t, :], xn[:, t, :], brow["o1"][:, :], ALU.add)
            ch.link(last)
            dve.wait_ge(sem("self_valued"), g(PAIRS, len(SELF.groups), 0))
            dve.memset(ring[:, 1, 0:P], 0.0)
            ch.link(dve.memset(ring[:, 3, 0:P], 0.0))
            normalise_heads(dve, ch, "self")
            norm_dve(dve, ch, "self", xn)
            turn_dve(dve, "self")
            queries_dve(dve, ch, "cross", bcol["q2"])
            bounds_dve(dve, "cross")
            ranges_dve(dve, ch, "cross")
            for t in range(QT):
                last = dve.tensor_tensor(xn[:, t, :], xn[:, t, :], brow["o2"][:, :], ALU.add)
            ch.link(last)
            ch.link(dve.memset(ones[:, :], 1.0))
            ch.link(dve.tensor_scalar(mku[:, :], mk[:, :], 0.0, None, ALU.is_ge))
            ch.link(dve.tensor_reduce(good[:, GOOD["mask_sign"]:GOOD["mask_sign"] + 1], mku[:, :], AX.X, ALU.add))
            ch.link(dve.tensor_scalar(mku[:, :], mk[:, :], 0.0, None, ALU.is_equal))
            dve.tensor_reduce(goods[:, 1:2], mku[:, :], AX.X, ALU.add).then_inc(sem("goods_summed"), 1)
            dve.wait_ge(sem("ld_row0"), 16)

            def check_mask(p, j):
                c, m = MPIECES[j]
                piece = mchk[j % 2][:, 0:m]
                dve.wait_ge(sem(f"ld_mask{j % 2}"), g(p, 8 * MCOLS, 16 * (j // 2 + 1)))
                dve.tensor_tensor(piece, piece, row0[:, c:c + m], ALU.is_equal).then_inc(sem("compared"), 1)
                dve.wait_ge(sem("compared"), g(p, MCOLS, j + 1))
                dve.tensor_reduce(good[:, bass.ds(p * MCOLS + GOOD["mask_rows"] + j, 1)], piece, AX.X, ALU.add)\
                    .then_inc(sem("checked"), 1)

            def cross_pair(p, first):
                for a in range(2):
                    for j in range(a * MCOLS // 2, (a + 1) * MCOLS // 2):
                        check_mask(p, j)
                    evict(dve, CROSS, p, first, a)

            cross_pair(0, True)
            with dve.Fori(1, PAIRS) as p:
                cross_pair(p, False)
            dve.wait_ge(sem("checked"), MCOLS * PAIRS)
            dve.tensor_reduce(goods[:, 0:1], good[:, :], AX.X, ALU.add).then_inc(sem("goods_summed"), 1)
            dve.wait_ge(sem("goods_counted"), 1)
            ch.link(dve.tensor_scalar(held[:, 0:1], ps[0:1, 0, 0:1], float(HOLD), None, ALU.not_equal))
            ch.link(dve.tensor_scalar(held[:, 1:2], ps[0:1, 0, 1:2], 0.5, None, ALU.is_lt))
            dve.tensor_tensor(flag[:, :], held[:, 0:1], held[:, 1:2], ALU.max).then_inc(sem("flagged"), 1)
            normalise_heads(dve, ch, "cross")
            with dve.If(fast_failed(dve)):
                gch = Chain(dve, "dve_general_chain")
                dve.wait_ge(sem("general_in"), 32)
                dve.wait_ge(sem("cross_heads"), 1)
                general_dve(dve, "gself", SELF, qT["self"], -float(np.finfo(np.float32).max))
                for t in range(QT):
                    last = dve.tensor_tensor(xn[:, t, :], xn[:, t, :], brow["o1"][:, :], ALU.add)
                last.then_inc(sem("gself_heads"), 1)
                dve.wait_ge(sem("gself_heads"), 1)
                norm_dve(dve, gch, "gself", xn)
                turn_dve(dve, "gself")
                dve.wait_ge(sem("gcross_q_projected"), 1)
                gch.link(dve.tensor_scalar(qT["cross"][:, :], flat[:, 0:T], bcol["q2"][:, :], SCALE, ALU.add, ALU.mult))
                for t in range(QT):
                    last = dve.tensor_tensor(xn[:, t, :], xn[:, t, :], brow["o2"][:, :], ALU.add)
                gch.link(last)
                gch.link(dve.memset(srow[:, LC:LP], 0.0))
                general_dve(dve, "gcross", CROSS, qT["cross"], MASKED)
                dve.tensor_copy(ring[:, 0, :], heads_g).then_inc(sem("general_done"), 1)
                dve.wait_ge(sem("general_done"), 1)
            with dve.Else():
                dve.nop()
            norm_dve(dve, ch, "cross", xn)
            turn_dve(dve, "cross")
            dve.wait_ge(sem("routed"), 1)
            ch.link(dve.tensor_copy(lg[:, :, :].rearrange("p t e -> p (t e)"), ps[:, 4, 0:QT * E]))
            lj = bass.AP(lg, 0, [[QT * E, P], [E, QT], [0, E], [1, E]])
            le = bass.AP(lg, 0, [[QT * E, P], [E, QT], [1, E], [0, E]])
            low = bass.AP(tri8, 0, [[E * E, P], [0, QT], [E, E], [1, E]])
            ch.link(dve.tensor_tensor(rk[0], lj, le, ALU.is_ge))
            ch.link(dve.tensor_tensor(rk[0], rk[0], low, ALU.mult))
            ch.link(dve.tensor_tensor(rk[1], lj, le, ALU.is_gt))
            ch.link(dve.tensor_tensor(rk[0], rk[0], rk[1], ALU.max))
            ch.link(dve.tensor_reduce(sel[:, :, :], rk[0], AX.X, ALU.add))
            ch.link(dve.tensor_reduce(mx8[:, :], lg[:, :, :], AX.X, ALU.max))
            ch.link(dve.tensor_scalar(sel[:, :, :], sel[:, :, :], 2.0, None, ALU.is_lt))
            dve.tensor_tensor(lg[:, :, :], lg[:, :, :], bass.AP(mx8, 0, [[QT, P], [1, QT], [0, E]]), ALU.subtract)\
                .then_inc(sem("logits_shifted"), 1)
            dve.wait_ge(sem("logits_exped"), 1)
            ch.link(dve.tensor_tensor(sel[:, :, :], sel[:, :, :], lg[:, :, :], ALU.mult))
            ch.link(dve.tensor_reduce(mx8[:, :], sel[:, :, :], AX.X, ALU.add))
            ch.link(dve.reciprocal(mx8[:, :], mx8[:, :]))
            dve.tensor_tensor(sel[:, :, :], sel[:, :, :], bass.AP(mx8, 0, [[QT, P], [1, QT], [0, E]]), ALU.mult)\
                .then_inc(sem("sel_ready"), 1)
            dve.wait_ge(sem("wT_turned"), 1)
            dve.tensor_copy(wT[:, :], flat[0:E, 4 * BANK:4 * BANK + T]).then_inc(sem("wT_ready"), 1)
            for i, (j, x) in enumerate(UNITS):
                m = FCH[j][1]
                h = hbuf(i)[0:m, :]
                dve.wait_ge(sem("silued"), i + 1)
                if j >= NEXP:
                    dve.tensor_tensor(h, ps[0:m, 2 * (i % 3) + 1, :], h, ALU.mult).then_inc(sem("gated"), 1)
                else:
                    dve.tensor_tensor(h, ps[0:m, 2 * (i % 3) + 1, :], h, ALU.mult).then_inc(sem("gated"), 1)
                    dve.wait_ge(sem("gated"), i + 1)
                    if j % SPREADS == 0 and x == 0:
                        dve.wait_ge(sem(f"w_spread{j // SPREADS}"), 16 * sum(map(segments, range(j, min(j + SPREADS, NEXP)))))
                    dve.tensor_tensor(h, h, wbc[j][0:m, x * BANK:(x + 1) * BANK], ALU.mult).then_inc(sem("activated"), 1)
            dve.wait_ge(sem("down"), len(UNITS))
            dve.tensor_copy(ring[:, 5, :], flat[:, 6 * BANK:8 * BANK]).then_inc(sem("yT_copied"), 1)
            norm_dve(dve, ch, "ffn", yn)



def kernel(**inputs):
    import numpy as _np
    import ml_dtypes as _ml
    import concourse.bacc as _bacc
    from concourse import mybir as _mybir
    from concourse.bass_utils import run_bass_kernel_spmd as _run

    i = {k: _np.asarray(v) for k, v in inputs.items()}
    bf = _ml.bfloat16
    f = _np.float32
    ctx = _np.zeros((LP, D), f)
    ctx[:LC] = i["ctx_1024"][0]
    mask = _np.ones((T, LP), f)
    mask[:, :LC] = i["mask_Bx1xSxS2_fk0"][0, 0]
    cat = lambda a, s: _np.concatenate([_np.transpose(i[a], (1, 0, 2)).reshape(D, E * HE), i[s]], 1)
    w3 = _np.zeros((len(FCH) * P, D), f)
    w3[:HID] = _np.concatenate([i["L0_ffn_W3"].reshape(E * HE, D), i["L0_ffn_Ws3"]], 0)
    arrays = {
        "x": i["x"], "xT": i["x"][0].T, "ctxT": ctx.T, "mask": mask,
        "w_q1": i["L0_attn_wq"], "w_k1": i["L0_attn_wk"], "w_v1": i["L0_attn_wv"], "w_o1": i["L0_attn_wo"],
        "w_q2": i["L0_xattn_Wq"].T, "w_k2": i["L0_xattn_Wk"].T, "w_v2": i["L0_xattn_Wv"].T, "w_o2": i["L0_xattn_Wo"].T,
        "b_q1": i["L0_attn_bq"][:, None], "b_k1": i["L0_attn_bk"][:, None],
        "b_q2": i["L0_xattn_bq"][:, None], "b_k2": i["L0_xattn_bk"][:, None],
        "b_v1": i["L0_attn_bv"][None], "b_o1": i["L0_attn_bo"][None],
        "b_v2": i["L0_xattn_bv"][None], "b_o2": i["L0_xattn_bo"][None],
        "wg": i["L0_ffn_Wg"], "w1": cat("L0_ffn_W1", "L0_ffn_Ws1"), "w2": cat("L0_ffn_W2", "L0_ffn_Ws2"),
        "w3": w3.reshape(len(FCH), P, D).transpose(1, 0, 2),
        "c_ones": _np.ones((1, LP), bf), "c_ident": _np.eye(P, dtype=f), "c_identb": _np.eye(P).astype(bf),
        "c_trib": _np.where(_np.arange(P)[None, :] < _np.arange(P)[:, None], -1e30, 0.0).astype(bf),
        "c_hblk": (_np.arange(P)[:, None] // HD == _np.arange(H)[None, :]).astype(f),
        "c_causal": (_np.arange(T)[None, :] > _np.arange(T)[:, None]).astype(f),
        "c_tri8": (_np.arange(E)[None, :] < _np.arange(E)[:, None]).astype(f),
    }
    nc = _bacc.Bacc("TRN2", target_bir_lowering=False, num_devices=1)
    sent, args = {}, {}
    for name, a in arrays.items():
        a = _np.ascontiguousarray(a)
        sent[f"in_{name}"] = a
        args[name] = nc.dram_tensor(f"in_{name}", a.shape, _mybir.dt.from_np(a.dtype), kind="ExternalInput").ap()
    out = nc.dram_tensor("out_0", (1, T, D), _mybir.dt.float32, kind="ExternalOutput").ap()
    nc.disable_value_cache = True
    build(nc, args, out)
    r = _run(nc, [sent], core_ids=[0])
    return r.results[0]["out_0"]
```

```python
from contextlib import ExitStack

import numpy as np

import concourse.bass as bass
from concourse import mybir

F32 = mybir.dt.float32
BF16 = mybir.dt.bfloat16
I32 = mybir.dt.int32
ALU = mybir.AluOpType
ACT = mybir.ActivationFunctionType
AX = mybir.AxisListType

P = 128
BANK = 512
T = 1024
D = 128
H = 16
HD = D // H
PAIRS = H // 2
QT = T // P
HALVES = T // BANK
LC = 6404
NC_ = -(-LC // P)
LP = NC_ * P
CH = [(c, min(BANK, LP - c)) for c in range(0, LP, BANK)]
E, HE, HS = 8, 176, 352
HID = E * HE + HS
FCH = [(c, min(P, HID - c)) for c in range(0, HID, P)]
FORDER = [j for j, (c, _) in enumerate(FCH) if c >= E * HE] + [j for j, (c, _) in enumerate(FCH) if c < E * HE]
NEXP = sum(c < E * HE for c, _ in FCH)
SCALE = float(1.0 / np.sqrt(np.float32(HD)))
MASKED = -1.0e9
EPS = 1e-5
SPREAD = 60.0
LARGEST = 1024.0
VW = 2 * HD

QPART = (0, 1, 2, 0, 1, 0)
KPART = (0, 0, 0, 1, 1, 2)
NTERM = len(QPART)
STACK = 64
ONES_PAIR = float(np.array([0x3F803F80], np.uint32).view(np.float32)[0])
SHIFT_ROW = NTERM * HD
MASK_ROW = SHIFT_ROW + 1
RING = 6
SLOTS = 3


class Plan:

    def __init__(self, name, tiles, lag, causal):
        self.name, self.tiles, self.causal = name, tiles, causal
        self.lag = lag
        self.width = tiles * P
        packed = [k for k in range(tiles) if causal and k * P >= BANK]
        self.steps = []
        for a in range(2):
            for kt in range(tiles - len(packed)):
                pieces = [(kt, x, self.first_query(kt, x), self.first_query(kt, x)) for x in range(HALVES)]
                self.steps.append((a, [q for q in pieces if q[2] < (q[1] + 1) * BANK]))
            for kt in packed[::2]:
                q = [self.first_query(k, 1) for k in (kt, kt + 1)]
                self.steps.append((a, [(kt, 1, q[0], BANK), (kt + 1, 1, q[1], q[1] - BANK)]))
        self.n = len(self.steps)
        assert self.n % SLOTS == 0 and self.n % RING == 0
        self.groups = [(a, list(range(k, min(k + 2, tiles)))) for a in range(2) for k in range(0, tiles, 2)]
        self.per_head = len(self.groups) // 2

    def group_of(self, s):
        a, pieces = self.steps[s]
        return a * self.per_head + pieces[0][0] // 2

    def last_step(self, g):
        return max(s for s in range(self.n) if self.group_of(s) == g)

    def span(self, s):
        pieces = self.steps[s][1]
        return min(at for _, _, _, at in pieces), max(at + (x + 1) * BANK - q0 for _, x, q0, at in pieces)

    def first_query(self, kt, half):
        return max(half * BANK, kt * P if self.causal else 0)

    def pieces_of(self, g):
        a, kts = self.groups[g]
        return sorted(((s, q) for s, (b, pieces) in enumerate(self.steps) if b == a for q in pieces if q[0] in kts),
                      key=lambda i: i[1][:2])


SELF = Plan("self", T // P, 3, True)
CROSS = Plan("cross", NC_, 2, False)


def build(nc, A, out):
    ctx = ExitStack()
    with ctx:
        def sb(name, shape, dt=F32):
            return ctx.enter_context(nc.sbuf_tensor(name, shape, dt))

        def dram(name, shape, dt):
            return nc.dram_tensor(name, shape, dt)

        sems = {}

        def sem(name):
            if name not in sems:
                sems[name] = ctx.enter_context(nc.semaphore(name))
            return sems[name]

        class Chain:

            def __init__(self, eng, name):
                self.eng, self.sem, self.n = eng, sem(name), 0

            def link(self, ins):
                self.n += 1
                ins.then_inc(self.sem, 1)
                self.eng.wait_ge(self.sem, self.n)

        ps = ctx.enter_context(nc.psum_tensor("ps", [P, 8, BANK], F32))
        flat = ps[:, :, :].rearrange("p b n -> p (b n)")
        region_k = sb("region_k", [P, LP])
        region_m = sb("region_m", [P, LP])
        ctxT = region_k
        kT_cross = region_m
        kst = {"cross": region_k[:, :].bitcast(BF16), "self": sb("kst_self", [P, 2 * T], BF16)[:, :]}
        qs = sb("qs", [P, H, T], BF16)
        ring = sb("ring", [P, RING, T])
        vx = {"self": sb("vx_self", [P, H, SELF.tiles, HD]), "cross": sb("vx_cross", [P, H, CROSS.tiles, HD])}
        vh = [sb(f"vh{a}", [P, NC_, VW]) for a in range(2)]
        oev = [sb(f"oev{a}", [P, HALVES, BANK]) for a in range(2)]
        PIECE = LP // PAIRS
        spare = ring[:, 4:6, :].rearrange("p s n -> p (s n)")
        half = LP // 2
        kp_tmp = region_k[:, half:half + PIECE]
        kp = region_k[:, half + PIECE:LP].bitcast(BF16)
        qp = sb("qp", [P, 3, T], BF16)
        dens = qp[:, :, :].rearrange("p i n -> p (i n)").bitcast(F32)[:, 0:T]
        kp_self = spare[:, 0:3 * T // 2].bitcast(BF16).rearrange("p (i n) -> p i n", i=3)
        qT = {"self": sb("qT_self", [P, T]), "cross": sb("qT_cross", [P, T])}
        kT_self = sb("kT_self", [P, T])
        xT = sb("xT", [P, T])
        xn = sb("xn", [P, QT, D])
        yn = sb("yn", [P, QT, D])
        w = {n: sb("w_" + n, [P, D]) for n in ("q1", "k1", "v1", "o1", "q2", "k2", "v2", "o2")}
        bcol = {n: sb("b_" + n, [P, 1]) for n in ("q1", "k1", "q2", "k2")}
        brow = {n: sb("b_" + n, [P, D]) for n in ("v1", "o1", "v2", "o2")}
        ident = sb("ident", [P, P])
        qs_flat = qs[:, :, :].rearrange("p h n -> p (h n)")
        qs32 = qs[:, :, :].rearrange("p h n -> p (h n)").bitcast(F32).rearrange("p (h n) -> p h n", h=H)
        identb = sb("identb", [P, P], BF16)
        trib = sb("trib", [P, P], BF16)
        hblk = sb("hblk", [P, H])
        ext = {n: sb("ext_" + n, [P, 2]) for n in ("self", "cross")}
        size = sb("size", [P, 2])
        bound_q = {x: sb("bound_q" + x, [P, T], BF16) for x in ("pos", "neg")}
        bound_k = {x: sb("bound_k" + x, [P, 3 * 32], BF16) for x in ("pos", "neg")}
        limits = sb("limits", [P, 1])
        extc = sb("extc", [P, 2, PAIRS])
        shift = sb("shift", [H, T], BF16)
        inr = sb("inr", [P, T], BF16)
        good = sb("good", [P, 72])
        mk = sb("mk", [P, NC_])
        mku = sb("mku", [P, NC_])
        mkp = sb("mkp", [P, 3, NC_], BF16)
        st = sb("st", [P, QT, 6])
        mv = sb("mv", [P, QT, 2])
        rstd = sb("rstd", [P, QT])
        wg = sb("wg", [P, E])
        tri8 = sb("tri8", [P, E, E])
        lg = sb("lg", [P, QT, E])
        mx8 = sb("mx8", [P, QT])
        rk = [spare[:, i * QT * E * E:(i + 1) * QT * E * E].rearrange("p (t e j) -> p t e j", e=E, j=E) for i in range(2)]
        sel = sb("sel", [P, QT, E])
        wT = sb("wT", [E, T])
        ones = sb("ones", [P, 1])
        goods = sb("goods", [P, 2])
        held = sb("held", [1, 4])
        flag = sb("flag", [1, 1], I32)
        stat = sb("stat", [P, 4])
        MW = -(-LC // 8)
        MPIECES = [(c, min(MW, LC - c)) for c in range(0, LC, MW)]
        MCOLS = len(MPIECES)
        mchk = [kst["self"].bitcast(F32), yn[:, :, :].rearrange("p t c -> p (t c)")]
        row0 = region_m[:, 0:LC]

        qscr = {n: dram("qscr_" + n, [H, 3, HD, T], BF16) for n in ("self", "cross")}
        kscr = {"self": dram("kscr_self", [H, 3, HD, T], BF16), "cross": dram("kscr_cross", [H, 3, HD, LP], BF16)}
        sscr = {n: dram("sscr_" + n, [H, T], BF16) for n in ("self", "cross")}
        mscr = dram("mscr", [3, LP], BF16)
        oscr = {n: dram("oscr_" + n, [2, P, T], F32) for n in ("self", "cross")}
        wscr = dram("wscr", [E, T], F32)
        kTscr = dram("kTscr", [P, LP], F32)

        block = ctx.enter_context(nc.Block())
        g = lambda pair, per, off: pair * per + off

        def quadrant(a, part, half):
            return (2 * part + half + a) % 4

        def scores_and_values(pe, pl):
            n = pl.name
            scored, exped, valued = sem(n + "_scored"), sem(n + "_exped"), sem(n + "_valued")
            evicted, vh_ready, k_loaded = sem(n + "_evicted"), sem(n + "_vh_ready"), sem(n + "_k_loaded")

            def scores(p, first, s, q_base, k_base):
                a, pieces = pl.steps[s]
                if not (first and s < SLOTS):
                    pe.wait_ge(exped, g(p, pl.n, s - SLOTS + 1))
                if s == 0:
                    pe.wait_ge(k_loaded, g(p, 16 * NTERM, 16 * NTERM))
                for kt, x, q0, at in pieces:
                    keys = kst[n][:, bass.ds(k_base + kt * P, P)]
                    queries = lambda lo, hi: qs_flat[:, bass.ds(q_base[a] + lo, hi - lo)]
                    at += 2 * (s % SLOTS) * BANK
                    if pl.causal and q0 == kt * P:
                        pe.matmul(flat[:, at:at + P], identb[:, :], trib[:, :], start=True, stop=False)
                        last = pe.matmul(flat[:, at:at + P], keys, queries(q0, q0 + P), start=False, stop=True)
                        q0, at = q0 + P, at + P
                    m = (x + 1) * BANK - q0
                    if m:
                        last = pe.matmul(flat[:, at:at + m], keys, queries(q0, q0 + m), start=True, stop=True)
                last.then_inc(scored, 1)

            def values(p, first, gi):
                a, kts = pl.groups[gi]
                pe.wait_ge(exped, g(p, pl.n, pl.last_step(gi) + 1))
                if gi % pl.per_head == 0:
                    pe.wait_ge(vh_ready, g(p, 2, a + 1))
                    if not first:
                        pe.wait_ge(evicted, g(p - 1, 2, a + 1))
                if first and gi == 0:
                    pe.wait_ge(sem(n + "_ranged"), 2)
                for s, (kt, x, q0, at) in pl.pieces_of(gi):
                    row = 32 * quadrant(a, kt % 2, x)
                    last = pe.matmul(ps[row:row + VW, 6 + x, q0 - x * BANK:BANK], vh[a][:, kt, :],
                                     ring[:, s % RING, at:at + (x + 1) * BANK - q0],
                                     start=kt < 2, stop=pl.causal or kt + 2 >= pl.tiles, skip_group_check=True)
                last.then_inc(valued, 1)

            def pair(p, first):
                q_base, k_base = [(2 * p + a) * T for a in range(2)], (p % 2) * pl.width
                if not first:
                    for reg, base in zip(base_regs, q_base + [k_base]):
                        pe.reg_mov(reg, base)
                    q_base = [pe.snap(reg, min_val=0, max_val=(H - 1) * T) for reg in base_regs[:2]]
                    k_base = pe.snap(base_regs[2], min_val=0, max_val=pl.width)
                for s in range(pl.n):
                    scores(p, first, s, q_base, k_base)
                    for gi in range(len(pl.groups)):
                        at = pl.last_step(gi) + pl.lag
                        if at == s:
                            values(p, first, gi)
                        elif at == s + pl.n and not first:
                            values(p - 1, False, gi)

            base_regs = [pe.alloc_register(f"{n}_{base}") for base in ("q_base0", "q_base1", "k_base")]
            pair(0, True)
            pe.wait_ge(sem(n + "_q_loaded1"), 16 * QLOADS)
            if n == "cross":
                pe.wait_ge(sem("kfix_cross1"), 64)
            with pe.Fori(1, PAIRS) as p:
                pair(p, False)
            for gi in range(len(pl.groups)):
                if pl.last_step(gi) + pl.lag >= pl.n:
                    values(PAIRS - 1, False, gi)

        def exponentials(act, pl):
            n = pl.name
            scored, exped, valued = sem(n + "_scored"), sem(n + "_exped"), sem(n + "_valued")

            def pair(p, first):
                for s in range(pl.n):
                    at = 2 * (s % SLOTS) * BANK
                    lo, hi = pl.span(s)
                    before = s - RING
                    if before >= 0:
                        act.wait_ge(valued, g(p, len(pl.groups), pl.group_of(before) + 1))
                    elif not first:
                        act.wait_ge(valued, g(p - 1, len(pl.groups), pl.group_of(before + pl.n) + 1))
                    act.wait_ge(scored, g(p, pl.n, s + 1))
                    act.activation(ring[:, s % RING, lo:hi], flat[:, at + lo:at + hi], ACT.Exp).then_inc(exped, 1)

            pair(0, True)
            with act.Fori(1, PAIRS) as p:
                pair(p, False)

        def evict(dve, pl, p, first, a):
            n = pl.name
            dve.wait_ge(sem(n + "_valued"), g(p, len(pl.groups), (a + 1) * pl.per_head))
            if not first:
                dve.wait_ge(sem(f"{n}_stored{a}"), g(p, 32, 0))
            for x in range(HALVES):
                r0 = 32 * quadrant(a, 0, x)
                dve.tensor_copy(oev[a][0:VW, x, :], ps[r0:r0 + VW, 6 + x, :]).then_inc(sem(n + "_copied"), 1)
            for x in range(HALVES):
                r1 = 32 * quadrant(a, 1, x)
                c = P if pl.causal and x == 0 else 0
                dve.wait_ge(sem(n + "_copied"), g(p, 4, 2 * a + x + 1))
                last = dve.tensor_tensor(oev[a][0:VW, x, c:], oev[a][0:VW, x, c:], ps[r1:r1 + VW, 6 + x, c:], ALU.add)
            last.then_inc(sem(n + "_evicted"), 1)

        def head_values(pool, pl, meanwhile=None, then=None):
            n = pl.name

            def copy(p, a, first):
                if not first:
                    pool.wait_ge(sem(n + "_valued"), g(p - 1, len(pl.groups), (a + 1) * pl.per_head))
                pool.tensor_copy(vh[a][:, 0:pl.tiles, 0:HD],
                                 vx[n][:, bass.ds(2 * p + a, 1), :, :].rearrange("p h t c -> p (h t) c"))\
                    .then_inc(sem(n + "_vh_ready"), 1)

            def pair(p, first, last):
                copy(p, 1, first)
                if meanwhile:
                    meanwhile(p, first)
                if not last:
                    copy(p + 1, 0, False)
                if then:
                    then(p, first)

            copy(0, 0, True)
            pair(0, True, False)
            with pool.Fori(1, PAIRS - 1) as p:
                pair(p, False, False)
            pair(PAIRS - 1, False, True)

        def load_keys(sp, pl, p):
            n = pl.name
            for a in range(2):
                row = STACK * a
                for part in range(3):
                    terms = [i for i in range(NTERM) if KPART[i] == part]
                    src = kscr[n][bass.ds(2 * p + a, 1), part]
                    src = bass.AP(src.tensor, src.offset, [[0, len(terms)], [pl.width, HD], [1, pl.width]])
                    sp.dma_start(kst[n][row:row + HD * len(terms), bass.ds((p % 2) * pl.width, pl.width)], src)\
                        .then_inc(sem(n + "_k_loaded"), 16)
                    row += HD * len(terms)

        def store_heads(sp, pl):
            n = pl.name

            def store(p, a, last):
                sp.wait_ge(sem(n + "_evicted"), g(p, 2, a + 1))
                for i, dst in enumerate((xT[:, :], dens)):
                    row = 2 * HD * p + HD * a
                    dst = dst[row:row + HD, :] if last else oscr[n][i, bass.ds(row, HD), :]
                    sp.dma_start(dst, oev[a][i * HD:(i + 1) * HD, :, :].rearrange("c x n -> c (x n)"))\
                        .then_inc(sem(f"{n}_stored{a}"), 16)

            def pair(p, first):
                if not first:
                    sp.wait_ge(sem(n + "_scored"), g(p, pl.n, 0))
                sp.wait_ge(sem(n + "_k_loaded"), g(p, 16 * NTERM, 16 * NTERM))
                load_keys(sp, pl, p + 1)
                if not first:
                    store(p - 1, 1, False)
                store(p, 0, False)

            pair(0, True)
            with sp.Fori(1, PAIRS - 1) as p:
                pair(p, False)
            store(PAIRS - 2, 1, False)
            for a in range(2):
                sp.wait_ge(sem(f"{n}_stored{a}"), g(PAIRS - 1, 32, 0))
            rows = 2 * HD * (PAIRS - 1)
            for i, dst in enumerate((xT[:, :], dens)):
                sp.dma_start(dst[0:rows, :], oscr[n][i, 0:rows, :]).then_inc(sem(n + "_gathered"), 16)
            for a in range(2):
                store(PAIRS - 1, a, True)

        def split(dve, ch, src, parts, tmp, done):
            dve.tensor_copy(parts[0], src).then_inc(done, 1)
            dve.wait_ge(done, 1)
            ch.link(dve.tensor_tensor(tmp, src, parts[0], ALU.subtract))
            dve.tensor_copy(parts[1], tmp).then_inc(done, 1)
            dve.wait_ge(done, 2)
            dve.tensor_tensor(parts[2], tmp, parts[1], ALU.subtract).then_inc(done, 1)

        def queries_pe(pe, n, wq, turned=None):
            for x in range(HALVES):
                if turned:
                    pe.wait_ge(sem(turned + "_xT"), x + 1)
                pe.matmul(ps[:, x, :], wq[:, :], xT[:, x * BANK:(x + 1) * BANK], start=True, stop=True)\
                    .then_inc(sem(n + "_q_projected"), 1)

        def bounds_pe(pe, n):
            pe.wait_ge(sem(n + "_bound_keys"), 6)
            pe.wait_ge(sem(n + "_bound_queries"), 2)
            for x in range(HALVES):
                for sign in ("pos", "neg"):
                    last = pe.matmul(ps[0:3 * 32, 6 + x, :], bound_k[sign][:, :], bound_q[sign][:, x * BANK:(x + 1) * BANK],
                                     start=sign == "pos", stop=sign == "neg")
            last.then_inc(sem(n + "_bounds"), 1)

        def bounds_act(act, n):
            act.wait_ge(sem(n + "_q_ready"), 1)
            for sign, scale in (("pos", 1.0), ("neg", -1.0)):
                act.activation(bound_q[sign][:, :], qT[n][:, :], ACT.Relu, scale=scale).then_inc(sem(n + "_bound_queries"), 1)

        def bound_keys_dve(dve, ch, n):
            kmax, kmin = ext[n][:, 0:1], ext[n][:, 1:2]
            ch.link(dve.tensor_scalar(size[:, 1:2], kmin, -1.0, kmax, ALU.mult, ALU.max))
            ch.link(dve.tensor_tensor(size[:, 0:1], kmax, kmin, ALU.subtract))
            for sign, f, scale in (("pos", kmax, 1.0), ("neg", kmin, -1.0)):
                for i, (factor, s) in enumerate(((f, scale), (size[:, 0:1], 1.0), (size[:, 1:2], 1.0))):
                    dve.tensor_scalar(bound_k[sign][:, 32 * i:32 * i + H], hblk[:, :], factor, s, ALU.mult, ALU.mult)\
                        .then_inc(sem(n + "_bound_keys"), 1)

        def queries_dve(dve, ch, n, bq):
            for x in range(HALVES):
                dve.wait_ge(sem(n + "_q_projected"), x + 1)
                last = dve.tensor_scalar(qT[n][:, x * BANK:(x + 1) * BANK], ps[:, x, :], bq[:, :], SCALE, ALU.add, ALU.mult)
            last.then_inc(sem(n + "_q_ready"), 1)
            dve.wait_ge(sem(n + "_q_ready"), 1)
            split(dve, ch, qT[n][:, :], [qp[:, i, :] for i in range(3)], ring[:, 1, :], sem(n + "_q_split"))

        def shift_dve(dve, n):
            dve.wait_ge(sem(n + "_bounds"), 1)
            dve.tensor_scalar(shift[:, :], flat[0:H, 6 * BANK:8 * BANK], -1.0, None, ALU.mult).then_inc(sem(n + "_shift"), 1)

        def ranges_dve(dve, ch, n):
            lo, hi = 32, 64 + H
            dve.tensor_scalar(inr[lo:64, :], flat[lo:64, 6 * BANK:8 * BANK], limits[lo:64, :], None, ALU.is_le)\
                .then_inc(sem(n + "_ranged"), 1)
            dve.tensor_scalar(inr[64:hi, :], flat[64:hi, 6 * BANK:8 * BANK], limits[64:hi, :], None, ALU.is_le)\
                .then_inc(sem(n + "_ranged"), 1)
            dve.wait_ge(sem(n + "_ranged"), 2)
            ch.link(dve.tensor_reduce(good[lo:64, GOOD[n]:GOOD[n] + 1], inr[lo:64, :], AX.X, ALU.add))
            ch.link(dve.tensor_reduce(good[64:hi, GOOD[n]:GOOD[n] + 1], inr[64:hi, :], AX.X, ALU.add))

        def queries_sp(sp, n):
            for part in range(3):
                sp.wait_ge(sem(n + "_q_split"), part + 1)
                src = bass.AP(qscr[n], part * HD * T, [[3 * HD * T, H], [T, HD], [1, T]])
                sp.dma_start(src, qp[:, part, :]).then_inc(sem(n + "_q_stored"), 16)
            sp.wait_ge(sem(n + "_shift"), 1)
            sp.dma_start(sscr[n][:, :], shift[:, :]).then_inc(sem(n + "_shift_stored"), 16)
            sp.wait_ge(sem(n + "_q_stored"), 48)
            if n == "self":
                sp.wait_ge(sem("q_cleared"), 4)
            for wave, (lo, hi) in enumerate(WAVES):
                for a in range(2):
                    row, t = STACK * a, 0
                    while t < NTERM:
                        m = 1
                        while t + m < NTERM and QPART[t + m] == QPART[t + m - 1] + 1:
                            m += 1
                        src = qscr[n][2 * lo + a:2 * hi:2, 0:m].rearrange("h r d n -> h (r d) n").rearrange("h r n -> r h n")
                        sp.dma_start(qs[row:row + m * HD, 2 * lo + a:2 * hi:2, :], src)\
                            .then_inc(sem(f"{n}_q_loaded{wave}"), 16)
                        row, t = row + m * HD, t + m
                sp.wait_ge(sem(n + "_shift_stored"), 16)
                for a in range(2):
                    row = STACK * a + SHIFT_ROW
                    sp.dma_start(qs[row:row + 1, 2 * lo + a:2 * hi:2, :],
                                 bass.AP(sscr[n], (2 * lo + a) * T, [[0, 1], [2 * T, hi - lo], [1, T]]))\
                        .then_inc(sem(f"{n}_q_loaded{wave}"), 16)

        WAVES = ((0, 1), (1, PAIRS))
        QLOADS = 2 * 3 + 2
        BOUNDS_AT = 6
        LOADED = 4
        GOOD = {"self": 0, "cross": 1, "mask_sign": 2, "mask_rows": 3}
        HOLD = 2 * (32 + H) * T + T * LC + LP

        def normalise_heads(dve, ch, n):
            dve.wait_ge(sem(n + "_gathered"), 32)
            for a in range(2):
                dve.wait_ge(sem(f"{n}_stored{a}"), g(PAIRS, 32, 0))
            for x in range(HALVES):
                cols = slice(x * BANK, (x + 1) * BANK)
                ch.link(dve.reciprocal(ring[:, 2, cols], dens[:, cols]))
                dve.tensor_tensor(ring[:, 0, cols], xT[:, cols], ring[:, 2, cols], ALU.mult).then_inc(sem(n + "_heads"), 1)

        def project_out(pe, n, wo, heads):
            for x in range(HALVES):
                pe.wait_ge(sem(n + "_heads"), x + 1)
                for i in range(QT // HALVES):
                    t = x * QT // HALVES + i
                    last = pe.matmul(ps[:, x, i * P:(i + 1) * P], heads[:, t * P:(t + 1) * P], wo[:, :], start=True, stop=True)
                last.then_inc(sem(n + "_y"), 1)

        def norm_sums(dve, ch, n, x, bank):
            ts = range(x * QT // HALVES, (x + 1) * QT // HALVES)
            dve.wait_ge(sem(n + "_y"), x + 1)
            ch.link(dve.tensor_tensor(yn[:, ts.start:ts.stop, :].rearrange("p t c -> p (t c)"), ps[:, bank, :],
                                      xn[:, ts.start:ts.stop, :].rearrange("p t c -> p (t c)"), ALU.add))
            for t in ts:
                last = dve.bn_stats(st[:, t, :], yn[:, t, :])
            ch.link(last)

        def norm_dve(dve, ch, n, dst):
            for x in range(HALVES):
                norm_sums(dve, ch, n, x, x)
            norm_scale(dve, ch, n, dst)

        def norm_scale(dve, ch, n, dst):
            for t in range(QT):
                last = dve.bn_aggr(mv[:, t, :], st[:, t, :])
            ch.link(last)
            dve.tensor_scalar(rstd[:, :], mv[:, :, 1], EPS, None, ALU.add).then_inc(sem(n + "_var"), 1)
            dve.wait_ge(sem(n + "_std"), 1)
            ch.link(dve.reciprocal(rstd[:, :], rstd[:, :]))
            for t in range(QT):
                dve.tensor_scalar(dst[:, t, :], yn[:, t, :], mv[:, t, 0:1], rstd[:, t:t + 1], ALU.subtract, ALU.mult)\
                    .then_inc(sem(n + "_normed"), 1)

        def norm_act(act, n):
            act.wait_ge(sem(n + "_var"), 1)
            act.activation(rstd[:, :], rstd[:, :], ACT.Sqrt).then_inc(sem(n + "_std"), 1)

        def turn_pe(pe, n, src):
            for t in range(QT):
                pe.wait_ge(sem(n + "_normed"), t + 1)
                last = pe.transpose(ps[:, 2 + t // 4, t % 4 * P:(t % 4 + 1) * P], src[:, t, :], ident[:, :])
                if t % (QT // HALVES) == QT // HALVES - 1:
                    last.then_inc(sem(n + "_turned"), 1)

        def turn_dve(dve, n):
            for x in range(HALVES):
                dve.wait_ge(sem(n + "_turned"), x + 1)
                dve.tensor_copy(xT[:, x * BANK:(x + 1) * BANK], ps[:, 2 + x, :]).then_inc(sem(n + "_xT"), 1)

        srow = qs[:, :, :].rearrange("p h n -> p (h n)").bitcast(F32)
        mrow = [ring[:, :, :].rearrange("p s n -> p (s n)"), oev[0][:, :, :].rearrange("p x n -> p (x n)")]
        MR = RING * T
        heads_g = oev[1][:, :, :].rearrange("p x n -> p (x n)")
        probT = xT[:, :].rearrange("p (b n) -> p b n", b=2)
        qhead, orow = w["q1"], w["k1"]
        keys_of = {"gself": T, "gcross": LC}

        def key_chunks(n):
            return [(c, min(BANK, keys_of[n] - c)) for c in range(0, keys_of[n], BANK)]

        def key_groups(pl):
            return [list(range(k, min(k + 4, pl.tiles))) for k in range(0, pl.tiles, 4)]

        def general_pe(pe, n, pl, kT, q):
            chunks, groups = key_chunks(n), key_groups(pl)
            with pe.Fori(0, QT) as qt:
                with pe.Fori(0, H) as h:
                    it = qt * H + h
                    pe.wait_ge(sem(n + "_qhead"), it + 1)
                    for c, (k0, m) in enumerate(chunks):
                        if c >= 4:
                            pe.wait_ge(sem(n + "_masked"), it * len(chunks) + c - 3)
                        pe.matmul(ps[:, c % 4, 0:m], qhead[:, :], kT[:, k0:k0 + m], start=True, stop=True)\
                            .then_inc(sem(n + "_scored"), 1)
                    pe.wait_ge(sem(n + "_exped"), it + 1)

                    def turn(i):
                        if i >= 2:
                            pe.wait_ge(sem(n + "_probT"), it * len(groups) + i - 1)
                        for j, kt in enumerate(groups[i]):
                            last = pe.transpose(ps[:, 4 + i % 2, j * P:(j + 1) * P], srow[:, kt * P:(kt + 1) * P], ident[:, :])
                        last.then_inc(sem(n + "_turned_p"), 1)

                    turn(0)
                    for i, kts in enumerate(groups):
                        if i + 1 < len(groups):
                            turn(i + 1)
                        pe.wait_ge(sem(n + "_probT"), it * len(groups) + i + 1)
                        for j, kt in enumerate(kts):
                            last = pe.matmul(ps[:, 6, 0:HD], probT[:, i % 2, j * P:(j + 1) * P],
                                             vx[pl.name][:, bass.ds(h, 1), kt, 0:HD].rearrange("p h d -> p (h d)"),
                                             start=kt == 0, stop=kt == pl.tiles - 1)
                        last.then_inc(sem(n + "_summed"), 1)
                pe.wait_ge(sem(n + "_headed"), qt * (H + 1) + H)
                pe.transpose(ps[:, 7, 0:P], orow[:, :], ident[:, :]).then_inc(sem(n + "_turned_o"), 1)

        def general_act(act, n, pl):
            groups = key_groups(pl)
            with act.Fori(0, QT) as qt:
                with act.Fori(0, H) as h:
                    it = qt * H + h
                    act.wait_ge(sem(n + "_maxed"), it + 1)
                    act.activation(srow[:, 0:keys_of[n]], srow[:, 0:keys_of[n]], ACT.Exp, bias=stat[:, 1:2],
                                   accum_out=stat[:, 2:3]).then_inc(sem(n + "_exped"), 1)
                    for i, kts in enumerate(groups):
                        act.wait_ge(sem(n + "_turned_p"), it * len(groups) + i + 1)
                        if i >= 2:
                            act.wait_ge(sem(n + "_summed"), it * len(groups) + i - 1)
                        act.activation(probT[:, i % 2, 0:len(kts) * P], ps[:, 4 + i % 2, 0:len(kts) * P], ACT.Copy)\
                            .then_inc(sem(n + "_probT"), 1)

        def general_dve(dve, n, pl, q, factor):
            chunks, groups = key_chunks(n), key_groups(pl)
            with dve.Fori(0, QT) as qt:
                with dve.Fori(0, H) as h:
                    it = qt * H + h
                    dve.tensor_scalar(qhead[:, :], q[:, bass.ds(qt * P, P)], hblk[:, bass.ds(h, 1)], None, ALU.mult)\
                        .then_inc(sem(n + "_qhead"), 1)
                    dve.wait_ge(sem(n + "_mask_in"), (qt + 1) * 32)
                    for c, (k0, m) in enumerate(chunks):
                        mask = mrow[0][:, k0:k0 + m] if k0 < MR else mrow[1][:, k0 - MR:k0 - MR + m]
                        dve.wait_ge(sem(n + "_scored"), it * len(chunks) + c + 1)
                        dve.scalar_tensor_tensor(out=srow[:, k0:k0 + m], in0=mask, scalar=factor, in1=ps[:, c % 4, 0:m],
                                                 op0=ALU.mult, op1=ALU.add).then_inc(sem(n + "_masked"), 1)
                    dve.wait_ge(sem(n + "_masked"), (it + 1) * len(chunks))
                    dve.tensor_reduce(stat[:, 0:1], srow[:, 0:keys_of[n]], AX.X, ALU.max).then_inc(sem(n + "_stat"), 1)
                    dve.wait_ge(sem(n + "_stat"), 2 * it + 1)
                    dve.tensor_scalar(stat[:, 1:2], stat[:, 0:1], -1.0, None, ALU.mult).then_inc(sem(n + "_maxed"), 1)
                    dve.wait_ge(sem(n + "_exped"), it + 1)
                    dve.reciprocal(stat[:, 3:4], stat[:, 2:3]).then_inc(sem(n + "_stat"), 1)
                    dve.wait_ge(sem(n + "_stat"), 2 * it + 2)
                    dve.wait_ge(sem(n + "_summed"), (it + 1) * len(groups))
                    dve.tensor_scalar(orow[:, bass.ds(h * HD, HD)], ps[:, 6, 0:HD], stat[:, 3:4], None, ALU.mult)\
                        .then_inc(sem(n + "_headed"), 1)
                dve.wait_ge(sem(n + "_turned_o"), qt + 1)
                dve.tensor_copy(heads_g[:, bass.ds(qt * P, P)], ps[:, 7, 0:P]).then_inc(sem(n + "_headed"), 1)
            dve.wait_ge(sem(n + "_headed"), QT * (H + 1))

        def general_sp(sp, n, mask):
            wide = keys_of[n]
            cut = MR if wide > MR else wide // 2

            def load(qt):
                rows = mask[bass.ds(qt * P, P), :]
                second = mrow[1][:, 0:wide - cut] if wide > MR else mrow[0][:, cut:wide]
                sp.dma_start(mrow[0][:, 0:cut], rows[:, 0:cut]).then_inc(sem(n + "_mask_in"), 16)
                sp.dma_start(second, rows[:, cut:wide]).then_inc(sem(n + "_mask_in"), 16)

            load(0)
            with sp.Fori(1, QT) as qt:
                sp.wait_ge(sem(n + "_masked"), qt * H * len(key_chunks(n)))
                load(qt)

        def fast_failed(eng):
            eng.wait_ge(sem("flagged"), 1)
            return eng.value_load(flag[0:1, 0:1], min_val=0, max_val=1) != 0

        w1 = region_m[:, 0:HID]
        w2 = region_m[:, HID:2 * HID]
        w3 = region_m[:, 2 * HID:2 * HID + len(FCH) * D].rearrange("p (j c) -> p j c", c=D)
        wbc = [qs[:, :, :].rearrange("p h n -> p (h n)").bitcast(F32)[:, i * T:(i + 1) * T] for i in range(8)] + \
            [region_k[:, i * T:(i + 1) * T] for i in range(3)]
        SPREADS = 6
        segments = lambda j: (FCH[j][0] + FCH[j][1] - 1) // HE - FCH[j][0] // HE + 1
        UNITS = [(j, x) for x in range(HALVES) for j in FORDER if j >= NEXP] + \
            [(j, x) for x in range(HALVES) for j in FORDER if j < NEXP]
        FIRST_HALF = UNITS.index((FORDER[-1], 0))

        def queries_sp_self(sp):
            sp.wait_ge(sem("self_k_split"), 1)
            for part in range(3):
                sp.dma_start(bass.AP(kscr["self"], part * HD * T, [[3 * HD * T, H], [T, HD], [1, T]]), kp_self[:, part, :])\
                    .then_inc(sem("self_k_stored"), 16)
            sp.wait_ge(sem("self_k_stored"), 48)
            sp.wait_ge(sem("k_cleared"), 2)
            for a in range(2):
                for b in range(2):
                    row = STACK * a + SHIFT_ROW
                    sp.dma_start(kst["self"][row:row + 1, b * T:(b + 1) * T], A["c_ones"][:, 0:T]).then_inc(sem("kfix_self"), 16)
            load_keys(sp, SELF, 0)
            queries_sp(sp, "self")

        def hbuf(i):
            return ring[:, i % 4, 0:BANK]

        @block.sync
        def _(sp):
            ld = lambda dst, src, s: sp.dma_start(dst, src).then_inc(sem(s), 16)
            ld(xT[:, :], A["xT"], "ld_q1")
            ld(w["q1"][:, :], A["w_q1"], "ld_q1")
            for n in ("q1", "k1"):
                ld(bcol[n][:, :], A["b_" + n], "ld_bcol")
            ld(w["v1"][:, :], A["w_v1"], "ld_v1")
            ld(brow["v1"][:, :], bass.AP(A["b_v1"].tensor, 0, [[0, P], [1, D]]), "ld_v1")
            for i, n in enumerate(("hblk", "trib", "identb", "ident")):
                ld({"hblk": hblk, "trib": trib, "identb": identb, "ident": ident}[n][:, :], A["c_" + n], "ld_const")
            for n in ("k2", "v2"):
                ld(w[n][:, :], A["w_" + n], "ld_kv2")
            ld(bcol["k2"][:, :], A["b_k2"], "ld_kv2")
            ld(brow["v2"][:, :], bass.AP(A["b_v2"].tensor, 0, [[0, P], [1, D]]), "ld_kv2")
            queries_sp_self(sp)
            store_heads(sp, SELF)
            sp.wait_ge(sem("mask_split"), 3)
            for i in range(3):
                sp.dma_start(mscr[i, :].rearrange("(p j) -> p j", p=P), mkp[:, i, :]).then_inc(sem("mask_stored"), 16)
            sp.wait_ge(sem("k_stored"), 8 * 48)
            sp.wait_ge(sem("mask_stored"), 48)
            for b in range(2):
                sp.wait_ge(sem("cross_cleared"), b + 1)
                for a in range(2):
                    row = STACK * a + SHIFT_ROW
                    sp.dma_start(kst["cross"][row:row + 1, b * LP:(b + 1) * LP], A["c_ones"]).then_inc(sem(f"kfix_cross{b}"), 16)
                    sp.dma_start(kst["cross"][row + 1:row + 4, b * LP:(b + 1) * LP], mscr[:, :]).then_inc(sem(f"kfix_cross{b}"), 16)
                if b == 0:
                    load_keys(sp, CROSS, 0)
                    queries_sp(sp, "cross")
            store_heads(sp, CROSS)
            with sp.If(fast_failed(sp)):
                sp.wait_ge(sem("cross_heads"), 2)
                sp.dma_start(region_k[:, :], kTscr[:, :]).then_inc(sem("general_in"), 16)
                sp.dma_start(xn[:, :, :], A["x"][0].rearrange("(t p) c -> p t c", p=P)).then_inc(sem("general_in"), 16)
                general_sp(sp, "gself", A["c_causal"])
                sp.wait_ge(sem("gself_masked"), QT * H * len(key_chunks("gself")))
                general_sp(sp, "gcross", A["mask"])
            with sp.Else():
                sp.nop()
            sp.wait_ge(sem("wT_ready"), 1)
            sp.dma_start(wscr[:, :], wT[:, :]).then_inc(sem("w_stored"), 16)
            sp.wait_ge(sem("w_stored"), 16)
            for x in range(HALVES):
                for j, (c, m) in enumerate(FCH[:NEXP]):
                    r = 0
                    while r < m:
                        e = (c + r) // HE
                        k = min(m - r, (e + 1) * HE - c - r)
                        sp.dma_start(wbc[j][r:r + k, x * BANK:(x + 1) * BANK], bass.AP(wscr, e * T + x * BANK, [[0, k], [1, BANK]]))\
                            .then_inc(sem("w_spread_late") if x else sem(f"w_spread{j // SPREADS}"), 16)
                        r += k
            sp.wait_ge(sem("ffn_normed"), QT)
            sp.dma_start(out[0].rearrange("(t p) c -> p t c", p=P), yn[:, :, :]).then_inc(sem("stored"), 16)
            sp.wait_ge(sem("stored"), 16)

        @block.gpsimd
        def _(pool):
            ld = lambda dst, src, s: pool.dma_start(dst, src).then_inc(sem(s), 16)
            for a in range(2):
                r = STACK * a + 32
                pool.memset(kst["self"][r:r + 32, :].bitcast(F32), 0.0).then_inc(sem("k_cleared"), 1)
            pool.wait_ge(sem("k_cleared"), 2)
            for a in range(2):
                r = STACK * a + 32
                pool.memset(qs32[r:r + 32, a:H:2, :], ONES_PAIR).then_inc(sem("q_cleared"), 1)
            pool.wait_ge(sem("q_cleared"), 4)
            for a in range(2):
                pool.memset(vh[a][:, :, HD:VW], 1.0).then_inc(sem("v_ones"), 1)
                pool.wait_ge(sem("v_ones"), a + 1)
            pool.wait_ge(sem("self_v_ready"), 1)
            pool.wait_ge(sem("ctx_v_projected"), len(CH))
            pool.wait_ge(sem("k_evicted"), len(CH))

            def store_key_piece(p, first):
                pool.wait_ge(sem("k_split"), g(p, 1, 1))
                if not first:
                    pool.wait_ge(sem("k_stored"), g(p, 48, 0))
                for part in range(3):
                    pool.dma_start(bass.AP(kscr["cross"], p * PIECE + part * HD * LP, [[3 * HD * LP, H], [LP, HD], [1, PIECE]]),
                                   kp[:, bass.ds((p % 2) * 3 * PIECE + part * PIECE, PIECE)]).then_inc(sem("k_stored"), 16)
                piece = bass.ds(p * PIECE, PIECE)
                pool.dma_start(kTscr[:, piece], kT_cross[:, piece]).then_inc(sem("kT_saved"), 16)
                if first:
                    pool.memset(region_k[:, 0:half], 0.0).then_inc(sem("cross_cleared"), 1)

            head_values(pool, SELF, then=store_key_piece)
            pool.wait_ge(sem("k_stored"), PAIRS * 48)
            pool.memset(region_k[:, half:LP], 0.0).then_inc(sem("cross_cleared"), 1)
            pool.wait_ge(sem("extrema"), 2 * PAIRS)
            pool.wait_ge(sem("cross_v_ready"), len(CH))
            pool.wait_ge(sem("self_valued"), g(PAIRS, len(SELF.groups), 0))

            def load_mask_rows(p, first):
                for j, (c, m) in enumerate(MPIECES):
                    if j >= 2 or not first:
                        pool.wait_ge(sem("checked"), g(p, MCOLS, j - 1))
                    pool.dma_start(mchk[j % 2][:, 0:m], A["mask"][bass.ds(p * P, P), c:c + m])\
                        .then_inc(sem(f"ld_mask{j % 2}"), 16)

            def mask_rows(p, first):
                if first:
                    pool.wait_ge(sem("self_normed"), QT)
                    pool.wait_ge(sem("kT_saved"), 16 * PAIRS)
                    pool.wait_ge(sem("cross_q_loaded1"), 16 * QLOADS)
                    ld(row0, bass.AP(A["mask"].tensor, 0, [[0, P], [1, LC]]), "ld_row0")
                load_mask_rows(p, first)

            head_values(pool, CROSS, meanwhile=mask_rows)
            pool.wait_ge(sem("checked"), MCOLS * PAIRS)
            for dst, src in ((w1, "w1"), (w2, "w2"), (w3, "w3")):
                ld(dst, A[src], "ld_ffn")

        @block.tensor
        def _(pe):
            pe.wait_ge(sem("ld_q1"), 32)
            queries_pe(pe, "self", w["q1"])
            pe.wait_ge(sem("ld_k1"), 16)
            for x in range(HALVES):
                last = pe.matmul(ps[:, 2 + x, :], w["k1"][:, :], xT[:, x * BANK:(x + 1) * BANK], start=True, stop=True)
            last.then_inc(sem("self_kv_projected"), 1)
            pe.wait_ge(sem("ld_v1"), 32)
            for t in range(QT):
                last = pe.matmul(ps[:, 4 + t // 4, t % 4 * P:(t % 4 + 1) * P], xT[:, t * P:(t + 1) * P], w["v1"][:, :],
                                 start=True, stop=True)
            last.then_inc(sem("self_kv_projected"), 1)
            pe.wait_ge(sem("ld_kv2"), 64)
            pe.wait_ge(sem("self_k_out"), 1)
            for i, (c, m) in enumerate(CH):
                if i == BOUNDS_AT:
                    pe.wait_ge(sem("ld_const"), 64)
                    bounds_pe(pe, "self")
                pe.wait_ge(sem(f"ld_ctx{i // LOADED}"), 16)
                if i >= 2:
                    pe.wait_ge(sem("k_evicted"), i - 1)
                pe.matmul(ps[:, 2 + i % 2, 0:m], w["k2"][:, :], ctxT[:, c:c + m], start=True, stop=True)\
                    .then_inc(sem("ctx_k_projected"), 1)
            for i, (c, m) in enumerate(CH):
                if i == 0:
                    pe.wait_ge(sem("k_evicted"), len(CH))
                elif i >= 2:
                    pe.wait_ge(sem("cross_v_ready"), i - 1)
                for t in range(m // P):
                    last = pe.matmul(ps[:, 2 + i % 2, t * P:(t + 1) * P], ctxT[:, c + t * P:c + (t + 1) * P], w["v2"][:, :],
                                     start=True, stop=True)
                last.then_inc(sem("ctx_v_projected"), 1)
            pe.wait_ge(sem("cross_v_ready"), len(CH))
            pe.wait_ge(sem("self_v_ready"), 1)
            pe.wait_ge(sem("self_q_loaded0"), 16 * QLOADS)
            pe.wait_ge(sem("kfix_self"), 64)
            pe.wait_ge(sem("self_shift"), 1)
            scores_and_values(pe, SELF)
            pe.wait_ge(sem("ld_late"), 16 * 10)
            project_out(pe, "self", w["o1"], ring[:, 0, :])
            turn_pe(pe, "self", xn)
            queries_pe(pe, "cross", w["q2"], "self")
            bounds_pe(pe, "cross")
            pe.wait_ge(sem("cross_q_loaded0"), 16 * QLOADS)
            pe.wait_ge(sem("kfix_cross0"), 64)
            scores_and_values(pe, CROSS)
            pe.wait_ge(sem("goods_summed"), 2)
            pe.matmul(ps[0:1, 0, 0:2], ones[:, :], goods[:, :], start=True, stop=True).then_inc(sem("goods_counted"), 1)
            with pe.If(fast_failed(pe)):
                general_pe(pe, "gself", SELF, kT_self[:, :], qT["self"])
                project_out(pe, "gself", w["o1"], heads_g)
                turn_pe(pe, "gself", xn)
                queries_pe(pe, "gcross", w["q2"], "gself")
                general_pe(pe, "gcross", CROSS, region_k[:, :], qT["cross"])
                pe.wait_ge(sem("general_done"), 1)
            with pe.Else():
                pe.nop()
            project_out(pe, "cross", w["o2"], ring[:, 0, :])
            turn_pe(pe, "cross", xn)
            pe.wait_ge(sem("cross_xT"), 2)
            for t in range(QT):
                last = pe.matmul(ps[:, 4, t * E:(t + 1) * E], xT[:, t * P:(t + 1) * P], wg[:, :], start=True, stop=True)
            last.then_inc(sem("routed"), 1)
            pe.wait_ge(sem("ld_ffn"), 48)

            def hidden(i):
                j, x = UNITS[i]
                c, m = FCH[j]
                if i >= 3:
                    pe.wait_ge(sem("gated"), i - 2)
                if i == 2:
                    pe.wait_ge(sem("wT_ready"), 1)
                for k, wk in enumerate((w1, w2)):
                    last = pe.matmul(ps[0:m, 2 * (i % 3) + k, :], wk[:, c:c + m], xT[:, x * BANK:(x + 1) * BANK],
                                     start=True, stop=True)
                last.then_inc(sem("hidden"), 1)

            def down(i):
                j, x = UNITS[i]
                c, m = FCH[j]
                if j >= NEXP:
                    pe.wait_ge(sem("gated"), i + 1)
                else:
                    pe.wait_ge(sem("activated"), i + 1 - 2 * (len(FCH) - NEXP))
                pe.matmul(ps[:, 6 + x, :], w3[0:m, j, :], hbuf(i)[0:m, :], start=j == FORDER[0],
                          stop=j == FORDER[-1]).then_inc(sem("down"), 1)

            def turn_y(x):
                pe.wait_ge(sem("yT_copied"), x + 1)
                for t in range(QT // HALVES):
                    at = x * BANK + t * P
                    last = pe.transpose(ps[:, 6 + x, t * P:(t + 1) * P], ring[:, 5, at:at + P], ident[:, :])
                last.then_inc(sem("ffn_y"), 1)

            hidden(0)
            hidden(1)
            pe.wait_ge(sem("sel_ready"), 1)
            for t in range(QT):
                last = pe.transpose(ps[0:E, 4 + t // 4, t % 4 * P:(t % 4 + 1) * P], sel[:, t, :], ident[:, :])
            last.then_inc(sem("wT_turned"), 1)
            for i in range(2, len(UNITS) + 2):
                if i < len(UNITS):
                    hidden(i)
                down(i - 2)
                if i - 2 == FIRST_HALF + 2:
                    turn_y(0)
            turn_y(1)

        @block.scalar
        def _(act):
            ld = lambda dst, src, s: act.dma_start(dst, src).then_inc(sem(s), 16)
            ld(w["k1"][:, :], A["w_k1"], "ld_k1")
            for i in range(0, len(CH), LOADED):
                c, m = CH[i][0], sum(m for _, m in CH[i:i + LOADED])
                ld(ctxT[:, c:c + m], A["ctxT"][:, c:c + m], f"ld_ctx{i // LOADED}")
            act.wait_ge(sem("ld_bcol"), 32)
            act.wait_ge(sem("self_kv_projected"), 1)
            act.activation(kT_self[:, :], flat[:, 2 * BANK:2 * BANK + T], ACT.Identity, bias=bcol["k1"][:, :])\
                .then_inc(sem("self_k_out"), 1)
            act.wait_ge(sem("self_k_out"), 1)
            act.activation(kp_self[:, 0, :], kT_self[:, :], ACT.Copy).then_inc(sem("self_k_out"), 1)
            bounds_act(act, "self")
            act.wait_ge(sem("ld_kv2"), 64)
            for i, (c, m) in enumerate(CH):
                act.wait_ge(sem("ctx_k_projected"), i + 1)
                act.activation(kT_cross[:, c:c + m], ps[:, 2 + i % 2, 0:m], ACT.Identity, bias=bcol["k2"][:, :])\
                    .then_inc(sem("k_evicted"), 1)
            ld(mk[:, :], A["mask"][0, :].rearrange("(p j) -> p j", p=P), "ld_late")
            ld(xn[:, :, :], A["x"][0].rearrange("(t p) c -> p t c", p=P), "ld_late")
            for n in ("o1", "q2", "o2"):
                ld(w[n][:, :], A["w_" + n], "ld_late")
            ld(bcol["q2"][:, :], A["b_q2"], "ld_late")
            for n in ("o1", "o2"):
                ld(brow[n][:, :], bass.AP(A["b_" + n].tensor, 0, [[0, P], [1, D]]), "ld_late")
            ld(wg[:, :], A["wg"], "ld_late")
            ld(tri8[:, :, :], bass.AP(A["c_tri8"].tensor, 0, [[0, P], [E, E], [1, E]]), "ld_late")
            exponentials(act, SELF)
            norm_act(act, "self")
            bounds_act(act, "cross")
            exponentials(act, CROSS)
            with act.If(fast_failed(act)):
                general_act(act, "gself", SELF)
                norm_act(act, "gself")
                general_act(act, "gcross", CROSS)
            with act.Else():
                act.nop()
            norm_act(act, "cross")
            act.wait_ge(sem("logits_shifted"), 1)
            act.activation(lg[:, :, :], lg[:, :, :], ACT.Exp).then_inc(sem("logits_exped"), 1)
            for i, (j, x) in enumerate(UNITS):
                m = FCH[j][1]
                act.wait_ge(sem("hidden"), i + 1)
                if i >= 4:
                    act.wait_ge(sem("down"), i - 3)
                act.activation(hbuf(i)[0:m, :], ps[0:m, 2 * (i % 3), :], ACT.Silu).then_inc(sem("silued"), 1)
            norm_act(act, "ffn")

        @block.vector
        def _(dve):
            ch = Chain(dve, "dve_chain")
            for a in range(2):
                r = STACK * (1 - a)
                dve.memset(qs32[r:r + STACK, a:H:2, :], 0.0).then_inc(sem("q_cleared"), 1)
            dve.memset(good[:, :], 0.0)
            for sign in ("pos", "neg"):
                dve.memset(bound_k[sign][:, :], 0.0)
            dve.memset(limits[32:64, :], SPREAD)
            ch.link(dve.memset(limits[64:96, :], LARGEST))
            dve.wait_ge(sem("ld_bcol"), 32)
            queries_dve(dve, ch, "self", bcol["q1"])
            dve.wait_ge(sem("self_k_out"), 2)
            tmp, parts = ring[:, 2, :], [kp_self[:, i, :] for i in range(3)]
            ch.link(dve.tensor_tensor(tmp, kT_self[:, :], parts[0], ALU.subtract))
            ch.link(dve.tensor_copy(parts[1], tmp))
            dve.tensor_tensor(parts[2], tmp, parts[1], ALU.subtract).then_inc(sem("self_k_split"), 1)
            ch.link(dve.tensor_reduce(ext["self"][:, 0:1], kT_self[:, :], AX.X, ALU.max))
            ch.link(dve.tensor_reduce(ext["self"][:, 1:2], kT_self[:, :], AX.X, ALU.min))
            dve.wait_ge(sem("ld_const"), 64)
            bound_keys_dve(dve, ch, "self")
            shift_dve(dve, "self")
            by_head = lambda v: v.rearrange("p (t h d) -> p t h d", h=H, d=HD)
            rows = lambda b, n: bass.AP(b, 0, [[D, P], [0, n], [HD, H], [1, HD]])
            dve.wait_ge(sem("self_kv_projected"), 2)
            dve.wait_ge(sem("ld_v1"), 32)
            for x in range(HALVES):
                n = QT // HALVES
                last = dve.tensor_tensor(vx["self"][:, :, x * n:(x + 1) * n, 0:HD].rearrange("p h t d -> p t h d"),
                                         by_head(ps[:, 4 + x, :]), rows(brow["v1"], n), ALU.add)
            last.then_inc(sem("self_v_ready"), 1)
            ranges_dve(dve, ch, "self")

            def extremum(i):
                j, op = i // 2, (ALU.max, ALU.min)[i % 2]
                piece = kT_cross[:, j * PIECE:min((j + 1) * PIECE, LC)]
                dve.wait_ge(sem("k_evicted"), -(-min((j + 1) * PIECE, LP) // BANK))
                dve.tensor_reduce(extc[:, i % 2, j:j + 1], piece, AX.X, op).then_inc(sem("extrema"), 1)

            for i in range(2):
                extremum(i)
            dve.wait_ge(sem("ld_kv2"), 64)
            for i, (c, m) in enumerate(CH):
                n = m // P
                dve.wait_ge(sem("ctx_v_projected"), i + 1)
                dve.tensor_tensor(vx["cross"][:, :, 4 * i:4 * i + n, 0:HD].rearrange("p h t d -> p t h d"),
                                  by_head(ps[:, 2 + i % 2, 0:m]), rows(brow["v2"], n), ALU.add)\
                    .then_inc(sem("cross_v_ready"), 1)
            dve.wait_ge(sem("ld_late"), 16 * 10)
            ch.link(dve.tensor_scalar(mku[:, :], mk[:, :], MASKED, None, ALU.mult))
            split(dve, ch, mku[:, :], [mkp[:, i, :] for i in range(3)], mku[:, :], sem("mask_split"))
            for p in range(PAIRS):
                src = kT_cross[:, p * PIECE:(p + 1) * PIECE]
                parts = [kp[:, (3 * (p % 2) + i) * PIECE:(3 * (p % 2) + i + 1) * PIECE] for i in range(3)]
                if p == 0:
                    dve.wait_ge(sem("ctx_v_projected"), len(CH))
                elif p >= 2:
                    dve.wait_ge(sem("k_stored"), 48 * (p - 1))
                ch.link(dve.tensor_copy(parts[0], src))
                ch.link(dve.tensor_tensor(kp_tmp, src, parts[0], ALU.subtract))
                evict(dve, SELF, p, p == 0, 0)
                ch.link(dve.tensor_copy(parts[1], kp_tmp))
                dve.tensor_tensor(parts[2], kp_tmp, parts[1], ALU.subtract).then_inc(sem("k_split"), 1)
                dve.wait_ge(sem("k_split"), p + 1)
                for i in range(2 * p + 2, min(2 * p + 4, 2 * PAIRS)):
                    extremum(i)
                evict(dve, SELF, p, p == 0, 1)
            dve.wait_ge(sem("extrema"), 2 * PAIRS)
            ch.link(dve.tensor_reduce(ext["cross"][:, 0:1], extc[:, 0, :], AX.X, ALU.max))
            ch.link(dve.tensor_reduce(ext["cross"][:, 1:2], extc[:, 1, :], AX.X, ALU.min))
            bound_keys_dve(dve, ch, "cross")
            for t in range(QT):
                last = dve.tensor_tensor(xn[:, t, :], xn[:, t, :], brow["o1"][:, :], ALU.add)
            ch.link(last)
            dve.wait_ge(sem("self_valued"), g(PAIRS, len(SELF.groups), 0))
            normalise_heads(dve, ch, "self")
            norm_dve(dve, ch, "self", xn)
            turn_dve(dve, "self")
            queries_dve(dve, ch, "cross", bcol["q2"])
            shift_dve(dve, "cross")
            ranges_dve(dve, ch, "cross")
            for t in range(QT):
                last = dve.tensor_tensor(xn[:, t, :], xn[:, t, :], brow["o2"][:, :], ALU.add)
            ch.link(last)
            ch.link(dve.memset(ones[:, :], 1.0))
            ch.link(dve.tensor_scalar(mku[:, :], mk[:, :], 0.0, None, ALU.is_ge))
            ch.link(dve.tensor_reduce(good[:, GOOD["mask_sign"]:GOOD["mask_sign"] + 1], mku[:, :], AX.X, ALU.add))
            ch.link(dve.tensor_scalar(mku[:, :], mk[:, :], 0.0, None, ALU.is_equal))
            dve.tensor_reduce(goods[:, 1:2], mku[:, :], AX.X, ALU.add).then_inc(sem("goods_summed"), 1)
            dve.wait_ge(sem("ld_row0"), 16)

            def check_mask(p, j):
                c, m = MPIECES[j]
                piece = mchk[j % 2][:, 0:m]
                dve.wait_ge(sem(f"ld_mask{j % 2}"), g(p, 8 * MCOLS, 16 * (j // 2 + 1)))
                dve.tensor_tensor(piece, piece, row0[:, c:c + m], ALU.is_equal).then_inc(sem("compared"), 1)
                dve.wait_ge(sem("compared"), g(p, MCOLS, j + 1))
                dve.tensor_reduce(good[:, bass.ds(p * MCOLS + GOOD["mask_rows"] + j, 1)], piece, AX.X, ALU.add)\
                    .then_inc(sem("checked"), 1)

            def cross_pair(p, first):
                for a in range(2):
                    for j in range(a * MCOLS // 2, (a + 1) * MCOLS // 2):
                        check_mask(p, j)
                    evict(dve, CROSS, p, first, a)

            cross_pair(0, True)
            with dve.Fori(1, PAIRS) as p:
                cross_pair(p, False)
            dve.wait_ge(sem("checked"), MCOLS * PAIRS)
            dve.tensor_reduce(goods[:, 0:1], good[:, :], AX.X, ALU.add).then_inc(sem("goods_summed"), 1)
            dve.wait_ge(sem("goods_counted"), 1)
            ch.link(dve.tensor_scalar(held[:, 0:1], ps[0:1, 0, 0:1], float(HOLD), None, ALU.not_equal))
            ch.link(dve.tensor_scalar(held[:, 1:2], ps[0:1, 0, 1:2], 0.5, None, ALU.is_lt))
            dve.tensor_tensor(flag[:, :], held[:, 0:1], held[:, 1:2], ALU.max).then_inc(sem("flagged"), 1)
            normalise_heads(dve, ch, "cross")
            with dve.If(fast_failed(dve)):
                gch = Chain(dve, "dve_general_chain")
                dve.wait_ge(sem("general_in"), 32)
                dve.wait_ge(sem("cross_heads"), 2)
                general_dve(dve, "gself", SELF, qT["self"], -float(np.finfo(np.float32).max))
                for t in range(QT):
                    last = dve.tensor_tensor(xn[:, t, :], xn[:, t, :], brow["o1"][:, :], ALU.add)
                last.then_inc(sem("gself_heads"), 2)
                dve.wait_ge(sem("gself_heads"), 2)
                norm_dve(dve, gch, "gself", xn)
                turn_dve(dve, "gself")
                dve.wait_ge(sem("gcross_q_projected"), 2)
                gch.link(dve.tensor_scalar(qT["cross"][:, :], flat[:, 0:T], bcol["q2"][:, :], SCALE, ALU.add, ALU.mult))
                for t in range(QT):
                    last = dve.tensor_tensor(xn[:, t, :], xn[:, t, :], brow["o2"][:, :], ALU.add)
                gch.link(last)
                gch.link(dve.memset(srow[:, LC:LP], 0.0))
                general_dve(dve, "gcross", CROSS, qT["cross"], MASKED)
                dve.tensor_copy(ring[:, 0, :], heads_g).then_inc(sem("general_done"), 1)
                dve.wait_ge(sem("general_done"), 1)
            with dve.Else():
                dve.nop()
            norm_dve(dve, ch, "cross", xn)
            turn_dve(dve, "cross")
            dve.wait_ge(sem("routed"), 1)
            ch.link(dve.tensor_copy(lg[:, :, :].rearrange("p t e -> p (t e)"), ps[:, 4, 0:QT * E]))
            lj = bass.AP(lg, 0, [[QT * E, P], [E, QT], [0, E], [1, E]])
            le = bass.AP(lg, 0, [[QT * E, P], [E, QT], [1, E], [0, E]])
            low = bass.AP(tri8, 0, [[E * E, P], [0, QT], [E, E], [1, E]])
            ch.link(dve.tensor_tensor(rk[0], lj, le, ALU.is_ge))
            ch.link(dve.tensor_tensor(rk[0], rk[0], low, ALU.mult))
            ch.link(dve.tensor_tensor(rk[1], lj, le, ALU.is_gt))
            ch.link(dve.tensor_tensor(rk[0], rk[0], rk[1], ALU.max))
            ch.link(dve.tensor_reduce(sel[:, :, :], rk[0], AX.X, ALU.add))
            ch.link(dve.tensor_reduce(mx8[:, :], lg[:, :, :], AX.X, ALU.max))
            ch.link(dve.tensor_scalar(sel[:, :, :], sel[:, :, :], 2.0, None, ALU.is_lt))
            dve.tensor_tensor(lg[:, :, :], lg[:, :, :], bass.AP(mx8, 0, [[QT, P], [1, QT], [0, E]]), ALU.subtract)\
                .then_inc(sem("logits_shifted"), 1)
            dve.wait_ge(sem("logits_exped"), 1)
            ch.link(dve.tensor_tensor(sel[:, :, :], sel[:, :, :], lg[:, :, :], ALU.mult))
            ch.link(dve.tensor_reduce(mx8[:, :], sel[:, :, :], AX.X, ALU.add))
            ch.link(dve.reciprocal(mx8[:, :], mx8[:, :]))
            dve.tensor_tensor(sel[:, :, :], sel[:, :, :], bass.AP(mx8, 0, [[QT, P], [1, QT], [0, E]]), ALU.mult)\
                .then_inc(sem("sel_ready"), 1)
            dve.wait_ge(sem("wT_turned"), 1)
            dve.tensor_copy(wT[:, :], flat[0:E, 4 * BANK:4 * BANK + T]).then_inc(sem("wT_ready"), 1)
            def copy_y(x, summed):
                dve.wait_ge(sem("down"), summed)
                dve.tensor_copy(ring[:, 5, x * BANK:(x + 1) * BANK], ps[:, 6 + x, :]).then_inc(sem("yT_copied"), 1)

            for i, (j, x) in enumerate(UNITS):
                if i == FIRST_HALF + 3:
                    copy_y(0, FIRST_HALF + 1)
                if i == FIRST_HALF + 7:
                    norm_sums(dve, ch, "ffn", 0, 6)
                m = FCH[j][1]
                h = hbuf(i)[0:m, :]
                dve.wait_ge(sem("silued"), i + 1)
                if j >= NEXP:
                    dve.tensor_tensor(h, ps[0:m, 2 * (i % 3) + 1, :], h, ALU.mult).then_inc(sem("gated"), 1)
                else:
                    dve.tensor_tensor(h, ps[0:m, 2 * (i % 3) + 1, :], h, ALU.mult).then_inc(sem("gated"), 1)
                    dve.wait_ge(sem("gated"), i + 1)
                    if x == 1 and j == 0:
                        dve.wait_ge(sem("w_spread_late"), 16 * sum(map(segments, range(NEXP))))
                    elif x == 0 and j % SPREADS == 0:
                        dve.wait_ge(sem(f"w_spread{j // SPREADS}"), 16 * sum(map(segments, range(j, min(j + SPREADS, NEXP)))))
                    dve.tensor_tensor(h, h, wbc[j][0:m, x * BANK:(x + 1) * BANK], ALU.mult).then_inc(sem("activated"), 1)
            copy_y(1, len(UNITS))
            norm_sums(dve, ch, "ffn", 1, 7)
            norm_scale(dve, ch, "ffn", yn)



def kernel(**inputs):
    import numpy as _np
    import ml_dtypes as _ml
    import concourse.bacc as _bacc
    from concourse import mybir as _mybir
    from concourse.bass_utils import run_bass_kernel_spmd as _run

    i = {k: _np.asarray(v) for k, v in inputs.items()}
    bf = _ml.bfloat16
    f = _np.float32
    ctx = _np.zeros((LP, D), f)
    ctx[:LC] = i["ctx_1024"][0]
    mask = _np.ones((T, LP), f)
    mask[:, :LC] = i["mask_Bx1xSxS2_fk0"][0, 0]
    cat = lambda a, s: _np.concatenate([_np.transpose(i[a], (1, 0, 2)).reshape(D, E * HE), i[s]], 1)
    w3 = _np.zeros((len(FCH) * P, D), f)
    w3[:HID] = _np.concatenate([i["L0_ffn_W3"].reshape(E * HE, D), i["L0_ffn_Ws3"]], 0)
    arrays = {
        "x": i["x"], "xT": i["x"][0].T, "ctxT": ctx.T, "mask": mask,
        "w_q1": i["L0_attn_wq"], "w_k1": i["L0_attn_wk"], "w_v1": i["L0_attn_wv"], "w_o1": i["L0_attn_wo"],
        "w_q2": i["L0_xattn_Wq"].T, "w_k2": i["L0_xattn_Wk"].T, "w_v2": i["L0_xattn_Wv"].T, "w_o2": i["L0_xattn_Wo"].T,
        "b_q1": i["L0_attn_bq"][:, None], "b_k1": i["L0_attn_bk"][:, None],
        "b_q2": i["L0_xattn_bq"][:, None], "b_k2": i["L0_xattn_bk"][:, None],
        "b_v1": i["L0_attn_bv"][None], "b_o1": i["L0_attn_bo"][None],
        "b_v2": i["L0_xattn_bv"][None], "b_o2": i["L0_xattn_bo"][None],
        "wg": i["L0_ffn_Wg"], "w1": cat("L0_ffn_W1", "L0_ffn_Ws1"), "w2": cat("L0_ffn_W2", "L0_ffn_Ws2"),
        "w3": w3.reshape(len(FCH), P, D).transpose(1, 0, 2),
        "c_ones": _np.ones((1, LP), bf), "c_ident": _np.eye(P, dtype=f), "c_identb": _np.eye(P).astype(bf),
        "c_trib": _np.where(_np.arange(P)[None, :] < _np.arange(P)[:, None], -1e30, 0.0).astype(bf),
        "c_hblk": (_np.arange(P)[:, None] // HD == _np.arange(H)[None, :]).astype(f),
        "c_causal": (_np.arange(T)[None, :] > _np.arange(T)[:, None]).astype(f),
        "c_tri8": (_np.arange(E)[None, :] < _np.arange(E)[:, None]).astype(f),
    }
    nc = _bacc.Bacc("TRN2", target_bir_lowering=False, num_devices=1)
    sent, args = {}, {}
    for name, a in arrays.items():
        a = _np.ascontiguousarray(a)
        sent[f"in_{name}"] = a
        args[name] = nc.dram_tensor(f"in_{name}", a.shape, _mybir.dt.from_np(a.dtype), kind="ExternalInput").ap()
    out = nc.dram_tensor("out_0", (1, T, D), _mybir.dt.float32, kind="ExternalOutput").ap()
    nc.disable_value_cache = True
    build(nc, args, out)
    r = _run(nc, [sent], core_ids=[0])
    return r.results[0]["out_0"]
```
